# Optimizing a Trainium2 kernel written in Bass

```python
import numpy as np
import jax
import jax.numpy as jnp

def _softmax(x, axis=-1):
    return jax.nn.softmax(x, axis=axis)

def _gelu(x):
    return jax.nn.gelu(x, approximate=True)

def _silu(x):
    return jax.nn.silu(x)

def _sigmoid(x):
    return jax.nn.sigmoid(x)

def _layernorm(x, axis=-1, eps=1e-05):
    m = jnp.mean(x, axis=axis, keepdims=True)
    v = jnp.var(x, axis=axis, keepdims=True)
    return (x - m) / jnp.sqrt(v + eps)

def _scatter_add(tgt, idx, src, axis=0):
    return tgt.at[idx].add(src)

def _segment_sum(src, seg, n):
    return jax.ops.segment_sum(src, seg, n)
kernel_name = 'mk_prb_d4_jaxref_r8_c8f0d7'

def setup_inputs(seed: int=0):
    np.random.seed(seed)
    _w = jnp.asarray

    def _L0_attn_setup():
        import jax, jax.numpy as jnp
        import numpy as np
        NUM_HEADS = 16
        ROPE_BASE = 10000.0

        def _rotate_half(x):
            half = x.shape[-1] // 2
            x1, x2 = (x[..., :half], x[..., half:])
            return jnp.concatenate((-x2, x1), axis=-1)

        def _rope_cos_sin(seq_len, dim, dtype):
            inv_freq = 1.0 / ROPE_BASE ** (jnp.arange(0, dim, 2, dtype=jnp.float32) / dim)
            t = jnp.arange(seq_len, dtype=jnp.float32)
            freqs = jnp.einsum('i,j->ij', t, inv_freq)
            emb = jnp.concatenate((freqs, freqs), axis=-1)
            return (emb.astype(dtype), None)
        key = jax.random.key(seed)
        k1, k2, k3 = jax.random.split(key, 3)
        B, S, D = (4, 128, 256)
        return {'hidden_states': jax.random.normal(k1, (B, S, D), dtype=jnp.float32), 'w_qkv': jax.random.normal(k2, (3 * D, D), dtype=jnp.float32) * 0.02, 'b_qkv': jax.random.normal(k3, (3 * D,), dtype=jnp.float32) * 0.02}
    _L0_attn_in = _L0_attn_setup()

    def _L0_ffn_setup():
        import jax, jax.numpy as jnp
        import numpy as np
        K_TOP = 2
        key = jax.random.key(seed)
        ks = jax.random.split(key, 6)
        s = 0.02
        B, S, H, D = (4, 128, 256, 128)
        E_SH, E_RT = (2, 16)
        return {'x': jax.random.normal(ks[0], (B, S, H), dtype=jnp.float32), 'Wsh_up': jax.random.normal(ks[1], (E_SH, H, D), dtype=jnp.float32) * s, 'Wsh_down': jax.random.normal(ks[2], (E_SH, D, H), dtype=jnp.float32) * s, 'Wrt_up': jax.random.normal(ks[3], (E_RT, H, D), dtype=jnp.float32) * s, 'Wrt_down': jax.random.normal(ks[4], (E_RT, D, H), dtype=jnp.float32) * s, 'W_router': jax.random.normal(ks[5], (H, E_RT), dtype=jnp.float32) * s}
    _L0_ffn_in = _L0_ffn_setup()

    def _L1_attn_setup():
        import jax, jax.numpy as jnp
        import numpy as np
        N_HEAD_HALF = 8
        LAMBDA_INIT = 0.2
        RMS_EPS = 1.1920929e-07
        ROPE_BASE = 10000.0

        def _rms_norm(x):
            var = jnp.mean(x * x, axis=-1, keepdims=True)
            return x * jax.lax.rsqrt(var + RMS_EPS)

        def _rotary(x):
            d = x.shape[-1]
            inv_freq = (1.0 / ROPE_BASE) ** (jnp.arange(0, d, 2, dtype=jnp.float32) / d)
            t = jnp.arange(x.shape[1], dtype=jnp.float32)
            freqs = jnp.outer(t, inv_freq)
            cos = jnp.cos(freqs)[None, :, None, :]
            sin = jnp.sin(freqs)[None, :, None, :]
            x1, x2 = jnp.split(x, 2, axis=-1)
            return jnp.concatenate((x1 * cos + x2 * sin, -x1 * sin + x2 * cos), axis=-1)

        def _causal_attn(q, k, v, scale):
            T = q.shape[2]
            s = jnp.einsum('bhqd,bhkd->bhqk', q, k) * scale
            mask = jnp.tril(jnp.ones((T, T), dtype=bool))
            s = jnp.where(mask, s, jnp.float32(-jnp.inf))
            p = jax.nn.softmax(s, axis=-1)
            return jnp.einsum('bhqk,bhkd->bhqd', p, v)
        key = jax.random.key(seed)
        ks = jax.random.split(key, 9)
        B, T, C = (2, 256, 256)
        HD = C // N_HEAD_HALF
        s = 0.02
        return {'x': jax.random.normal(ks[0], (B, T, C), jnp.float32), 'wq': jax.random.normal(ks[1], (C, C), jnp.float32) * s, 'wk': jax.random.normal(ks[2], (C, C), jnp.float32) * s, 'wv': jax.random.normal(ks[3], (C, C), jnp.float32) * s, 'wo': jax.random.normal(ks[4], (C, C), jnp.float32) * s, 'lq1': jax.random.normal(ks[5], (HD,), jnp.float32) * 0.1, 'lk1': jax.random.normal(ks[6], (HD,), jnp.float32) * 0.1, 'lq2': jax.random.normal(ks[7], (HD,), jnp.float32) * 0.1, 'lk2': jax.random.normal(ks[8], (HD,), jnp.float32) * 0.1}
    _L1_attn_in = _L1_attn_setup()

    def _L1_ffn_setup():
        import jax, jax.numpy as jnp
        import numpy as np
        HIDDEN = 256
        INTER = 1024
        COMPRESSION = 128.9

        def _n_ctrl(out_size, in_size):
            return max(16, int(out_size * in_size / COMPRESSION))

        def _catmull_rom_grid(n_ctrl, n_samples):
            t = np.linspace(0.0, n_ctrl - 1.0, n_samples, dtype=np.float64)
            i = np.clip(np.floor(t).astype(np.int64), 0, n_ctrl - 2)
            f = (t - i).astype(np.float32)
            idx = np.stack([np.clip(i + k, 0, n_ctrl - 1) for k in (-1, 0, 1, 2)], axis=0)
            return (jnp.asarray(idx.astype(np.int32)), jnp.asarray(f))

        def spline_reconstruct(control_points, out_size, in_size):
            n = out_size * in_size
            idx, f = _catmull_rom_grid(control_points.shape[0], n)
            p0, p1, p2, p3 = (control_points[idx[0]], control_points[idx[1]], control_points[idx[2]], control_points[idx[3]])
            f2 = f * f
            f3 = f2 * f
            w = 0.5 * (2.0 * p1 + (p2 - p0) * f + (2.0 * p0 - 5.0 * p1 + 4.0 * p2 - p3) * f2 + (3.0 * p1 - p0 - 3.0 * p2 + p3) * f3)
            return w.reshape(out_size, in_size)
        key = jax.random.key(seed)
        k0, k1, k2, k3 = jax.random.split(key, 4)
        hidden_states = jax.random.normal(k0, (4, 256, HIDDEN), dtype=jnp.float32)
        gate_cp = jax.random.normal(k1, (_n_ctrl(INTER, HIDDEN),), dtype=jnp.float32) * 0.02
        up_cp = jax.random.normal(k2, (_n_ctrl(INTER, HIDDEN),), dtype=jnp.float32) * 0.02
        down_cp = jax.random.normal(k3, (_n_ctrl(HIDDEN, INTER),), dtype=jnp.float32) * 0.02
        return {'hidden_states': hidden_states, 'gate_cp': gate_cp, 'up_cp': up_cp, 'down_cp': down_cp}
    _L1_ffn_in = _L1_ffn_setup()

    def _L2_attn_setup():
        import jax, jax.numpy as jnp
        import numpy as np
        from jax import lax
        EPS = 1e-05

        def _layernorm(x, w, b):
            m = jnp.mean(x, axis=-1, keepdims=True)
            v = jnp.mean(jnp.square(x - m), axis=-1, keepdims=True)
            return (x - m) * lax.rsqrt(v + EPS) * w + b

        def _wkv(r, k, v, time_decay, time_faaaa):
            w = jnp.exp(-jnp.exp(time_decay))
            r_sig = jax.nn.sigmoid(r)
            kv = k * v

            def step(state, kv_t):
                state = state * w + kv_t
                return (state, state)
            _, states = lax.scan(step, jnp.zeros_like(kv[:, 0]), jnp.swapaxes(kv, 0, 1))
            states = jnp.swapaxes(states, 0, 1)
            out = r_sig * states
            out = out.at[:, 0].add(r_sig[:, 0] * jnp.exp(time_faaaa) * kv[:, 0])
            return out
        D = 256
        B, S = (4, 512)
        key = jax.random.key(seed)
        ks = jax.random.split(key, 16)
        f32 = jnp.float32
        inp = {'x': jax.random.normal(ks[0], (B, S, D), f32), 'norm1_w': jnp.ones((D,), f32), 'norm1_b': jnp.zeros((D,), f32), 'norm2_w': jnp.ones((D,), f32), 'norm2_b': jnp.zeros((D,), f32), 'time_decay': jax.random.normal(ks[1], (D,), f32) * 0.01 - 5.0, 'time_faaaa': jax.random.normal(ks[2], (D,), f32) * 0.01, 'Wr': jax.random.normal(ks[3], (D, D), f32) * 0.02, 'Wk': jax.random.normal(ks[4], (D, D), f32) * 0.02, 'Wv': jax.random.normal(ks[5], (D, D), f32) * 0.02, 'Wo': jax.random.normal(ks[6], (D, D), f32) * 0.02, 'time_mix_r': jnp.full((1, 1, D), 0.5, f32), 'time_mix_k': jnp.full((1, 1, D), 0.5, f32), 'time_mix_v': jnp.full((1, 1, D), 0.5, f32), 'Wcr': jax.random.normal(ks[7], (D, D), f32) * 0.02, 'Wck': jax.random.normal(ks[8], (D, 3 * D), f32) * 0.02, 'Wcv': jax.random.normal(ks[9], (3 * D, D), f32) * 0.02, 'cm_mix': jnp.full((1, 1, D), 0.5, f32)}
        return inp
    _L2_attn_in = _L2_attn_setup()

    def _L2_ffn_setup():
        import jax, jax.numpy as jnp
        import numpy as np
        GROUP_SIZE = 64

        def ternary_quant(w_fp32, g=GROUP_SIZE):
            w = w_fp32.astype(jnp.bfloat16)
            w_g = w.reshape(-1, g)
            scale = jnp.clip(jnp.mean(jnp.abs(w_g), axis=-1, keepdims=True), 1e-08, None)
            q = jnp.clip(jnp.round(w_g / scale), -1, 1)
            w_hat = (q * scale).reshape(w.shape)
            return w + jax.lax.stop_gradient(w_hat - w)

        def rms_norm(x):
            eps = jnp.finfo(x.dtype).eps.astype(jnp.float32)
            xf = x.astype(jnp.float32)
            inv = jax.lax.rsqrt(jnp.mean(xf * xf, axis=-1, keepdims=True) + eps)
            return (xf * inv).astype(x.dtype)
        key = jax.random.key(seed)
        k1, k2, k3 = jax.random.split(key, 3)
        B, S, D = (2, 256, 256)
        H = 4 * D
        x = jax.random.normal(k1, (B, S, D), dtype=jnp.float32).astype(jnp.bfloat16)
        w_gate_up = jax.random.normal(k2, (2 * H, D), dtype=jnp.float32) * 0.02
        w_proj = jax.random.normal(k3, (D, H), dtype=jnp.float32) * 0.02
        return {'x': x, 'w_gate_up': w_gate_up, 'w_proj': w_proj}
    _L2_ffn_in = _L2_ffn_setup()

    def _L3_attn_setup():
        import jax, jax.numpy as jnp
        import numpy as np
        import math
        NUM_HEADS = 16
        BASE = 10000.0

        def _rope_tables(T, head_size, dtype):
            half = head_size // 2
            thetas = BASE ** (-jnp.arange(half, dtype=jnp.float32) / half)
            ang = jnp.arange(T, dtype=jnp.float32)[:, None] * thetas[None, :]
            return (jnp.sin(ang).astype(dtype), jnp.cos(ang).astype(dtype))

        def _apply_rope(x, sin, cos):
            x1 = x[..., 0::2]
            x2 = x[..., 1::2]
            r1 = x1 * cos - x2 * sin
            r2 = x1 * sin + x2 * cos
            return jnp.stack([r1, r2], axis=-1).reshape(x.shape)
        key = jax.random.key(seed)
        ks = jax.random.split(key, 5)
        B, T, C = (4, 256, 256)
        return {'x': jax.random.normal(ks[0], (B, T, C), dtype=jnp.float32), 'w_qkv': jax.random.normal(ks[1], (3 * C, C), dtype=jnp.float32) * (1.0 / math.sqrt(C)), 'b_qkv': jax.random.normal(ks[2], (3 * C,), dtype=jnp.float32) * 0.02, 'w_out': jax.random.normal(ks[3], (C, C), dtype=jnp.float32) * (1.0 / math.sqrt(C)), 'b_out': jax.random.normal(ks[4], (C,), dtype=jnp.float32) * 0.02}
    _L3_attn_in = _L3_attn_setup()

    def _L3_ffn_setup():
        import jax, jax.numpy as jnp
        import numpy as np
        NUM_EXPERTS = 8
        TOP_K = 2
        LORA_ALPHA = 2.0
        LORA_RANK = 16
        D_MODEL = 256
        D_HIDDEN = 704
        key = jax.random.key(seed)
        ks = jax.random.split(key, 11)
        B, S, D, H, E, R = (2, 128, D_MODEL, D_HIDDEN, NUM_EXPERTS, LORA_RANK)
        sd = 1.0 / np.sqrt(D)
        sh = 1.0 / np.sqrt(H)
        x = jax.random.normal(ks[0], (B, S, D), jnp.float32)
        gate_w = jax.random.normal(ks[1], (E, D), jnp.float32) * sd
        w_up = jax.random.normal(ks[2], (H, D), jnp.float32) * sd
        w_gate = jax.random.normal(ks[3], (H, D), jnp.float32) * sd
        w_down = jax.random.normal(ks[4], (D, H), jnp.float32) * sh
        up_A = jax.random.normal(ks[5], (E, R, D), jnp.float32) * sd
        up_B = jax.random.normal(ks[6], (E, H, R), jnp.float32) * 0.02
        gate_A = jax.random.normal(ks[7], (E, R, D), jnp.float32) * sd
        gate_B = jax.random.normal(ks[8], (E, H, R), jnp.float32) * 0.02
        down_A = jax.random.normal(ks[9], (E, R, H), jnp.float32) * sh
        down_B = jax.random.normal(ks[10], (E, D, R), jnp.float32) * 0.02
        return {'x': x, 'gate_w': gate_w, 'w_up': w_up, 'w_gate': w_gate, 'w_down': w_down, 'up_A': up_A, 'up_B': up_B, 'gate_A': gate_A, 'gate_B': gate_B, 'down_A': down_A, 'down_B': down_B}
    _L3_ffn_in = _L3_ffn_setup()
    _d = {'L0_attn_hidden_states': _L0_attn_in['hidden_states'], 'L0_attn_w_qkv': _L0_attn_in['w_qkv'], 'L0_attn_b_qkv': _L0_attn_in['b_qkv'], 'L0_ffn_Wsh_up': _L0_ffn_in['Wsh_up'], 'L0_ffn_Wsh_down': _L0_ffn_in['Wsh_down'], 'L0_ffn_Wrt_up': _L0_ffn_in['Wrt_up'], 'L0_ffn_Wrt_down': _L0_ffn_in['Wrt_down'], 'L0_ffn_W_router': _L0_ffn_in['W_router'], 'L1_attn_wq': _L1_attn_in['wq'], 'L1_attn_wk': _L1_attn_in['wk'], 'L1_attn_wv': _L1_attn_in['wv'], 'L1_attn_wo': _L1_attn_in['wo'], 'L1_attn_lq1': _L1_attn_in['lq1'], 'L1_attn_lk1': _L1_attn_in['lk1'], 'L1_attn_lq2': _L1_attn_in['lq2'], 'L1_attn_lk2': _L1_attn_in['lk2'], 'L1_ffn_gate_cp': _L1_ffn_in['gate_cp'], 'L1_ffn_up_cp': _L1_ffn_in['up_cp'], 'L1_ffn_down_cp': _L1_ffn_in['down_cp'], 'L2_attn_norm1_w': _L2_attn_in['norm1_w'], 'L2_attn_norm1_b': _L2_attn_in['norm1_b'], 'L2_attn_norm2_w': _L2_attn_in['norm2_w'], 'L2_attn_norm2_b': _L2_attn_in['norm2_b'], 'L2_attn_time_decay': _L2_attn_in['time_decay'], 'L2_attn_time_faaaa': _L2_attn_in['time_faaaa'], 'L2_attn_Wr': _L2_attn_in['Wr'], 'L2_attn_Wk': _L2_attn_in['Wk'], 'L2_attn_Wv': _L2_attn_in['Wv'], 'L2_attn_Wo': _L2_attn_in['Wo'], 'L2_attn_time_mix_r': _L2_attn_in['time_mix_r'], 'L2_attn_time_mix_k': _L2_attn_in['time_mix_k'], 'L2_attn_time_mix_v': _L2_attn_in['time_mix_v'], 'L2_attn_Wcr': _L2_attn_in['Wcr'], 'L2_attn_Wck': _L2_attn_in['Wck'], 'L2_attn_Wcv': _L2_attn_in['Wcv'], 'L2_attn_cm_mix': _L2_attn_in['cm_mix'], 'L2_ffn_w_gate_up': _L2_ffn_in['w_gate_up'], 'L2_ffn_w_proj': _L2_ffn_in['w_proj'], 'L3_attn_w_qkv': _L3_attn_in['w_qkv'], 'L3_attn_b_qkv': _L3_attn_in['b_qkv'], 'L3_attn_w_out': _L3_attn_in['w_out'], 'L3_attn_b_out': _L3_attn_in['b_out'], 'L3_ffn_gate_w': _L3_ffn_in['gate_w'], 'L3_ffn_w_up': _L3_ffn_in['w_up'], 'L3_ffn_w_gate': _L3_ffn_in['w_gate'], 'L3_ffn_w_down': _L3_ffn_in['w_down'], 'L3_ffn_up_A': _L3_ffn_in['up_A'], 'L3_ffn_up_B': _L3_ffn_in['up_B'], 'L3_ffn_gate_A': _L3_ffn_in['gate_A'], 'L3_ffn_gate_B': _L3_ffn_in['gate_B'], 'L3_ffn_down_A': _L3_ffn_in['down_A'], 'L3_ffn_down_B': _L3_ffn_in['down_B']}
    _x0 = _d['L0_attn_hidden_states']
    _d['L0_attn_hidden_states'] = jax.random.normal(jax.random.fold_in(jax.random.key(seed), 1), (4, 1024, 256), dtype=_x0.dtype)
    del _x0
    return _d

def reference(L0_attn_hidden_states, L0_attn_w_qkv, L0_attn_b_qkv, L0_ffn_Wsh_up, L0_ffn_Wsh_down, L0_ffn_Wrt_up, L0_ffn_Wrt_down, L0_ffn_W_router, L1_attn_wq, L1_attn_wk, L1_attn_wv, L1_attn_wo, L1_attn_lq1, L1_attn_lk1, L1_attn_lq2, L1_attn_lk2, L1_ffn_gate_cp, L1_ffn_up_cp, L1_ffn_down_cp, L2_attn_norm1_w, L2_attn_norm1_b, L2_attn_norm2_w, L2_attn_norm2_b, L2_attn_time_decay, L2_attn_time_faaaa, L2_attn_Wr, L2_attn_Wk, L2_attn_Wv, L2_attn_Wo, L2_attn_time_mix_r, L2_attn_time_mix_k, L2_attn_time_mix_v, L2_attn_Wcr, L2_attn_Wck, L2_attn_Wcv, L2_attn_cm_mix, L2_ffn_w_gate_up, L2_ffn_w_proj, L3_attn_w_qkv, L3_attn_b_qkv, L3_attn_w_out, L3_attn_b_out, L3_ffn_gate_w, L3_ffn_w_up, L3_ffn_w_gate, L3_ffn_w_down, L3_ffn_up_A, L3_ffn_up_B, L3_ffn_gate_A, L3_ffn_gate_B, L3_ffn_down_A, L3_ffn_down_B):

    def _L0_attn_ref(hidden_states, w_qkv, b_qkv):
        import jax, jax.numpy as jnp
        import numpy as np
        NUM_HEADS = 16
        ROPE_BASE = 10000.0

        def _rotate_half(x):
            half = x.shape[-1] // 2
            x1, x2 = (x[..., :half], x[..., half:])
            return jnp.concatenate((-x2, x1), axis=-1)

        def _rope_cos_sin(seq_len, dim, dtype):
            inv_freq = 1.0 / ROPE_BASE ** (jnp.arange(0, dim, 2, dtype=jnp.float32) / dim)
            t = jnp.arange(seq_len, dtype=jnp.float32)
            freqs = jnp.einsum('i,j->ij', t, inv_freq)
            emb = jnp.concatenate((freqs, freqs), axis=-1)
            return (emb.astype(dtype), None)
        B, S, D = hidden_states.shape
        H = NUM_HEADS
        hd = D // H
        qkv = jnp.einsum('bsd,ed->bse', hidden_states, w_qkv) + b_qkv
        qkv = qkv.reshape(B, S, H, 3 * hd)
        q = jnp.transpose(qkv[..., :hd], (0, 2, 1, 3))
        k = jnp.transpose(qkv[..., hd:2 * hd], (0, 2, 1, 3))
        v = jnp.transpose(qkv[..., 2 * hd:], (0, 2, 1, 3))
        emb, _ = _rope_cos_sin(S, hd, hidden_states.dtype)
        cos = jnp.cos(emb)[None, None, :, :]
        sin = jnp.sin(emb)[None, None, :, :]
        q = q * cos + _rotate_half(q) * sin
        k = k * cos + _rotate_half(k) * sin
        norm = jnp.sqrt(jnp.asarray(hd, dtype=jnp.float32)).astype(q.dtype)
        scores = jnp.einsum('bhqd,bhkd->bhqk', q, k) / norm
        causal = jnp.tril(jnp.ones((S, S), dtype=bool))[None, None]
        mask_value = jnp.finfo(scores.dtype).min
        scores = jnp.where(causal, scores, mask_value)
        attn = jax.nn.softmax(scores, axis=-1)
        out = jnp.einsum('bhqk,bhkd->bhqd', attn, v)
        return jnp.transpose(out, (0, 2, 1, 3)).reshape(B, S, D)

    def _L0_ffn_ref(x, Wsh_up, Wsh_down, Wrt_up, Wrt_down, W_router):
        import jax, jax.numpy as jnp
        import numpy as np
        K_TOP = 2
        B, S, H = x.shape
        E_rt = Wrt_up.shape[0]
        xt = x.reshape(B * S, H)
        sh_mid = jax.nn.gelu(jnp.einsum('th,ehd->ted', xt, Wsh_up), approximate=False)
        shared_out = jnp.einsum('ted,edh->th', sh_mid, Wsh_down)
        probs = jax.nn.softmax(xt @ W_router, axis=-1)
        top_v, top_i = jax.lax.top_k(probs, K_TOP)
        gate = jnp.sum(jax.nn.one_hot(top_i, E_rt, dtype=xt.dtype) * top_v[..., None], axis=1)
        rt_mid = jax.nn.gelu(jnp.einsum('th,ehd->ted', xt, Wrt_up), approximate=False)
        routed_out = jnp.einsum('ted,edh->th', rt_mid * gate[:, :, None], Wrt_down)
        return (shared_out + routed_out).reshape(B, S, H)

    def _L1_attn_ref(x, wq, wk, wv, wo, lq1, lk1, lq2, lk2):
        import jax, jax.numpy as jnp
        import numpy as np
        N_HEAD_HALF = 8
        LAMBDA_INIT = 0.2
        RMS_EPS = 1.1920929e-07
        ROPE_BASE = 10000.0

        def _rms_norm(x):
            var = jnp.mean(x * x, axis=-1, keepdims=True)
            return x * jax.lax.rsqrt(var + RMS_EPS)

        def _rotary(x):
            d = x.shape[-1]
            inv_freq = (1.0 / ROPE_BASE) ** (jnp.arange(0, d, 2, dtype=jnp.float32) / d)
            t = jnp.arange(x.shape[1], dtype=jnp.float32)
            freqs = jnp.outer(t, inv_freq)
            cos = jnp.cos(freqs)[None, :, None, :]
            sin = jnp.sin(freqs)[None, :, None, :]
            x1, x2 = jnp.split(x, 2, axis=-1)
            return jnp.concatenate((x1 * cos + x2 * sin, -x1 * sin + x2 * cos), axis=-1)

        def _causal_attn(q, k, v, scale):
            T = q.shape[2]
            s = jnp.einsum('bhqd,bhkd->bhqk', q, k) * scale
            mask = jnp.tril(jnp.ones((T, T), dtype=bool))
            s = jnp.where(mask, s, jnp.float32(-jnp.inf))
            p = jax.nn.softmax(s, axis=-1)
            return jnp.einsum('bhqk,bhkd->bhqd', p, v)
        B, T, C = x.shape
        NH = N_HEAD_HALF
        HD = C // NH
        HH = HD // 2
        lam1 = jnp.exp(jnp.sum(lq1 * lk1))
        lam2 = jnp.exp(jnp.sum(lq2 * lk2))
        lam = lam1 - lam2 + LAMBDA_INIT
        q = (x @ wq.T).reshape(B, T, NH, 2, HH).transpose(0, 2, 1, 3, 4)
        k = (x @ wk.T).reshape(B, T, NH, 2, HH).transpose(0, 2, 1, 3, 4)
        v = (x @ wv.T).reshape(B, T, NH, HD).transpose(0, 2, 1, 3)
        q1 = _rotary(_rms_norm(q[..., 0, :]))
        q2 = _rotary(_rms_norm(q[..., 1, :]))
        k1 = _rotary(_rms_norm(k[..., 0, :]))
        k2 = _rotary(_rms_norm(k[..., 1, :]))
        scale = 1.0 / jnp.sqrt(jnp.float32(HH))
        y = _causal_attn(q1, k1, v, scale) - lam * _causal_attn(q2, k2, v, scale)
        y = y.transpose(0, 2, 1, 3).reshape(B, T, C)
        y = y @ wo.T * (1.0 - LAMBDA_INIT)
        return y

    def _L1_ffn_ref(hidden_states, gate_cp, up_cp, down_cp):
        import jax, jax.numpy as jnp
        import numpy as np
        HIDDEN = 256
        INTER = 1024
        COMPRESSION = 128.9

        def _n_ctrl(out_size, in_size):
            return max(16, int(out_size * in_size / COMPRESSION))

        def _catmull_rom_grid(n_ctrl, n_samples):
            t = np.linspace(0.0, n_ctrl - 1.0, n_samples, dtype=np.float64)
            i = np.clip(np.floor(t).astype(np.int64), 0, n_ctrl - 2)
            f = (t - i).astype(np.float32)
            idx = np.stack([np.clip(i + k, 0, n_ctrl - 1) for k in (-1, 0, 1, 2)], axis=0)
            return (jnp.asarray(idx.astype(np.int32)), jnp.asarray(f))

        def spline_reconstruct(control_points, out_size, in_size):
            n = out_size * in_size
            idx, f = _catmull_rom_grid(control_points.shape[0], n)
            p0, p1, p2, p3 = (control_points[idx[0]], control_points[idx[1]], control_points[idx[2]], control_points[idx[3]])
            f2 = f * f
            f3 = f2 * f
            w = 0.5 * (2.0 * p1 + (p2 - p0) * f + (2.0 * p0 - 5.0 * p1 + 4.0 * p2 - p3) * f2 + (3.0 * p1 - p0 - 3.0 * p2 + p3) * f3)
            return w.reshape(out_size, in_size)
        gate_w = spline_reconstruct(gate_cp, INTER, HIDDEN)
        up_w = spline_reconstruct(up_cp, INTER, HIDDEN)
        down_w = spline_reconstruct(down_cp, HIDDEN, INTER)
        gate = jnp.einsum('bsh,ih->bsi', hidden_states, gate_w)
        up = jnp.einsum('bsh,ih->bsi', hidden_states, up_w)
        inter = jax.nn.silu(gate) * up
        return jnp.einsum('bsi,hi->bsh', inter, down_w)

    def _L2_attn_ref(x, norm1_w, norm1_b, norm2_w, norm2_b, time_decay, time_faaaa, Wr, Wk, Wv, Wo, time_mix_r, time_mix_k, time_mix_v, Wcr, Wck, Wcv, cm_mix):
        import jax, jax.numpy as jnp
        import numpy as np
        from jax import lax
        EPS = 1e-05

        def _layernorm(x, w, b):
            m = jnp.mean(x, axis=-1, keepdims=True)
            v = jnp.mean(jnp.square(x - m), axis=-1, keepdims=True)
            return (x - m) * lax.rsqrt(v + EPS) * w + b

        def _wkv(r, k, v, time_decay, time_faaaa):
            w = jnp.exp(-jnp.exp(time_decay))
            r_sig = jax.nn.sigmoid(r)
            kv = k * v

            def step(state, kv_t):
                state = state * w + kv_t
                return (state, state)
            _, states = lax.scan(step, jnp.zeros_like(kv[:, 0]), jnp.swapaxes(kv, 0, 1))
            states = jnp.swapaxes(states, 0, 1)
            out = r_sig * states
            out = out.at[:, 0].add(r_sig[:, 0] * jnp.exp(time_faaaa) * kv[:, 0])
            return out
        h = _layernorm(x, norm1_w, norm1_b)
        prev = jnp.pad(h[:, :-1], ((0, 0), (1, 0), (0, 0)))
        r = (h * time_mix_r + prev * (1.0 - time_mix_r)) @ Wr
        k = (h * time_mix_k + prev * (1.0 - time_mix_k)) @ Wk
        v = (h * time_mix_v + prev * (1.0 - time_mix_v)) @ Wv
        wkv = _wkv(r, k, v, time_decay, time_faaaa)
        x = x + wkv @ Wo
        h = _layernorm(x, norm2_w, norm2_b)
        prev = jnp.pad(h[:, :-1], ((0, 0), (1, 0), (0, 0)))
        mixed = h * cm_mix + prev * (1.0 - cm_mix)
        r_cm = jax.nn.sigmoid(mixed @ Wcr)
        k_cm = jax.nn.relu(jnp.square(mixed @ Wck))
        x = x + r_cm * (k_cm @ Wcv)
        return x

    def _L2_ffn_ref(x, w_gate_up, w_proj):
        import jax, jax.numpy as jnp
        import numpy as np
        GROUP_SIZE = 64

        def ternary_quant(w_fp32, g=GROUP_SIZE):
            w = w_fp32.astype(jnp.bfloat16)
            w_g = w.reshape(-1, g)
            scale = jnp.clip(jnp.mean(jnp.abs(w_g), axis=-1, keepdims=True), 1e-08, None)
            q = jnp.clip(jnp.round(w_g / scale), -1, 1)
            w_hat = (q * scale).reshape(w.shape)
            return w + jax.lax.stop_gradient(w_hat - w)

        def rms_norm(x):
            eps = jnp.finfo(x.dtype).eps.astype(jnp.float32)
            xf = x.astype(jnp.float32)
            inv = jax.lax.rsqrt(jnp.mean(xf * xf, axis=-1, keepdims=True) + eps)
            return (xf * inv).astype(x.dtype)
        wq_gu = ternary_quant(w_gate_up)
        gu = jnp.einsum('bsd,hd->bsh', x, wq_gu)
        gate, up = jnp.split(gu, 2, axis=-1)
        h = jax.nn.silu(gate) * up
        hn = rms_norm(h)
        wq_p = ternary_quant(w_proj)
        return jnp.einsum('bsh,dh->bsd', hn, wq_p)

    def _L3_attn_ref(x, w_qkv, b_qkv, w_out, b_out):
        import jax, jax.numpy as jnp
        import numpy as np
        import math
        NUM_HEADS = 16
        BASE = 10000.0

        def _rope_tables(T, head_size, dtype):
            half = head_size // 2
            thetas = BASE ** (-jnp.arange(half, dtype=jnp.float32) / half)
            ang = jnp.arange(T, dtype=jnp.float32)[:, None] * thetas[None, :]
            return (jnp.sin(ang).astype(dtype), jnp.cos(ang).astype(dtype))

        def _apply_rope(x, sin, cos):
            x1 = x[..., 0::2]
            x2 = x[..., 1::2]
            r1 = x1 * cos - x2 * sin
            r2 = x1 * sin + x2 * cos
            return jnp.stack([r1, r2], axis=-1).reshape(x.shape)
        B, T, C = x.shape
        H = NUM_HEADS
        D = C // H
        scale = 1.0 / math.sqrt(D)
        qkv = x @ w_qkv.T + b_qkv
        qkv = qkv.reshape(B, T, 3, H, D)
        qkv = jnp.transpose(qkv, (2, 0, 3, 1, 4))
        q, k, v = (qkv[0], qkv[1], qkv[2])
        sin, cos = _rope_tables(T, D, x.dtype)
        q = _apply_rope(q, sin, cos)
        k = _apply_rope(k, sin, cos)
        att = jnp.einsum('bhtd,bhsd->bhts', q, k) * scale
        causal = jnp.triu(jnp.ones((T, T), dtype=bool), k=1)
        att = jnp.where(causal, -jnp.inf, att)
        att_prob = jax.nn.softmax(att, axis=-1)
        att_v = jnp.einsum('bhts,bhsd->bhtd', att_prob, v)
        att_v = jnp.transpose(att_v, (0, 2, 1, 3)).reshape(B, T, C)
        return att_v @ w_out.T + b_out

    def _L3_ffn_ref(x, gate_w, w_up, w_gate, w_down, up_A, up_B, gate_A, gate_B, down_A, down_B):
        import jax, jax.numpy as jnp
        import numpy as np
        NUM_EXPERTS = 8
        TOP_K = 2
        LORA_ALPHA = 2.0
        LORA_RANK = 16
        D_MODEL = 256
        D_HIDDEN = 704
        B, S, D = x.shape
        H = w_up.shape[0]
        gate_logits = jnp.einsum('bsd,ed->bse', x, gate_w)
        topw, sel = jax.lax.top_k(gate_logits, TOP_K)
        topw = jax.nn.softmax(topw.astype(jnp.float32), axis=1).astype(x.dtype)
        xt = x.reshape(-1, D)
        wf = topw.reshape(-1, TOP_K)
        sf = sel.reshape(-1, TOP_K)
        base_up = xt @ w_up.T
        base_gate = xt @ w_gate.T
        mixed_h = jnp.zeros((xt.shape[0], H), x.dtype)
        lora_down = jnp.zeros_like(xt)
        for e in range(NUM_EXPERTS):
            c = jnp.sum(jnp.where(sf == e, wf, 0.0), axis=1)
            lo_up = LORA_ALPHA * (xt @ up_A[e].T @ up_B[e].T)
            lo_gate = LORA_ALPHA * (xt @ gate_A[e].T @ gate_B[e].T)
            h_e = jax.nn.silu(base_up + lo_up) * (base_gate + lo_gate)
            ch = c[:, None] * h_e
            mixed_h = mixed_h + ch
            lora_down = lora_down + LORA_ALPHA * (ch @ down_A[e].T @ down_B[e].T)
        out = mixed_h @ w_down.T + lora_down
        return out.reshape(B, S, D)
    x = L0_attn_hidden_states
    xn = _layernorm(x, axis=-1)
    x = x + _L0_attn_ref(xn, L0_attn_w_qkv, L0_attn_b_qkv) + _L0_ffn_ref(xn, L0_ffn_Wsh_up, L0_ffn_Wsh_down, L0_ffn_Wrt_up, L0_ffn_Wrt_down, L0_ffn_W_router)
    xn = _layernorm(x, axis=-1)
    x = x + _L1_attn_ref(xn, L1_attn_wq, L1_attn_wk, L1_attn_wv, L1_attn_wo, L1_attn_lq1, L1_attn_lk1, L1_attn_lq2, L1_attn_lk2) + _L1_ffn_ref(xn, L1_ffn_gate_cp, L1_ffn_up_cp, L1_ffn_down_cp)
    xn = _layernorm(x, axis=-1)
    x = x + _L2_attn_ref(xn, L2_attn_norm1_w, L2_attn_norm1_b, L2_attn_norm2_w, L2_attn_norm2_b, L2_attn_time_decay, L2_attn_time_faaaa, L2_attn_Wr, L2_attn_Wk, L2_attn_Wv, L2_attn_Wo, L2_attn_time_mix_r, L2_attn_time_mix_k, L2_attn_time_mix_v, L2_attn_Wcr, L2_attn_Wck, L2_attn_Wcv, L2_attn_cm_mix) + _L2_ffn_ref(xn, L2_ffn_w_gate_up, L2_ffn_w_proj)
    xn = _layernorm(x, axis=-1)
    x = x + _L3_attn_ref(xn, L3_attn_w_qkv, L3_attn_b_qkv, L3_attn_w_out, L3_attn_b_out) + _L3_ffn_ref(xn, L3_ffn_gate_w, L3_ffn_w_up, L3_ffn_w_gate, L3_ffn_w_down, L3_ffn_up_A, L3_ffn_up_B, L3_ffn_gate_A, L3_ffn_gate_B, L3_ffn_down_A, L3_ffn_down_B)
    return x

_drawn_inputs = setup_inputs


def setup_inputs(seed=0):
    import zlib

    import numpy as np

    out = dict(_drawn_inputs(seed))
    spreads = {'L2_attn_norm1_w': (1.0, 0.6),
     'L2_attn_norm1_b': (0.0, 0.516),
     'L2_attn_norm2_w': (1.0, 0.6),
     'L2_attn_norm2_b': (0.0, 0.8),
     'L2_attn_time_mix_r': (0.5, 0.6),
     'L2_attn_time_mix_k': (0.5, 0.6),
     'L2_attn_time_mix_v': (0.5, 0.6),
     'L2_attn_cm_mix': (0.5, 0.6)}
    factors = {'L0_ffn_Wrt_up': 8.0,
     'L0_ffn_Wrt_down': 8.0,
     'L0_ffn_W_router': 8.0,
     'L1_attn_wq': 6.5,
     'L1_attn_wk': 6.438,
     'L1_attn_wv': 4.988,
     'L1_attn_wo': 5.047,
     'L1_attn_lq1': 8.0,
     'L1_attn_lk1': 8.0,
     'L1_attn_lq2': 8.0,
     'L1_attn_lk2': 8.0,
     'L1_ffn_up_cp': 2.934,
     'L1_ffn_down_cp': 3.105,
     'L2_attn_time_decay': 8.0,
     'L2_attn_time_faaaa': 64.0,
     'L2_attn_Wr': 7.303,
     'L2_attn_Wcr': 8.0,
     'L2_attn_Wck': 4.966,
     'L2_attn_Wcv': 3.9,
     'L3_attn_b_qkv': 37.8,
     'L3_attn_b_out': 129.298,
     'L3_ffn_gate_w': 8.0,
     'L3_ffn_w_up': 8.0,
     'L3_ffn_w_gate': 8.0,
     'L3_ffn_w_down': 8.0,
     'L3_ffn_up_A': 8.0,
     'L3_ffn_up_B': 8.0,
     'L3_ffn_gate_A': 8.0,
     'L3_ffn_gate_B': 8.0,
     'L3_ffn_down_A': 8.0,
     'L3_ffn_down_B': 8.0,
     'L3_attn_w_qkv': 3.504,
     'L3_attn_w_out': 3.491}
    for name, (base, spread) in spreads.items():
        noise = np.random.default_rng([zlib.crc32(name.encode()), seed]).standard_normal(out[name].shape)
        drawn = base * np.exp(spread * noise) if base else spread * noise
        out[name] = jnp.asarray(drawn.astype(out[name].dtype))
    for name, factor in factors.items():
        out[name] = (out[name] * factor).astype(out[name].dtype)
    return out
```

```python
import concourse.bass as bass
from concourse import mybir
from contextlib import ExitStack, contextmanager
import numpy as np

F32 = mybir.dt.float32
F16 = mybir.dt.float16
BF16 = mybir.dt.bfloat16
U32 = mybir.dt.uint32
ALU = mybir.AluOpType
ACT = mybir.ActivationFunctionType
AX = mybir.AxisListType
RMAX = bass.bass_isa.ReduceOp.max
RADD = bass.bass_isa.ReduceOp.add

B, S, D = 4, 1024, 256
P = 128
NT = S // P
KD = D // P
CH = 512
NC = S // CH
TC = CH // P
HD = 16
NM = 16
LN_EPS = 1e-5
RMS_EPS = 1.1920929e-07
NEG = -1.0e30
E_SH, E_RT, F0 = 2, 16, 128
F1 = 1024
F2 = 768
H3, E3, R3 = 704, 8, 16
M3 = -(-H3 // P)
LAMBDA_INIT = 0.2
NSEG = 6
GROUP = 64
MIXED = M3 + 3
M_ROW = 48


class Memory:
    pass


@contextmanager
def stage(nc, *names, pool=False):
    with ExitStack() as ctx:
        sems = [ctx.enter_context(nc.semaphore(n)) for n in names]
        with nc.Block(no_gpsimd_drain=not pool) as block:
            yield (block, *sems)
        for s in sems:
            nc.sync.sem_clear(s)
        nc.all_engine_barrier(sem_only=True)


class Steps:

    def __init__(self, engine, sem):
        self.engine, self.sem, self.count = engine, sem, 0

    def __call__(self, instruction):
        self.count += 1
        instruction.then_inc(self.sem, 1)
        self.engine.wait_ge(self.sem, self.count)


def view(ap, *dims):
    if len(dims) == 1:
        return ap
    names = " ".join(f"d{i}" for i in range(len(dims)))
    return ap.rearrange(f"p ({names}) -> p {names}", **{f"d{i}": n for i, n in enumerate(dims)})


def sum_so_far(m, batch, t):
    return sum_place(m, batch if m.acc is None else None, t)


def sum_place(m, batch, t):
    if batch is None:
        return m.acc[:, t, :]
    return m.x[:, bass.ds(batch * NT + t, 1), :].rearrange("p a c -> p (a c)")


class Arena:

    def __init__(self, tensor, start=0):
        self.tensor, self.at = tensor, start

    def take(self, *dims, dtype=F32):
        n = int(np.prod(dims))
        words = n if dtype in (F32, U32) else -(-n // 2)
        ap = self.tensor[:, self.at:self.at + words]
        self.at += words
        assert self.at <= self.tensor.shape[1], self.at
        return view(ap if dtype == F32 else ap.bitcast(dtype), *dims)


def rows(dram, p=P):
    return dram.rearrange("(k p) n -> p k n", p=p)



def setup_constants(nc, m, io):
    with stage(nc, "cleared", "selected", "psum_cleared", "tables_in", pool=True) as (block, cleared, selected, psum_cleared, tables_in):
        @block.gpsimd
        def _(pool):
            pool.memset(m.ident[:, :], 0.0).then_inc(cleared, 1)
            pool.memset(m.mask_qk[:, :], 0.0).then_inc(cleared, 1)
            pool.memset(m.mask_kq[:, :], 0.0).then_inc(cleared, 1)
            pool.memset(m.ones_col[:, :], 1.0)
            pool.iota(m.iota16[:, :], [[1, 16]], base=0, channel_multiplier=0, allow_small_or_imprecise_dtypes=True)
            pool.iota(m.iota_x[:, :], [[1, E3], [0, R3]], base=0, channel_multiplier=0,
                      allow_small_or_imprecise_dtypes=True)
            pool.wait_ge(cleared, 3)
            pool.affine_select(out=m.ident[:, :], in_=m.ident[:, :], compare_op=ALU.not_equal, fill=1.0,
                               base=0, pattern=[[-1, P]], channel_multiplier=1).then_inc(selected, 1)
            pool.affine_select(out=m.mask_qk[:, :], in_=m.mask_qk[:, :], compare_op=ALU.is_ge, fill=NEG,
                               base=0, pattern=[[-1, P]], channel_multiplier=1).then_inc(selected, 1)
            pool.affine_select(out=m.mask_kq[:, :], in_=m.mask_kq[:, :], compare_op=ALU.is_ge, fill=NEG,
                               base=0, pattern=[[1, P]], channel_multiplier=-1).then_inc(selected, 1)

        @block.vector
        def _(dve):
            dve.memset(m.ps[:, :, :], 0.0).then_inc(psum_cleared, 1)
            dve.wait_ge(selected, 1)
            dve.tensor_copy(m.ident_h[:, :], m.ident[:, :])
            dve.tensor_copy(m.ident_b[:, :], m.ident[:, :])

        @block.sync
        def _(sp):
            for b in range(B):
                sp.dma_start(m.x[:, b * NT:(b + 1) * NT, :], rows(io.x[b])).then_inc(tables_in, 16)
            n = B
            for i, (cos, sin) in enumerate(((io.cos0, io.sin0), (io.cos3, io.sin3))):
                sp.dma_start(m.cos[:, i, :, :], rows(cos)).then_inc(tables_in, 16)
                sp.dma_start(m.sin[:, i, :, :], rows(sin)).then_inc(tables_in, 16)
                n += 2
            sp.wait_ge(tables_in, 16 * n)


def load_weights(nc, pairs):
    with stage(nc, "weights_in") as (block, weights_in):
        @block.sync
        def _(sp):
            for dst, src in pairs[0::2]:
                sp.dma_start(dst, src).then_inc(weights_in, 16)
            sp.wait_ge(weights_in, 16 * len(pairs))

        @block.scalar
        def _(act):
            for dst, src in pairs[1::2]:
                act.dma_start(dst, src).then_inc(weights_in, 16)



def normalise(nc, m, src, dst, dst_t, xload=None, bias=None, scale_w=None, scale_b=None, add_dst=None):
    with stage(nc, "src_in", "stats", "std_in", "std_done", "rstd_in", "normed", "turned", "stored") as \
            (block, src_in, stats, std_in, std_done, rstd_in, normed, turned, stored):
        var = m.small[:, 0:2 * NT].rearrange("p (t c) -> p t c", c=2)
        st = m.small[:, 2 * NT:8 * NT].rearrange("p (t c) -> p t c", c=6)
        std = m.small[:, 8 * NT:9 * NT]
        rstd = m.small[:, 9 * NT:10 * NT]
        veps = m.small[:, 10 * NT:11 * NT]

        @block.vector
        def _(dve):
            for t in range(NT):
                if xload is not None and t % 2 == 0:
                    dve.wait_ge(src_in, t // 2 + 1)
                dve.bn_stats(st[:, t, :], src[:, t, :]).then_inc(stats, 1)
            for t in range(NT):
                dve.wait_ge(stats, t + 1)
                dve.bn_aggr(var[:, t, :], st[:, t, :]).then_inc(std_in, 1)
            dve.wait_ge(std_in, NT)
            dve.tensor_scalar(veps, var[:, :, 1], LN_EPS, None, ALU.add).then_inc(std_in, 1)
            dve.wait_ge(std_done, 1)
            dve.reciprocal(rstd, std).then_inc(rstd_in, 1)
            dve.wait_ge(rstd_in, 1)
            for t in range(NT):
                dve.tensor_scalar(dst[:, t, :], src[:, t, :], var[:, t, 0:1], rstd[:, t:t + 1],
                                  ALU.subtract, ALU.mult).then_inc(normed, 1)
            if bias is not None:
                dve.wait_ge(normed, NT)
                dve.tensor_tensor(m.x[:, bass.ds(xload * NT, NT), :], src[:, :, :],
                                  bias[:, :].unsqueeze(1).broadcast_to([P, NT, D]), ALU.add)
            if add_dst is not None:
                dve.wait_ge(normed, NT)
                dve.tensor_tensor(add_dst[:, :, :], add_dst[:, :, :], dst[:, :, :], ALU.add)

        @block.tensor
        def _(pe):
            for t in range(NT):
                pe.wait_ge(normed, t + 1)
                for k in range(KD):
                    last = pe.transpose(m.ps[:, 4 * k + t // TC, (t % TC) * P:(t % TC + 1) * P],
                                        dst[:, t, k * P:(k + 1) * P], m.ident[:, :])
                last.then_inc(turned, 1)

        @block.scalar
        def _(act):
            if xload is not None:
                for t in range(0, NT, 2):
                    act.activation(src[:, t:t + 2, :], m.x[:, bass.ds(xload * NT + t, 2), :], ACT.Copy).then_inc(src_in, 1)
            act.wait_ge(std_in, NT + 1)
            act.activation(std, veps, ACT.Sqrt).then_inc(std_done, 1)
            for c in range(NC):
                act.wait_ge(turned, TC * (c + 1))
                for k in range(KD):
                    out = dst_t[:, k, c * CH:(c + 1) * CH]
                    if scale_w is None:
                        act.activation(out, m.ps[:, 4 * k + c, :], ACT.Identity)
                    else:
                        act.activation(out, m.ps[:, 4 * k + c, :], ACT.Identity,
                                       bias=scale_b[:, k:k + 1], scale=scale_w[:, k:k + 1])



def attention_operands(nc, m, a, wqkv, bias, table, rms, heads, vd):
    gh = 2 * NM
    half = HD // 2
    if isinstance(table, int):
        cos = [m.cos[:, table, t, :].unsqueeze(1).broadcast_to([P, gh, HD]) for t in range(NT)]
        sin = [m.sin[:, table, t, :].unsqueeze(1).broadcast_to([P, gh, HD]) for t in range(NT)]
    else:
        cos, sin = ([v.rearrange("p (h c) -> p h c", c=HD)] * NT for v in table)
    names = ["proj", "taken", "steps", "pool_done", "rotated", "hi", "lo", "stacked", "turned", "stored", "cleared",
             "rms_in", "rms_std", "squared"]
    with stage(nc, *names, pool=True) as (block, proj, taken, steps, pool_done, rotated, hi, lo, stacked, turned, stored,
                               cleared, rms_in, rms_std, squared):
        def kcols(buf, parity, slot, n=1, step=1):
            c0 = P * parity + 64 * parity + HD * slot
            v = a.ks[:, buf, :].rearrange("p (n c) -> p n c", c=2 * P)
            if n == 1:
                return v[:, :, c0:c0 + HD]
            return v[:, :, c0:c0 + HD * step * n].rearrange("p n (s c) -> p n s c", c=HD * step)[:, :, :, 0:HD]

        @block.tensor
        def _(pe):
            def turn(t):
                pe.wait_ge(stacked, 3 * (t + 1))
                if t >= 1:
                    pe.wait_ge(stored, 2 * t)
                psq = m.ps[:, 4, :].bitcast(F16)
                psk = m.ps[:, 5:7, :].rearrange("p a b -> p (a b)").bitcast(F16)
                for n in range(NM // 2):
                    pe.transpose(psq[:, n * P:(n + 1) * P], a.qs[:, t % 2, n * P:(n + 1) * P], m.ident_h[:, :])
                for n in range(NM):
                    last = pe.transpose(psk[:, n * P:(n + 1) * P], a.ks[:, t % 2, n * P:(n + 1) * P], m.ident_h[:, :])
                last.then_inc(turned, 1)

            for t in range(NT):
                if t >= 2:
                    pe.wait_ge(taken, 2 * (t - 1))
                for j, (c0, w) in enumerate(((0, 512), (512, 256))):
                    for k in range(KD):
                        last = pe.matmul(m.ps[:, 2 * (t % 2) + j, 0:w], m.xn_t[:, k, t * P:(t + 1) * P],
                                         wqkv[:, k, c0:c0 + w], start=(k == 0), stop=(k == KD - 1))
                last.then_inc(proj, 1)
                if t >= 1:
                    turn(t - 1)
            turn(NT - 1)

        @block.vector
        def _(dve):
            step = Steps(dve, steps)
            for t in range(NT):
                qk = a.qk[:, t % 2, :]
                qk3 = qk.rearrange("p (h c) -> p h c", c=HD)
                t1 = a.t1[:, t % 2, :]
                t13 = t1.rearrange("p (h c) -> p h c", c=HD)
                t23 = a.t2[:, t % 2, :].rearrange("p (h c) -> p h c", c=HD)
                nh = heads
                v_out = a.v[:, t, :, 0:vd]
                dve.wait_ge(proj, t + 1)
                psv = m.ps[:, 2 * (t % 2) + 1, 0:D].rearrange("p (h c) -> p h c", h=nh)
                if bias is not None:
                    dve.tensor_tensor(qk, m.ps[:, 2 * (t % 2), :], bias[:, 0:512], ALU.add).then_inc(taken, 1)
                    dve.tensor_tensor(v_out, psv, bias[:, 512:768].rearrange("p (h c) -> p h c", h=nh),
                                      ALU.add).then_inc(taken, 1)
                else:
                    dve.tensor_copy(qk, m.ps[:, 2 * (t % 2), :]).then_inc(taken, 1)
                    dve.tensor_copy(v_out, psv).then_inc(taken, 1)
                dve.wait_ge(taken, 2 * t + 1)
                if rms:
                    dve.wait_ge(squared, t + 1)
                    ss = m.small[:, 0:gh]
                    rr = m.small[:, gh:2 * gh]
                    std = m.small[:, 2 * gh:3 * gh]
                    step(dve.tensor_reduce(ss, t13, AX.X, ALU.add))
                    dve.tensor_scalar(ss, ss, 1.0 / HD, RMS_EPS, ALU.mult, ALU.add).then_inc(rms_in, 1)
                    dve.wait_ge(rms_std, t + 1)
                    step(dve.reciprocal(rr, std))
                    step(dve.tensor_tensor(qk3, qk3, rr.unsqueeze(2).broadcast_to([P, gh, HD]), ALU.mult))
                step(dve.tensor_tensor(t13, qk3, cos[t], ALU.mult))
                dve.tensor_tensor(t23[:, :, 0:half], qk3[:, :, half:HD],
                                  sin[t][:, :, 0:half], ALU.mult)
                step(dve.tensor_tensor(t23[:, :, half:HD], qk3[:, :, 0:half],
                                       sin[t][:, :, half:HD], ALU.mult))
                if t >= 2:
                    dve.wait_ge(lo, 3 * (t - 1))
                dve.tensor_tensor(qk, t1, a.t2[:, t % 2, :], ALU.add).then_inc(rotated, 1)
                if t >= 1:
                    dve.wait_ge(turned, t)
                    dve.tensor_copy(a.q[:, :, (t - 1) * P:t * P],
                                    m.ps[:, 4, :].bitcast(F16).rearrange("p (n c) -> p n c", c=P)).then_inc(stored, 1)
            dve.wait_ge(turned, NT)
            dve.tensor_copy(a.q[:, :, (NT - 1) * P:NT * P],
                            m.ps[:, 4, :].bitcast(F16).rearrange("p (n c) -> p n c", c=P)).then_inc(stored, 1)

        @block.scalar
        def _(act):
            def store(t):
                act.wait_ge(turned, t + 1)
                act.activation(a.k[:, :, t * P:(t + 1) * P],
                               m.ps[:, 5:7, :].rearrange("p a b -> p (a b)").bitcast(F16).rearrange(
                                   "p (n c) -> p n c", c=P), ACT.Copy).then_inc(stored, 1)

            for t in range(NT):
                qk3 = a.qk[:, t % 2, :].rearrange("p (h c) -> p h c", c=HD)
                if rms:
                    act.wait_ge(taken, 2 * t + 1)
                    if t >= 2:
                        act.wait_ge(rotated, t - 1)
                    act.activation(a.t1[:, t % 2, :], a.qk[:, t % 2, :], ACT.Square).then_inc(squared, 1)
                    act.wait_ge(rms_in, t + 1)
                    act.activation(m.small[:, 4 * NM:6 * NM], m.small[:, 0:2 * NM], ACT.Sqrt).then_inc(rms_std, 1)
                act.wait_ge(rotated, t + 1)
                if t >= 2:
                    act.wait_ge(turned, t - 1)
                if t == 0:
                    act.wait_ge(cleared, 4)
                qs4 = a.qs[:, t % 2, :].rearrange("p (h s c) -> p h s c", h=NM, c=HD)
                act.activation(qs4[:, :, 0:2, :], qk3[:, 0:NM, :].unsqueeze(2).broadcast_to([P, NM, 2, HD]),
                               ACT.Copy).then_inc(hi, 1)
                for parity in range(2):
                    act.activation(kcols(t % 2, parity, 0, 2, 2),
                                   qk3[:, NM + parity:2 * NM:2, :].unsqueeze(2).broadcast_to([P, NM // 2, 2, HD]),
                                   ACT.Copy).then_inc(hi, 1)
                if t >= 1:
                    store(t - 1)
            store(NT - 1)

        @block.gpsimd
        def _(pool):
            pool.memset(a.qs[:, :, :].bitcast(F32), 0.0).then_inc(cleared, 1)
            pool.memset(a.ks[:, :, :].bitcast(F32), 0.0).then_inc(cleared, 1)
            pool.wait_ge(cleared, 2)
            for parity in range(2):
                c0 = 192 * parity + M_ROW
                pool.memset(a.ks[:, :, :].rearrange("p b (n c) -> p b n c", c=2 * P)[:, :, :, c0:c0 + 2],
                            1.0).then_inc(cleared, 1)
            pool.memset(a.v[:, :, :, vd:vd + 1], 1.0)
            for t in range(NT):
                qk3 = a.qk[:, t % 2, :].rearrange("p (h c) -> p h c", c=HD)
                qs4 = a.qs[:, t % 2, :].rearrange("p (h s c) -> p h s c", h=NM, c=HD)
                pool.wait_ge(hi, 3 * (t + 1))
                pool.tensor_tensor(qs4[:, :, 2, :], qk3[:, 0:NM, :], qs4[:, :, 0, :], ALU.subtract).then_inc(stacked, 1)
                for parity in range(2):
                    pool.tensor_tensor(kcols(t % 2, parity, 1), qk3[:, NM + parity:2 * NM:2, :],
                                       kcols(t % 2, parity, 0), ALU.subtract).then_inc(stacked, 1)
                pool.wait_ge(stacked, 3 * (t + 1))
                for _ in range(3):
                    pool.sem_inc(lo, 1)


class MaximumPass:

    SEMAPHORES = ("score_block_in", "score_block_out", "max_steps", "max_split", "max_rows_set_0", "max_rows_set_1")

    def __init__(self, m, a, sems):
        self.m, self.a, self.maps = m, a, 4
        self.block_in, self.block_out, self.steps, self.split_done, *self.rows_set = sems
        self.step_count = 0
        self.items, self.done = [], {}
        for g in range(NM // self.maps):
            i = 0
            for h in range(self.maps):
                for qt in range(NT):
                    for c in range(qt // TC + 1):
                        self.items.append(("block", g, h, qt, c))
                        i += 1
                        if i == 4 and g:
                            self.items.append(("turn", g - 1))
            self.done[len(self.items) - 1] = g
        self.items.append(("turn", NM // self.maps - 1))
        self.banks, self.share = [], {}

    def share_out(self, slots):
        total = 0.0
        for key, number, banks in slots:
            total += number
            start = len(self.banks)
            while len(self.banks) < min(round(total), len(self.items)):
                self.banks.append(banks[len(self.banks) % len(banks)])
            self.share[key] = range(start, len(self.banks))
        assert len(self.banks) == len(self.items)

    def bank(self, n):
        return self.m.ps[:, self.banks[n], :]

    def tensor_item(self, pe, n):
        m, a = self.m, self.a
        out = self.bank(n)
        if self.items[n][0] == "turn":
            g = self.items[n][1]
            pe.wait_ge(self.split_done, g + 1)
        before = [i for i in range(n) if self.banks[i] == self.banks[n]]
        if before:
            pe.wait_ge(self.block_out, before[-1] + 1)
        if self.items[n][0] == "turn":
            rows_out = out[0:2 * self.maps, :].bitcast(F16)
            for qt in range(NT):
                last = pe.transpose(rows_out[:, qt * P:(qt + 1) * P], a.mt[:, g % 2, qt, :], m.ident_h[:, :])
            last.then_inc(self.block_in, 1)
            return
        _, g, h, qt, c = self.items[n]
        w = min(CH, (qt + 1) * P - c * CH)
        diag = qt // TC == c
        hh = g * self.maps + h
        last = pe.matmul(out[:, 0:w], a.q[:, hh // 2, qt * P:(qt + 1) * P], a.k[:, hh, c * CH:c * CH + w],
                         start=True, stop=not diag)
        if diag:
            last = pe.matmul(out[:, w - P:w], m.ident_b[:, :], m.mask_qk[:, :], start=False, stop=True)
        last.then_inc(self.block_in, 1)

    def step(self, dve, instruction):
        self.step_count += 1
        instruction.then_inc(self.steps, 1)
        dve.wait_ge(self.steps, self.step_count)

    def tensor_share(self, pe, key):
        for n in self.share.get(key, ()):
            self.tensor_item(pe, n)

    def vector_share(self, dve, key):
        for n in self.share.get(key, ()):
            self.vector_item(dve, n)

    def vector_start(self, dve):
        self.step(dve, dve.memset(self.a.mp[:, :, :, :], NEG))

    def vector_item(self, dve, n):
        a, out = self.a, self.bank(n)
        dve.wait_ge(self.block_in, n + 1)
        if self.items[n][0] == "turn":
            g = self.items[n][1]
            if g >= 2:
                dve.wait_ge(self.rows_set[g % 2], 16 * self.maps * (g // 2))
            dve.tensor_copy(a.mrow[0:2 * self.maps, g % 2, :], out[0:2 * self.maps, :].bitcast(F16)
                            ).then_inc(self.block_out, 1)
            return
        _, g, h, qt, c = self.items[n]
        w = min(CH, (qt + 1) * P - c * CH)
        dve.reduce_max(a.mp[:, h, qt, c:c + 1], out[:, 0:w], AX.X).then_inc(self.block_out, 1)
        if n in self.done:
            dve.wait_ge(self.block_out, n + 1)
            mt = a.mt[:, g % 2, :, :].rearrange("p t (h s) -> p h t s", s=2)
            self.step(dve, dve.tensor_reduce(a.mf[:, :, :], a.mp[:, :, :, :], AX.X, ALU.max, negate=True))
            self.step(dve, dve.tensor_copy(mt[:, :, :, 0], a.mf[:, :, :]))
            dve.tensor_tensor(mt[:, :, :, 1], a.mf[:, :, :], mt[:, :, :, 0], ALU.subtract).then_inc(self.split_done, 1)

    def sync_rows(self, sp):
        for n, item in enumerate(self.items):
            if item[0] == "turn":
                g = item[1]
                sp.wait_ge(self.block_out, n + 1)
                for h in range(self.maps):
                    r0 = M_ROW + 64 * (h % 2)
                    sp.dma_start(self.a.q[r0:r0 + 2, (g * self.maps + h) // 2, :],
                                 self.a.mrow[2 * h:2 * h + 2, g % 2, :]).then_inc(self.rows_set[g % 2], 16)
        for rows_set in self.rows_set:
            sp.wait_ge(rows_set, 16 * NM // 2)


def attention(nc, m, a, maps, width):
    groups = NM // maps
    n_exp = NM * NT
    ring = a.p.shape[1]
    lag = 1 if maps == 4 else 2
    with stage(nc, "scored", "exped", "summed", "evac") as (block, scored, exped, summed, evac):
        @block.tensor
        def _(pe):
            def score(u):
                n, hh = divmod(u, maps)
                g, kt = divmod(n, NT)
                h = g * maps + hh
                if u >= 3:
                    pe.wait_ge(exped, u - 2)
                bank = 2 + 2 * (u % 3)
                for c in range(kt // TC, NC):
                    q0 = max(kt * P, c * CH)
                    diag = c == kt // TC
                    last = pe.matmul(m.ps[:, bank + c, q0 - c * CH:CH], a.k[:, h, kt * P:(kt + 1) * P],
                                     a.q[:, h // 2, q0:(c + 1) * CH], start=True, stop=not diag)
                    if diag:
                        last = pe.matmul(m.ps[:, bank + c, q0 - c * CH:q0 - c * CH + P], m.ident_b[:, :],
                                         m.mask_kq[:, :], start=False, stop=True)
                last.then_inc(scored, 1)

            def values(n):
                g, kt = divmod(n, NT)
                pe.wait_ge(exped, maps * (n + 1))
                for c in range(kt // TC, NC):
                    if kt == 0 and g >= 1:
                        pe.wait_ge(evac, NC * (g - 1) + c + 1)
                    q0 = max(kt * P, c * CH)
                    for hh in range(maps):
                        h = g * maps + hh
                        p = a.p[:, (maps * n + hh) % ring, q0:(c + 1) * CH]
                        vh = h * a.v.shape[2] // NM
                        w = a.v.shape[3]
                        last = pe.matmul(m.ps[width * hh:width * hh + w, c, q0 - c * CH:CH], a.v[:, kt, vh, :], p,
                                         start=(kt == 0), stop=(kt == TC * (c + 1) - 1))
                last.then_inc(summed, 1)

            for n in range(groups * NT):
                for hh in range(maps):
                    score(maps * n + hh)
                    if hh == 1 and n >= lag:
                        values(n - lag)
            for n in range(groups * NT - lag, groups * NT):
                values(n)

        @block.scalar
        def _(act):
            def store(g, c):
                act.wait_ge(summed, NT * g + TC * (c + 1))
                act.activation(a.o[:, g, c * CH:(c + 1) * CH], m.ps[:, c, :], ACT.Copy).then_inc(evac, 1)

            for u in range(n_exp):
                n, hh = divmod(u, maps)
                g, kt = divmod(n, NT)
                act.wait_ge(scored, u + 1)
                if u >= ring:
                    act.wait_ge(summed, (u - ring) // maps + 1)
                bank = 2 + 2 * (u % 3)
                act.activation(a.p[:, u % ring, kt * P:S],
                               m.ps[:, bank:bank + 2, :].rearrange("p a b -> p (a b)")[:, kt * P:S],
                               ACT.Exp, scale=HD ** -0.5).then_inc(exped, 1)
                if hh == maps - 1:
                    if kt == TC - 1 + lag:
                        store(g, 0)
                    if kt == lag - 1 and g >= 1:
                        store(g - 1, 1)
            store(groups - 1, 1)


def attention_finish(nc, m, a, maps, width, wout, out_scale, batch=None):
    groups = NM // maps
    banks = groups * P // CH
    with stage(nc, "turned", "steps", "given", "y_turned", "y_stored", "projected", "added") as \
            (block, turned, steps, given, y_turned, y_stored, projected, added):
        @block.tensor
        def _(pe):
            def project(t):
                pe.wait_ge(given, t + 1)
                if t >= 1:
                    pe.wait_ge(y_stored, t)
                for k in range(KD):
                    last = pe.transpose(m.ps[:, 6, k * P:(k + 1) * P], a.y[:, t % 2, k * P:(k + 1) * P], m.ident[:, :])
                last.then_inc(y_turned, 1)
                pe.wait_ge(y_stored, t + 1)
                if t >= 1:
                    pe.wait_ge(added, t)
                for k in range(KD):
                    last = pe.matmul(m.ps[:, 7, 0:D], a.yt[:, t % 2, k * P:(k + 1) * P], wout[:, k, :],
                                     start=(k == 0), stop=(k == KD - 1))
                last.then_inc(projected, 1)

            for t in range(NT):
                if t >= 2:
                    pe.wait_ge(given, t - 1)
                bank = banks * (t % 2)
                for g in range(groups):
                    last = pe.transpose(m.ps[:, bank + g // TC, (g % TC) * P:(g % TC + 1) * P],
                                        a.o[:, g, t * P:(t + 1) * P], m.ident[:, :])
                last.then_inc(turned, 1)
                if wout is not None and t >= 1:
                    project(t - 1)
            if wout is not None:
                project(NT - 1)

        if wout is not None:
            @block.scalar
            def _(act):
                for t in range(NT):
                    act.wait_ge(y_turned, t + 1)
                    act.activation(a.yt[:, t % 2, :], m.ps[:, 6, 0:D], ACT.Copy).then_inc(y_stored, 1)

        @block.vector
        def _(dve):
            step = Steps(dve, steps)

            def add(t):
                dve.wait_ge(projected, t + 1)
                dve.scalar_tensor_tensor(sum_place(m, batch, t), m.ps[:, 7, 0:D], out_scale, sum_so_far(m, batch, t),
                                         ALU.mult, ALU.add).then_inc(added, 1)

            for t in range(NT):
                bank = banks * (t % 2)
                sums = m.ps[:, bank:bank + banks, :].rearrange("p a b -> p (a b)").rearrange("p (h c) -> p h c", c=width)
                y = a.y[:, t % 2, :]
                dve.wait_ge(turned, t + 1)
                if t >= 1:
                    dve.wait_ge(given, t)
                if maps == 4:
                    r = m.small[:, 0:NM]
                    y3 = y.rearrange("p (h c) -> p h c", c=HD)
                    step(dve.reciprocal(r, sums[:, :, HD]))
                    if wout is not None and t >= 2:
                        dve.wait_ge(y_turned, t - 1)
                    ins = dve.tensor_tensor(y3, sums[:, :, 0:HD], r.unsqueeze(2).broadcast_to([P, NM, HD]), ALU.mult)
                    if wout is not None:
                        ins.then_inc(given, 1)
                    else:
                        ins.then_inc(given, 1)
                        dve.wait_ge(given, t + 1)
                        dve.tensor_tensor(sum_place(m, batch, t), m.acc[:, t, :], y, ALU.add)
                else:
                    vd = 2 * HD
                    r = m.small[:, 0:NM]
                    pair = sums.rearrange("p (h s) c -> p h s c", s=2)
                    r2 = r.rearrange("p (h s) -> p h s", s=2)
                    y3 = y.rearrange("p (h c) -> p h c", c=vd)
                    z3 = a.z[:, :].rearrange("p (h c) -> p h c", c=vd)
                    step(dve.reciprocal(r, sums[:, :, vd]))
                    step(dve.tensor_scalar(r2[:, :, 1], r2[:, :, 1], m.lam[:, 0:1], None, ALU.mult))
                    if t >= 2:
                        dve.wait_ge(y_turned, t - 1)
                    dve.tensor_tensor(y3, pair[:, :, 0, 0:vd], r2[:, :, 0].unsqueeze(2).broadcast_to([P, NM // 2, vd]),
                                      ALU.mult)
                    step(dve.tensor_tensor(z3, pair[:, :, 1, 0:vd],
                                           r2[:, :, 1].unsqueeze(2).broadcast_to([P, NM // 2, vd]), ALU.mult))
                    dve.tensor_tensor(y, y, a.z[:, :], ALU.subtract).then_inc(given, 1)
                    dve.wait_ge(given, t + 1)
                if wout is not None and t >= 1:
                    add(t - 1)
            if wout is not None:
                add(NT - 1)


def attention_memory(m, ar, heads, vd, groups, ring):
    a = Memory()
    a.q = ar.take(NM // 2, S, dtype=F16)
    a.k = ar.take(NM, S, dtype=F16)
    a.v = ar.take(NT, heads, vd + 1)
    a.mp = ar.take(4, NT, 2)
    a.mf = ar.take(4, NT)
    a.mt = ar.take(2, NT, 8, dtype=F16)
    a.mrow = ar.take(2, S, dtype=F16)
    base = ar.at
    a.free = base
    a.p = ar.take(ring, S)
    a.o = ar.take(groups, S)
    pre = Arena(ar.tensor, base)
    a.qk = pre.take(2, 512)
    a.t1 = pre.take(2, 512)
    a.t2 = pre.take(2, 512)
    a.qs = pre.take(2, NM * 64, dtype=F16)
    a.ks = pre.take(2, NM * P, dtype=F16)
    post = Arena(ar.tensor, base)
    a.y = post.take(2, D)
    a.yt = post.take(2, D)
    a.z = post.take(D)
    a.xn = Arena(ar.tensor, base).take(NT, D)
    return a



def gated_ffn(nc, m, f, wg, wu, wd, rms, batch):
    ni = F1 // P
    with stage(nc, "upped", "silued", "gated", "squared", "downed", "added", "steps", "sumsq", "ms_in", "rms_done") as \
            (block, upped, silued, gated, squared, downed, added, steps, sumsq, ms_in, rms_done):
        ms, root, inv = m.small[:, 0:TC], m.small[:, TC:2 * TC], m.small[:, 2 * TC:3 * TC]

        @block.tensor
        def _(pe):
            def up(c, i):
                n = c * ni + i
                if n >= 2:
                    pe.wait_ge(gated, n - 1)
                for j, w in enumerate((wg, wu)):
                    for k in range(KD):
                        last = pe.matmul(m.ps[:, 2 * (n % 2) + j, :], w[:, k, i * P:(i + 1) * P],
                                         m.xn_t[:, k, c * CH:(c + 1) * CH], start=(k == 0), stop=(k == KD - 1))
                last.then_inc(upped, 1)

            def down(c):
                pe.wait_ge(gated, ni * (c + 1))
                if rms:
                    pe.wait_ge(squared, ni * (c + 1))
                    for j in range(TC):
                        for i in range(ni):
                            last = pe.matmul(m.ps[:, 6, j:j + 1], f.sq[:, i, j * P:(j + 1) * P],
                                             m.ones_col[:, 0:1], start=(i == 0), stop=(i == ni - 1))
                    last.then_inc(sumsq, 1)
                for j in range(TC):
                    t = c * TC + j
                    if t >= 2:
                        pe.wait_ge(added, t - 1)
                    for i in range(ni):
                        last = pe.matmul(m.ps[:, 4 + t % 2, 0:D], f.inter[:, c % 2, i, j * P:(j + 1) * P], wd[:, i, :],
                                         start=(i == 0), stop=(i == ni - 1))
                    last.then_inc(downed, 1)

            for c in range(NC):
                for i in range(ni):
                    up(c, i)
                    if i == 1 and c >= 1:
                        down(c - 1)
            down(NC - 1)

        @block.scalar
        def _(act):
            def roots(c):
                act.wait_ge(ms_in, c + 1)
                act.activation(root, ms, ACT.Sqrt).then_inc(rms_done, 1)

            for c in range(NC):
                for i in range(ni):
                    n = c * ni + i
                    act.wait_ge(upped, n + 1)
                    if n >= 2:
                        act.wait_ge(gated, n - 1)
                    act.activation(f.gate[:, n % 2, :], m.ps[:, 2 * (n % 2), :], ACT.Silu).then_inc(silued, 1)
                    if rms and i == 1 and c >= 1:
                        roots(c - 1)
                if rms:
                    for i in range(ni):
                        if c >= 1 and i == 0:
                            act.wait_ge(sumsq, c)
                        act.wait_ge(gated, c * ni + i + 1)
                        act.activation(f.sq[:, i, :], f.inter[:, c % 2, i, :], ACT.Square).then_inc(squared, 1)
            if rms:
                roots(NC - 1)

        @block.vector
        def _(dve):
            step = Steps(dve, steps)

            def add(c):
                if rms:
                    dve.wait_ge(sumsq, c + 1)
                    dve.tensor_scalar(ms, m.ps[:, 6, 0:TC], 1.0 / F1, RMS_EPS, ALU.mult, ALU.add).then_inc(ms_in, 1)
                    dve.wait_ge(rms_done, c + 1)
                    if c >= 1:
                        dve.wait_ge(added, TC * c)
                    step(dve.reciprocal(inv, root))
                for j in range(TC):
                    t = c * TC + j
                    dve.wait_ge(downed, t + 1)
                    out = m.ps[:, 4 + t % 2, 0:D]
                    if rms:
                        dve.scalar_tensor_tensor(sum_place(m, batch, t), out, inv[:, j:j + 1], m.acc[:, t, :],
                                                 ALU.mult, ALU.add).then_inc(added, 1)
                    else:
                        dve.tensor_tensor(sum_place(m, batch, t), out, m.acc[:, t, :], ALU.add).then_inc(added, 1)

            for c in range(NC):
                for i in range(ni):
                    n = c * ni + i
                    dve.wait_ge(silued, n + 1)
                    if c >= 2 and i == 0:
                        dve.wait_ge(downed, TC * (c - 1))
                    dve.tensor_tensor(f.inter[:, c % 2, i, :], f.gate[:, n % 2, :], m.ps[:, 2 * (n % 2) + 1, :],
                                      ALU.mult).then_inc(gated, 1)
                    if i == 1 and c >= 1:
                        add(c - 1)
            add(NC - 1)



def route(nc, m, f, w_router):
    with stage(nc, "logits", "steps", "shifted", "exped") as (block, logits, steps, shifted, exped):
        @block.tensor
        def _(pe):
            for t in range(NT):
                for k in range(KD):
                    last = pe.matmul(m.ps[:, 0, t * E_RT:(t + 1) * E_RT], m.xn_t[:, k, t * P:(t + 1) * P],
                                     w_router[:, k, :], start=(k == 0), stop=(k == KD - 1))
            last.then_inc(logits, 1)

        @block.scalar
        def _(act):
            act.wait_ge(shifted, 1)
            act.activation(f.prob[:, :, :], f.prob[:, :, :], ACT.Exp).then_inc(exped, 1)

        @block.vector
        def _(dve):
            step = Steps(dve, steps)
            lg = m.ps[:, 0, 0:NT * E_RT].rearrange("p (t e) -> p t e", e=E_RT)
            mx = m.small[:, 0:NT]
            dve.wait_ge(logits, 1)
            step(dve.reduce_max(mx, lg, AX.X))
            dve.tensor_tensor(f.prob[:, :, :], lg, mx.unsqueeze(2).broadcast_to([P, NT, E_RT]),
                              ALU.subtract).then_inc(shifted, 1)
            dve.wait_ge(exped, 1)
            step(dve.tensor_reduce(mx, f.prob[:, :, :], AX.X, ALU.add))
            step(dve.reciprocal(mx, mx))
            step(dve.tensor_tensor(f.prob[:, :, :], f.prob[:, :, :], mx.unsqueeze(2).broadcast_to([P, NT, E_RT]),
                                   ALU.mult))
            for t in range(NT):
                dve.max(f.top[:, t, :], f.prob[:, t, :]).then_inc(steps, 1)
            step.count += NT
            dve.wait_ge(steps, step.count)
            for t in range(NT):
                dve.max_index(f.idx[:, t, :], f.top[:, t, :], f.prob[:, t, :]).then_inc(steps, 1)
            step.count += NT
            dve.wait_ge(steps, step.count)
            step(dve.tensor_copy(f.idxf[:, :, :], f.idx[:, :, :]))
            for t in range(NT):
                for r, out in enumerate((f.gate_w, f.prob)):
                    dve.tensor_scalar(out[:, t, :], m.iota16[:, :], f.idxf[:, t, r:r + 1], f.top[:, t, r:r + 1],
                                      ALU.is_equal, ALU.mult).then_inc(steps, 1)
            step.count += 2 * NT
            dve.wait_ge(steps, step.count)
            dve.tensor_tensor(f.gate_w[:, :, :], f.gate_w[:, :, :], f.prob[:, :, :], ALU.add)


def experts(nc, m, f, a, wup, wdown):
    ne = E_SH + E_RT
    units = NC * ne
    with stage(nc, "upped", "gelued", "downed", "added", *MaximumPass.SEMAPHORES) as \
            (block, upped, gelued, downed, added, *max_sems):
        mp = MaximumPass(m, a, max_sems)
        slots = KD + TC
        mp.share_out([((n, i), len(mp.items) / (slots * units), (4, 5, 6, 7))
                      for n in range(units) for i in range(slots)])

        def product(n, j):
            return m.ps[:, 2 + j // 2, (j % 2) * D:(j % 2 + 1) * D]

        @block.tensor
        def _(pe):
            def down(n, j):
                c, e = divmod(n, ne)
                if j == 0:
                    pe.wait_ge(gelued, n + 1)
                u = n * TC + j
                if j % 2 == 0 and n >= 1:
                    pe.wait_ge(added, u - TC + 2)
                last = pe.matmul(product(n, j), f.mid[:, n % 3, j * P:(j + 1) * P], wdown[:, e, :],
                                 start=True, stop=True)
                if j % 2 == 1:
                    last.then_inc(downed, 1)

            for n in range(units + 1):
                if n < units:
                    c, e = divmod(n, ne)
                    if n >= 2:
                        pe.wait_ge(gelued, n - 1)
                    for k in range(KD):
                        last = pe.matmul(m.ps[:, n % 2, :], wup[:, e, k, :], m.xn_t[:, k, c * CH:(c + 1) * CH],
                                         start=(k == 0), stop=(k == KD - 1))
                        if k == KD - 1:
                            last.then_inc(upped, 1)
                        mp.tensor_share(pe, (n, k))
                for j in range(TC):
                    mp.tensor_share(pe, (n, KD + j))
                    if n >= 1:
                        down(n - 1, j)

        @block.scalar
        def _(act):
            for n in range(units):
                act.wait_ge(upped, n + 1)
                if n >= 3:
                    act.wait_ge(downed, TC // 2 * (n - 2))
                act.activation(f.mid[:, n % 3, :], m.ps[:, n % 2, :], ACT.Gelu).then_inc(gelued, 1)

        @block.vector
        def _(dve):
            def add(n, j):
                c, e = divmod(n, ne)
                u = n * TC + j
                t = c * TC + j
                dve.wait_ge(downed, u // 2 + 1)
                if e >= 1:
                    dve.wait_ge(added, u - TC + 1)
                out = product(n, j)
                if e < E_SH:
                    dve.tensor_tensor(m.acc[:, t, :], out, m.acc[:, t, :], ALU.add).then_inc(added, 1)
                else:
                    dve.scalar_tensor_tensor(m.acc[:, t, :], out, f.gate_w[:, t, e - E_SH:e - E_SH + 1],
                                             m.acc[:, t, :], ALU.mult, ALU.add).then_inc(added, 1)

            mp.vector_start(dve)
            for n in range(units + 1):
                for k in range(KD):
                    mp.vector_share(dve, (n, k))
                for j in range(TC):
                    mp.vector_share(dve, (n, KD + j))
                    if n >= 1:
                        add(n - 1, j)

        @block.sync
        def _(sp):
            mp.sync_rows(sp)



def spline_weights(nc, m, f, io, wg, wu, wd):
    nt = F1 // P
    with stage(nc, "windows_in", "basis_in_0", "basis_in_1", "formed", "steps", "turned", "stored") as \
            (block, windows_in, basis_in_0, basis_in_1, formed, steps, turned, stored):
        basis_in = (basis_in_0, basis_in_1)
        basis_gu = io.basis.rearrange("s (t p) n -> t p s n", p=P)
        basis_d = io.basis.rearrange("s (h p c) n -> h c p s n", p=P, c=4)
        tiles = [("gu", t) for t in range(nt)] + [("d", t) for t in range(nt)]
        units = []
        for n, (kind, t) in enumerate(tiles):
            if kind == "gu":
                for w, win in ((wg, f.win[:, 0, t, :]), (wu, f.win[:, 1, t, :])):
                    units.append((n, win, w[:, :, t * P:(t + 1) * P]))
            else:
                h, c = divmod(t, 4)
                units.append((n, f.win[:, 2, t, :], wd[:, 2 * c:2 * c + 2, h * P:(h + 1) * P]))

        @block.sync
        def _(sp):
            for i, win in enumerate((io.win_gate, io.win_up)):
                sp.dma_start(f.win[:, i, :, :], rows(win)).then_inc(windows_in, 16)
            for h in range(KD):
                sp.dma_start(f.win[:, 2, 4 * h:4 * h + 4, :],
                             io.win_down.rearrange("(h p c) s -> h p c s", p=P, c=4)[h]).then_inc(windows_in, 16)
            for n, (kind, t) in enumerate(tiles):
                if n >= 2:
                    last_use = max(i for i, u in enumerate(units) if u[0] == n - 2)
                    sp.wait_ge(formed, last_use + 1)
                src = basis_gu[t] if kind == "gu" else basis_d[t // 4][t % 4]
                sp.dma_start(f.basis[:, n % 2, :, :], src).then_inc(basis_in[n % 2], 16)

        @block.vector
        def _(dve):
            step = Steps(dve, steps)
            dve.wait_ge(windows_in, 64)
            for i, (n, win, out) in enumerate(units):
                dve.wait_ge(basis_in[n % 2], 16 * (n // 2 + 1))
                if i >= 2:
                    dve.wait_ge(turned, i - 1)
                w = f.w[:, i % 2, :]
                step(dve.tensor_scalar(w, f.basis[:, n % 2, 0, :], win[:, 0:1], None, ALU.mult))
                for s in range(1, NSEG):
                    ins = dve.scalar_tensor_tensor(w, f.basis[:, n % 2, s, :], win[:, s:s + 1], w, ALU.mult, ALU.add)
                    if s < NSEG - 1:
                        step(ins)
                ins.then_inc(formed, 1)

        @block.tensor
        def _(pe):
            for i in range(len(units)):
                pe.wait_ge(formed, i + 1)
                if i >= 2:
                    pe.wait_ge(stored, i - 1)
                for k in range(KD):
                    last = pe.transpose(m.ps[:, i % 2, k * P:(k + 1) * P], f.w[:, i % 2, k * P:(k + 1) * P],
                                        m.ident[:, :])
                last.then_inc(turned, 1)

        @block.scalar
        def _(act):
            for i, (n, win, out) in enumerate(units):
                act.wait_ge(turned, i + 1)
                act.activation(out, m.ps[:, i % 2, 0:D].rearrange("p (k n) -> p k n", k=KD), ACT.Copy).then_inc(stored, 1)


def lambda_scalar(nc, m, f, io):
    n = 2 * HD
    with stage(nc, "lam_in", "steps", "dots", "exped") as (block, lam_in, steps, dots, exped):
        @block.sync
        def _(sp):
            for i, src in enumerate((io.lq1, io.lk1, io.lq2, io.lk2)):
                sp.dma_start(f.lqk[:, i, :], src.partition_broadcast(P)).then_inc(lam_in, 16)

        @block.vector
        def _(dve):
            step = Steps(dve, steps)
            dve.wait_ge(lam_in, 64)
            pair = f.lqk[:, :, :].rearrange("p (a b) n -> p a b n", b=2)
            step(dve.tensor_tensor(f.dot[:, :, :], pair[:, :, 0, :], pair[:, :, 1, :], ALU.mult))
            dve.tensor_reduce(m.small[:, 0:2], f.dot[:, :, :], AX.X, ALU.add).then_inc(dots, 1)
            dve.wait_ge(exped, 1)
            step(dve.tensor_tensor(m.lam[:, :], m.small[:, 2:3], m.small[:, 3:4], ALU.subtract))
            dve.tensor_scalar(m.lam[:, :], m.lam[:, :], LAMBDA_INIT, None, ALU.add)

        @block.scalar
        def _(act):
            act.wait_ge(dots, 1)
            act.activation(m.small[:, 2:4], m.small[:, 0:2], ACT.Exp).then_inc(exped, 1)



def ternary_weights(nc, m, f, io, wgu, wp):
    ngu, npj = 2 * F1 // P, D // P
    n_gu, n_p = ngu * D // GROUP, npj * F1 // GROUP
    ng = n_gu + n_p
    with stage(nc, "raw_in", "steps", "ready", "turned", "stored") as (block, raw_in, steps, ready, turned, stored):
        @block.sync
        def _(sp):
            sp.dma_start(f.raw[:, 0:n_gu * GROUP].rearrange("p (t n) -> p t n", n=D), rows(io.w_gate_up)).then_inc(raw_in, 16)
            sp.dma_start(f.raw[:, n_gu * GROUP:ng * GROUP].rearrange("p (t n) -> p t n", n=F1),
                         rows(io.w_proj)).then_inc(raw_in, 16)

        @block.vector
        def _(dve):
            step = Steps(dve, steps)
            g3 = lambda ap: ap.rearrange("p (g n) -> p g n", n=GROUP)
            bc = lambda s: s.unsqueeze(2).broadcast_to([P, ng, GROUP])
            dve.wait_ge(raw_in, 32)
            step(dve.tensor_copy(f.wb[:, :], f.raw[:, :]))
            step(dve.tensor_reduce(f.thr[:, :], g3(f.wb[:, :]), AX.X, ALU.add, apply_absolute_value=True))
            step(dve.tensor_scalar(f.sc[:, :], f.thr[:, :], 1.0 / GROUP, None, ALU.mult))
            step(dve.tensor_scalar(f.sc[:, :], f.sc[:, :], 1e-8, None, ALU.max))
            step(dve.tensor_scalar(f.thr[:, :], f.sc[:, :], 257.0 / 512.0, None, ALU.mult))
            step(dve.tensor_tensor(g3(f.q1[:, :]), g3(f.wb[:, :]), bc(f.thr[:, :]), ALU.is_gt))
            step(dve.tensor_scalar(f.thr[:, :], f.thr[:, :], -1.0, None, ALU.mult))
            step(dve.tensor_tensor(g3(f.q2[:, :]), g3(f.wb[:, :]), bc(f.thr[:, :]), ALU.is_lt))
            step(dve.tensor_tensor(f.q1[:, :], f.q1[:, :], f.q2[:, :], ALU.subtract))
            step(dve.tensor_tensor(g3(f.q1[:, :]), g3(f.q1[:, :]), bc(f.sc[:, :]), ALU.mult))
            step(dve.tensor_tensor(f.q1[:, :], f.q1[:, :], f.wb[:, :], ALU.subtract))
            dve.tensor_tensor(f.q1[:, :], f.q1[:, :], f.wb[:, :], ALU.add).then_inc(ready, 1)

        turns = [(f.q1[:, (2 * t + k) * P:(2 * t + k + 1) * P], wgu[:, k, t * P:(t + 1) * P])
                 for k in range(KD) for t in range(ngu)]
        turns += [(f.q1[:, n_gu * GROUP + h * F1 + j * P:n_gu * GROUP + h * F1 + (j + 1) * P],
                   wp[:, j, h * P:(h + 1) * P]) for h in range(npj) for j in range(F1 // P)]

        @block.tensor
        def _(pe):
            pe.wait_ge(ready, 1)
            for u in range(len(turns) // 4):
                if u >= 4:
                    pe.wait_ge(stored, 4 * (u - 3))
                for i in range(4):
                    last = pe.transpose(m.ps[:, u % 4, :].bitcast(BF16)[:, i * P:(i + 1) * P], turns[4 * u + i][0],
                                        m.ident_b[:, :])
                last.then_inc(turned, 1)

        @block.scalar
        def _(act):
            for u in range(len(turns) // 4):
                act.wait_ge(turned, u + 1)
                for i in range(4):
                    act.activation(turns[4 * u + i][1], m.ps[:, u % 4, :].bitcast(BF16)[:, i * P:(i + 1) * P],
                                   ACT.Copy).then_inc(stored, 1)


def time_mix_scalars(nc, m, w):
    with stage(nc, "steps") as (block, steps):
        @block.vector
        def _(dve):
            dve.tensor_scalar(w.omix[:, :, :], w.mix[:, :, :], -1.0, 1.0, ALU.mult, ALU.add)

        @block.scalar
        def _(act):
            act.activation(w.decay[:, :], w.td[:, :], ACT.Exp).then_inc(steps, 1)
            act.wait_ge(steps, 1)
            act.activation(w.decay[:, :], w.decay[:, :], ACT.Exp, scale=-1.0)
            act.activation(w.bonus[:, :], w.tf[:, :], ACT.Exp)


def mixed_with_last(dve, step, out, h_t, mix, omix, j):
    for k in range(KD):
        step(dve.tensor_scalar(out[:, k, :], h_t[:, k, 0:S], omix[:, j, k:k + 1], None, ALU.mult))
        ins = dve.scalar_tensor_tensor(out[:, k, :], h_t[:, k, 1:S + 1], mix[:, j, k:k + 1], out[:, k, :],
                                       ALU.mult, ALU.add)
        if k == 0:
            step(ins)
    return ins


def time_mix(nc, m, f, w):
    order = (("k", w.wk, 1), ("v", w.wv, 2), ("r", w.wr, 0))
    with stage(nc, "mixed", "steps", "proj", "k_kept", "kv_made", "r_kept", "wkv", "outed", "added", "summed") as \
            (block, mixed, steps, proj, k_kept, kv_made, r_kept, wkv, outed, added, summed):
        @block.tensor
        def _(pe):
            for n, (name, wt, j) in enumerate(order):
                pe.wait_ge(mixed, n + 1)
                for o in range(KD):
                    for c in range(NC):
                        u = 4 * n + 2 * o + c
                        if u >= 8:
                            pe.wait_ge(k_kept, u - 8 + 1)
                        for k in range(KD):
                            last = pe.matmul(m.ps[:, u % 8, :], wt[:, k, o * P:(o + 1) * P],
                                             f.mix[:, j, k, c * CH:(c + 1) * CH], start=(k == 0), stop=(k == KD - 1))
                        last.then_inc(proj, 1)
            for t in range(NT):
                pe.wait_ge(wkv, KD)
                if t < 4:
                    pe.wait_ge(kv_made, 4)
                else:
                    pe.wait_ge(summed, t - 3)
                for k in range(KD):
                    last = pe.matmul(m.ps[:, 4 + t % 4, 0:D], f.st[:, k, t * P:(t + 1) * P], w.wo[:, k, :],
                                     start=(k == 0), stop=(k == KD - 1))
                last.then_inc(outed, 1)

        @block.scalar
        def _(act):
            for u in range(4):
                act.wait_ge(proj, u + 1)
                act.activation(f.kk[:, u // 2, (u % 2) * CH:(u % 2 + 1) * CH], m.ps[:, u, :], ACT.Copy).then_inc(k_kept, 1)
            for u in range(4):
                act.wait_ge(proj, 8 + u + 1)
                act.activation(f.rs[:, u // 2, (u % 2) * CH:(u % 2 + 1) * CH], m.ps[:, u, :],
                               ACT.Sigmoid).then_inc(r_kept, 1)

        @block.vector
        def _(dve):
            step = Steps(dve, steps)
            for name, wt, j in order:
                mixed_with_last(dve, step, f.mix[:, j, :, :], f.h_t, w.mix, w.omix, j).then_inc(mixed, 1)
            for u in range(4):
                dve.wait_ge(proj, 4 + u + 1)
                dve.wait_ge(k_kept, u + 1)
                part = f.kk[:, u // 2, (u % 2) * CH:(u % 2 + 1) * CH]
                dve.tensor_tensor(part, part, m.ps[:, 4 + u, :], ALU.mult).then_inc(kv_made, 1)
            dve.wait_ge(kv_made, 4)
            for k in range(KD):
                step(dve.tensor_tensor_scan(f.st[:, k, :], w.decay[:, k:k + 1].broadcast_to([P, S]), f.kk[:, k, :],
                                            0.0, ALU.mult, ALU.add))
                step(dve.scalar_tensor_tensor(f.st[:, k, 0:1], f.kk[:, k, 0:1], w.bonus[:, k:k + 1], f.st[:, k, 0:1],
                                              ALU.mult, ALU.add))
                dve.wait_ge(r_kept, 2 * (k + 1))
                dve.tensor_tensor(f.st[:, k, :], f.st[:, k, :], f.rs[:, k, :], ALU.mult).then_inc(wkv, 1)
            for t in range(NT):
                dve.wait_ge(outed, t + 1)
                dve.tensor_tensor(f.xn[:, t, :], f.xn[:, t, :], m.ps[:, 4 + t % 4, 0:D], ALU.add).then_inc(summed, 1)
                dve.wait_ge(summed, t + 1)
                dve.tensor_tensor(m.acc[:, t, :], m.acc[:, t, :], f.xn[:, t, :], ALU.add)


def channel_mix(nc, m, f, w):
    nf = F2 // P
    with stage(nc, "mixed", "steps", "upped", "squared", "gate_in", "gated", "downed", "scaled", "added") as \
            (block, mixed, steps, upped, squared, gate_in, gated, downed, scaled, added):
        @block.tensor
        def _(pe):
            def down(c):
                for j in range(TC):
                    t = c * TC + j
                    if t >= 2:
                        pe.wait_ge(gated, t - 1)
                    for k in range(KD):
                        last = pe.matmul(m.ps[:, 4 + t % 2, 0:D], f.mix[:, 0, k, t * P:(t + 1) * P], w.wcr[:, k, :],
                                         start=(k == 0), stop=(k == KD - 1))
                    last.then_inc(gate_in, 1)
                    pe.wait_ge(squared, nf * (c + 1))
                    if t >= 2:
                        pe.wait_ge(scaled, t - 1)
                    for i in range(nf):
                        last = pe.matmul(m.ps[:, 6 + t % 2, 0:D], f.kc[:, c, i, j * P:(j + 1) * P], w.wcv[:, i, :],
                                         start=(i == 0), stop=(i == nf - 1))
                    last.then_inc(downed, 1)

            pe.wait_ge(mixed, 1)
            for c in range(NC):
                for i in range(nf):
                    n = c * nf + i
                    if n >= 4:
                        pe.wait_ge(squared, n - 3)
                    for k in range(KD):
                        last = pe.matmul(m.ps[:, n % 4, :], w.wck[:, k, i * P:(i + 1) * P],
                                         f.mix[:, 0, k, c * CH:(c + 1) * CH], start=(k == 0), stop=(k == KD - 1))
                    last.then_inc(upped, 1)
            for c in range(NC):
                down(c)

        @block.scalar
        def _(act):
            for n in range(NC * nf):
                act.wait_ge(upped, n + 1)
                act.activation(f.kc[:, n // nf, n % nf, :], m.ps[:, n % 4, :], ACT.Square).then_inc(squared, 1)
            for t in range(NT):
                act.wait_ge(gate_in, t + 1)
                if t >= 2:
                    act.wait_ge(scaled, t - 1)
                act.activation(f.sg[:, t % 2, :], m.ps[:, 4 + t % 2, 0:D], ACT.Sigmoid).then_inc(gated, 1)

        @block.vector
        def _(dve):
            step = Steps(dve, steps)
            mixed_with_last(dve, step, f.mix[:, 0, :, :], f.h_t, w.mix, w.omix, 3).then_inc(mixed, 1)
            for t in range(NT):
                dve.wait_ge(gated, t + 1)
                dve.wait_ge(downed, t + 1)
                if t >= 1:
                    dve.wait_ge(added, t)
                dve.tensor_tensor(f.tmp[:, :], f.sg[:, t % 2, :], m.ps[:, 6 + t % 2, 0:D], ALU.mult).then_inc(scaled, 1)
                dve.wait_ge(scaled, t + 1)
                dve.tensor_tensor(m.acc[:, t, :], m.acc[:, t, :], f.tmp[:, :], ALU.add).then_inc(added, 1)


def clear_first_column(nc, f):
    with stage(nc, "unused", pool=True) as (block, unused):
        @block.gpsimd
        def _(pool):
            pool.memset(f.h_t[:, :, 0:1], 0.0)



def route_pairs(nc, m, f, w_gate):
    with stage(nc, "logits", "kept", "steps", "maxes", "maxes_all", "shifted", "exped", "sums", "sums_all",
               "spread", "turned", pool=True) as \
            (block, logits, kept, steps, maxes, maxes_all, shifted, exped, sums, sums_all, spread, turned):
        tw = f.tw[:, :, :]
        by_slot = tw.rearrange("p t r -> p r t")

        @block.tensor
        def _(pe):
            for t in range(NT):
                for k in range(KD):
                    last = pe.matmul(m.ps[:, 7, t * E3:(t + 1) * E3], m.xn_t[:, k, t * P:(t + 1) * P],
                                     w_gate[:, k, :], start=(k == 0), stop=(k == KD - 1))
            last.then_inc(logits, 1)
            n = 0
            for r in range(2):
                for kind, src in enumerate((f.ohx, f.wx)):
                    for t in range(NT):
                        n += 1
                        pe.wait_ge(spread, n)
                        last = pe.transpose(m.ps[:, 4 * r + 2 * kind + t // TC, (t % TC) * P:(t % TC + 1) * P],
                                            src[:, r, t, :], m.ident[:, :])
                        if t % TC == TC - 1:
                            last.then_inc(turned, 1)

        @block.scalar
        def _(act):
            act.wait_ge(shifted, 1)
            act.activation(tw, tw, ACT.Exp).then_inc(exped, 1)
            for n in range(8):
                r, kind, c = n // 4, n // 2 % 2, n % 2
                act.wait_ge(turned, n + 1)
                dst = (f.oh, f.wb)[kind]
                act.activation(dst[:, r, c * CH:(c + 1) * CH], m.ps[:, n, :], ACT.Copy)

        @block.gpsimd
        def _(pool):
            pool.wait_ge(maxes, 1)
            pool.partition_all_reduce(f.red_all[:, 0:2], f.red[:, 0:2], P, RMAX).then_inc(maxes_all, 1)
            pool.wait_ge(sums, 1)
            pool.partition_all_reduce(f.red_all[:, 2:4], f.red[:, 2:4], P, RADD).then_inc(sums_all, 1)

        @block.vector
        def _(dve):
            step = Steps(dve, steps)
            dve.wait_ge(logits, 1)
            step(dve.tensor_copy(f.lg[:, :, :], m.ps[:, 7, 0:NT * E3].rearrange("p (t e) -> p t e", e=E3)))
            for t in range(NT):
                dve.max(f.top[:, t, :], f.lg[:, t, :]).then_inc(steps, 1)
            step.count += NT
            dve.wait_ge(steps, step.count)
            for t in range(NT):
                dve.max_index(f.idx[:, t, :], f.top[:, t, :], f.lg[:, t, :]).then_inc(steps, 1)
            dve.tensor_reduce(f.red[:, 0:2], f.top[:, :, 0:2].rearrange("p t r -> p r t"), AX.X,
                              ALU.max).then_inc(maxes, 1)
            step.count += NT
            dve.wait_ge(steps, step.count)
            step(dve.tensor_copy(f.idxf[:, :, :], f.idx[:, :, :]))
            dve.wait_ge(maxes_all, 1)
            dve.tensor_tensor(tw, f.top[:, :, 0:2], f.red_all[:, 0:2].unsqueeze(1).broadcast_to([P, NT, 2]),
                              ALU.subtract).then_inc(shifted, 1)
            dve.wait_ge(exped, 1)
            dve.tensor_reduce(f.red[:, 2:4], by_slot, AX.X, ALU.add).then_inc(sums, 1)
            dve.wait_ge(sums_all, 1)
            step(dve.reciprocal(f.red[:, 0:2], f.red_all[:, 2:4]))
            step(dve.tensor_tensor(tw, tw, f.red[:, 0:2].unsqueeze(1).broadcast_to([P, NT, 2]), ALU.mult))
            for r in range(2):
                for t in range(NT):
                    dve.tensor_scalar(f.ohx[:, r, t, :], m.iota_x[:, :], f.idxf[:, t, r:r + 1], 2.0,
                                      ALU.is_equal, ALU.mult).then_inc(spread, 1)
                for t in range(NT):
                    dve.tensor_copy(f.wx[:, r, t, :], f.tw[:, t, r:r + 1].broadcast_to([P, P])).then_inc(spread, 1)


def lora_experts(nc, m, f, w, a, batch):
    with stage(nc, "low_in", "low_read", "low_made", "firsts", "seconds", "silued", "gated", "weighted", "mixed",
               "lowered", "masked", "u_made", "downed", "added", *MaximumPass.SEMAPHORES, pool=True) as \
            (block, low_in, low_read, low_made, firsts, seconds, silued, gated, weighted, mixed,
             lowered, masked, u_made, downed, added, *max_sems):
        units = NC * M3
        slots = []
        for n in range(units):
            up = [("first", n, i) for i in range(2 * (KD + 1))]
            rest = [("second", n, j) for j in range(2) if n >= 1] + [("lower", n)] * (n >= 2)
            slots += rest + up if n == M3 else up + rest
            if n == M3 + 2:
                slots += [("down", 0, j, i) for j in range(TC) for i in range(3)]
        slots += [("down", 1, j, i) for j in range(TC - 1) for i in range(3)]
        mp = MaximumPass(m, a, max_sems)
        downs = sum(key[0] == "down" for key in slots)
        rate = (len(mp.items) - downs) / (len(slots) - downs)
        mp.share_out([(key, 1 if key[0] == "down" else rate, (7,) if key[0] == "down" else (6, 7)) for key in slots])

        def item_count(key):
            return mp.share[key].stop

        @block.tensor
        def _(pe):
            def low(c):
                if c >= 1:
                    pe.wait_ge(mp.block_out, item_count(("lower", M3)))
                for j in range(2):
                    if j == 1:
                        pe.wait_ge(low_read, 2 * c + 1)
                    for k in range(KD):
                        last = pe.matmul(m.ps[:, 6, :], w.a[:, k, j * P:(j + 1) * P],
                                         m.xn_t[:, k, c * CH:(c + 1) * CH], start=(k == 0), stop=(k == KD - 1))
                    last.then_inc(low_in, 1)

            def first(n):
                c, i = divmod(n, M3)
                if n >= 2:
                    pe.wait_ge(gated, 2 * (n - 1))
                if i == 0:
                    pe.wait_ge(low_made, 2 * (c + 1))
                for j, wt in enumerate((w.up, w.gate)):
                    for k in range(KD):
                        pe.matmul(m.ps[:, 2 * (n % 2) + j, :], wt[:, k, i * P:(i + 1) * P],
                                  m.xn_t[:, k, c * CH:(c + 1) * CH], start=(k == 0), stop=False)
                        mp.tensor_share(pe, ("first", n, 3 * j + k))
                    pe.matmul(m.ps[:, 2 * (n % 2) + j, :], w.b[:, j, i * P:(i + 1) * P],
                              f.m0[:, j, :], start=False, stop=True).then_inc(firsts, 1)
                    mp.tensor_share(pe, ("first", n, 3 * j + KD))

            def second(n):
                pe.wait_ge(gated, 2 * n + 1)
                for j in range(2):
                    i = n % M3
                    pe.matmul(m.ps[:, 2 * (n % 2) + j, :], w.b[:, j, i * P:(i + 1) * P], f.md[:, j, :],
                              start=False, stop=True, skip_group_check=True).then_inc(seconds, 1)
                    mp.tensor_share(pe, ("second", n + 1, j))

            def lower(n):
                c, i = divmod(n, M3)
                pe.wait_ge(weighted, 2 * (n + 1))
                if i == 0 and c >= 1:
                    pe.wait_ge(masked, 2 * c)
                for r in range(2):
                    last = pe.matmul(m.ps[:, 4 + r, :], w.da[:, i, :], f.h[:, r, n % 2, :],
                                     start=(i == 0), stop=(i == M3 - 1))
                    if r == 0:
                        mp.tensor_share(pe, ("lower", n + 2))
                last.then_inc(lowered, 1)

            def down(c):
                pe.wait_ge(mixed, M3 * (c + 1))
                pe.wait_ge(u_made, c + 1)
                pe.wait_ge(mp.block_out, item_count(("lower", M3 + 2 if c == 0 else units - 1)))
                for j in range(TC):
                    t = c * TC + j
                    if j % 2 == 0 and j >= 2:
                        pe.wait_ge(added, t)
                    out = m.ps[:, 6, (j % 2) * D:(j % 2 + 1) * D]
                    for i in range(M3):
                        pe.matmul(out, f.mixed[:, (c * M3 + i) % MIXED, j * P:(j + 1) * P], w.down[:, i, :],
                                  start=(i == 0), stop=False)
                        if i % 2 == 1:
                            mp.tensor_share(pe, ("down", c, j, i // 2))
                    last = pe.matmul(out, f.u[:, j * P:(j + 1) * P], w.db[:, :], start=False, stop=True)
                    if j % 2 == 1:
                        last.then_inc(downed, 1)
                if c + 1 < NC:
                    pe.wait_ge(added, TC * (c + 1))

            low(0)
            for n in range(units):
                if n == M3:
                    second(n - 1)
                    lower(n - 2)
                    low(1)
                    first(n)
                else:
                    first(n)
                    if n >= 1:
                        second(n - 1)
                    if n >= 2:
                        lower(n - 2)
                if n == M3 + 2:
                    down(0)
            second(units - 1)
            lower(units - 2)
            lower(units - 1)
            down(1)

        @block.scalar
        def _(act):
            def silu(n, r):
                act.wait_ge((firsts, seconds)[r], 2 * n + 1)
                if n >= 1:
                    act.wait_ge(gated, 2 * (n - 1) + r + 1)
                act.activation(f.s[:, r, :], m.ps[:, 2 * (n % 2), :], ACT.Silu).then_inc(silued, 1)

            for n in range(units):
                silu(n, 0)
                silu(n, 1)

        @block.vector
        def _(dve):
            def low(c):
                cols = slice(c * CH, (c + 1) * CH)
                if c >= 1:
                    dve.wait_ge(seconds, 2 * M3 * c)
                for j in range(2):
                    dve.wait_ge(low_in, 2 * c + j + 1)
                    mp.step(dve, dve.tensor_tensor(f.m0[:, j, :], f.oh[:, 0, cols], m.ps[:, 6, :], ALU.mult))
                    dve.tensor_tensor(f.md[:, j, :], f.oh[:, 1, cols], m.ps[:, 6, :], ALU.mult).then_inc(low_read, 1)
                    dve.wait_ge(low_read, 2 * c + j + 1)
                    dve.tensor_tensor(f.md[:, j, :], f.md[:, j, :], f.m0[:, j, :], ALU.subtract).then_inc(low_made, 1)

            def gate(n, r):
                dve.wait_ge(silued, 2 * n + r + 1)
                dve.wait_ge((firsts, seconds)[r], 2 * n + 2)
                if n >= 2:
                    dve.wait_ge(lowered, n - 1)
                    dve.wait_ge(mixed, n - 1)
                dve.tensor_tensor(f.h[:, r, n % 2, :], f.s[:, r, :], m.ps[:, 2 * (n % 2) + 1, :],
                                  ALU.mult).then_inc(gated, 1)

            def lowrank(c):
                cols = slice(c * CH, (c + 1) * CH)
                dve.wait_ge(lowered, M3 * (c + 1))
                if c >= 1:
                    dve.wait_ge(downed, TC // 2 * c)
                dve.tensor_tensor(f.u[:, :], f.oh[:, 0, cols], m.ps[:, 4, :], ALU.mult).then_inc(masked, 1)
                dve.tensor_tensor(f.uu[:, :], f.oh[:, 1, cols], m.ps[:, 5, :], ALU.mult).then_inc(masked, 1)
                dve.wait_ge(masked, 2 * (c + 1))
                dve.tensor_tensor(f.u[:, :], f.u[:, :], f.uu[:, :], ALU.add).then_inc(u_made, 1)

            def add(c):
                for j in range(TC):
                    t = c * TC + j
                    for i in range(3):
                        mp.vector_share(dve, ("down", c, j, i))
                    if j % 2 == 1:
                        dve.wait_ge(downed, t // 2 + 1)
                        for u in (t - 1, t):
                            dve.tensor_tensor(sum_place(m, batch, u), sum_place(m, batch, u),
                                              m.ps[:, 6, (u % 2) * D:(u % 2 + 1) * D], ALU.add).then_inc(added, 1)

            def up_share(n):
                for i in range(2 * (KD + 1)):
                    mp.vector_share(dve, ("first", n, i))

            def second_share(n):
                for j in range(2):
                    mp.vector_share(dve, ("second", n, j))

            mp.vector_start(dve)
            low(0)
            for n in range(units):
                if n == M3:
                    second_share(n)
                    gate(n - 1, 1)
                    mp.vector_share(dve, ("lower", n))
                    low(1)
                    up_share(n)
                    gate(n, 0)
                else:
                    up_share(n)
                    second_share(n)
                    if n >= 1:
                        gate(n - 1, 1)
                    gate(n, 0)
                    mp.vector_share(dve, ("lower", n))
                if n == M3 + 1:
                    lowrank(0)
                if n == M3 + 2:
                    add(0)
            gate(units - 1, 1)
            lowrank(1)
            add(1)

        @block.gpsimd
        def _(pool):
            for n in range(units):
                c, i = divmod(n, M3)
                for r in range(2):
                    pool.wait_ge(gated, 2 * n + r + 1)
                    pool.tensor_tensor(f.h[:, r, n % 2, :], f.h[:, r, n % 2, :], f.wb[:, r, c * CH:(c + 1) * CH],
                                       ALU.mult).then_inc(weighted, 1)
                pool.wait_ge(weighted, 2 * (n + 1))
                if n >= MIXED:
                    pool.wait_ge(downed, TC // 2)
                pool.tensor_tensor(f.mixed[:, n % MIXED, :], f.h[:, 0, n % 2, :], f.h[:, 1, n % 2, :],
                                   ALU.add).then_inc(mixed, 1)

        @block.sync
        def _(sp):
            mp.sync_rows(sp)



def program(nc, io, out):
    with ExitStack() as ctx:
        def sb(name, shape, dt=F32):
            return ctx.enter_context(nc.sbuf_tensor(name, shape, dt))

        m = Memory()
        m.ps = ctx.enter_context(nc.psum_tensor("ps", [P, 8, CH], F32))
        m.x = sb("x_all", [P, B * NT, D])
        m.ident = sb("ident", [P, P])
        m.ident_h = sb("ident_h", [P, P], F16)
        m.ident_b = sb("ident_b", [P, P], BF16)
        m.mask_qk = sb("mask_qk", [P, P], BF16)
        m.mask_kq = sb("mask_kq", [P, P], BF16)
        m.ones_col = sb("ones_col", [P, 1])
        m.iota16 = sb("iota16", [P, E_RT])
        m.iota_x = sb("iota_x", [P, P])
        m.cos = sb("cos", [P, 2, NT, HD])
        m.sin = sb("sin", [P, 2, NT, HD])
        m.small = sb("small", [P, 12 * NT])
        m.lam = sb("lam", [P, 1])
        arena = sb("arena", [P, 43600])

        setup_constants(nc, m, io)

        def start():
            ar = Arena(arena)
            m.acc = ar.take(NT, D)
            m.xn_t = ar.take(KD, S)
            return ar

        ar = start()
        wqkv = ar.take(KD, 3 * D)
        bqkv = ar.take(3 * D)
        wup = ar.take(E_SH + E_RT, KD, F0)
        wdown = ar.take(E_SH + E_RT, D)
        wroute = ar.take(KD, E_RT)
        load_weights(nc, [
            (wqkv, rows(io.w_qkv0)), (bqkv, io.b_qkv0.partition_broadcast(P)),
            *[(wup[:, :, k, :], io.w_up0[:, k * P:(k + 1) * P, :].rearrange("e p n -> p e n")) for k in range(KD)],
            (wdown, io.w_down0.rearrange("e p n -> p e n")), (wroute, rows(io.w_router0))])
        base = ar.at
        a = attention_memory(m, ar, NM, HD, NM // 4, 8)
        f = Memory()
        ar = Arena(arena, a.free)
        f.prob = ar.take(NT, E_RT)
        f.gate_w = ar.take(NT, E_RT)
        f.top = ar.take(NT, 8)
        f.idx = ar.take(NT, 8, dtype=U32)
        f.idxf = ar.take(NT, 8)
        f.mid = ar.take(3, CH)
        with nc.Fori(0, B) as b:
            normalise(nc, m, m.acc, a.xn, m.xn_t, xload=b)
            attention_operands(nc, m, a, wqkv, bqkv, 0, False, NM, HD)
            route(nc, m, f, wroute)
            experts(nc, m, f, a, wup, wdown)
            attention(nc, m, a, 4, 32)
            attention_finish(nc, m, a, 4, 32, None, 1.0, b)

        ar = start()
        wqkv = ar.take(KD, 3 * D)
        wo = ar.take(KD, D)
        turn = (ar.take(2 * NM * HD), ar.take(2 * NM * HD))
        wg = ar.take(KD, F1)
        wu = ar.take(KD, F1)
        wd = ar.take(F1 // P, D)
        load_weights(nc, [(wqkv[:, :, j * D:(j + 1) * D], rows(w)) for j, w in
                          enumerate((io.wq1, io.wk1, io.wv1))] + [(wo, rows(io.wo1)),
                          (turn[0], io.cos1.partition_broadcast(P)), (turn[1], io.sin1.partition_broadcast(P))])
        base = ar.at
        a = attention_memory(m, ar, NM // 2, 2 * HD, NM // 2, 6)
        f = Memory()
        ar = Arena(arena, base)
        f.win = ar.take(3, F1 // P, NSEG)
        f.basis = ar.take(2, NSEG, D)
        f.w = ar.take(2, D)
        f.lqk = ar.take(4, 2 * HD)
        f.dot = ar.take(2, 2 * HD)
        spline_weights(nc, m, f, io, wg, wu, wd)
        lambda_scalar(nc, m, f, io)
        f = Memory()
        ar = Arena(arena, base)
        f.inter = ar.take(2, F1 // P, CH)
        f.gate = ar.take(2, CH)
        with nc.Fori(0, B) as b:
            normalise(nc, m, m.acc, a.xn, m.xn_t, xload=b)
            attention_operands(nc, m, a, wqkv, None, turn, True, NM // 2, 2 * HD)
            attention(nc, m, a, 2, 64)
            attention_finish(nc, m, a, 2, 64, wo, 1.0 - LAMBDA_INIT)
            gated_ffn(nc, m, f, wg, wu, wd, False, b)
    
        ar = start()
        w = Memory()
        w.wr, w.wk, w.wv, w.wo, w.wcr = (ar.take(KD, D) for _ in range(5))
        w.wck = ar.take(KD, F2)
        w.wcv = ar.take(F2 // P, D)
        w.mix = ar.take(4, KD)
        w.omix = ar.take(4, KD)
        w.td, w.tf, w.decay, w.bonus, w.n1w, w.n1b, w.n2w, w.n2b = (ar.take(KD) for _ in range(8))
        wgu = ar.take(KD, 2 * F1)
        wp = ar.take(F1 // P, D)

        load_weights(nc, [(w.wr, rows(io.wr2)), (w.wk, rows(io.wk2)), (w.wv, rows(io.wv2)), (w.wo, rows(io.wo2)),
                          (w.wcr, rows(io.wcr2)), (w.wck, rows(io.wck2)), (w.wcv, rows(io.wcv2)),
                          *[(w.mix[:, j, :], v) for j, v in
                            enumerate((io.mix_r, io.mix_k, io.mix_v, io.mix_c))],
                          (w.td, io.td), (w.tf, io.tf), (w.n1w, io.n1w),
                          (w.n1b, io.n1b), (w.n2w, io.n2w), (w.n2b, io.n2b)])
        base = ar.at
        ng = (2 * F1 * D + D * F1) // P // GROUP
        f = Memory()
        f.raw = ar.take(ng * GROUP)
        f.wb = ar.take(ng * GROUP, dtype=BF16)
        f.q1 = ar.take(ng * GROUP, dtype=BF16)
        f.q2 = ar.take(ng * GROUP, dtype=BF16)
        f.thr = ar.take(ng)
        f.sc = ar.take(ng, dtype=BF16)
        ternary_weights(nc, m, f, io, wgu, wp)
        time_mix_scalars(nc, m, w)
        f = Memory()
        ar = Arena(arena, base)
        f.xn = ar.take(NT, D)
        f.n = ar.take(NT, D)
        f.h_t = ar.take(KD, S + 1)
        f.mix = ar.take(3, KD, S)
        f.rs = ar.take(KD, S)
        f.kk = ar.take(KD, S)
        f.st = ar.take(KD, S)
        g = Memory()
        ar = Arena(arena, base)
        g.inter = ar.take(2, F1 // P, CH)
        g.gate = ar.take(2, CH)
        g.sq = ar.take(F1 // P, CH)
        ar = Arena(arena, base + 4 * NT * D + 2)
        f.kc = Arena(arena, base + 2 * NT * D + KD * (S + 1) + KD * S).take(NC, F2 // P, CH)
        f.sg = Arena(arena, base).take(2, D)
        f.tmp = Arena(arena, base + 2 * D).take(D)
        clear_first_column(nc, f)
        with nc.Fori(0, B) as b:
            normalise(nc, m, m.acc, f.xn, m.xn_t, xload=b)
            clear_first_column(nc, f)
            normalise(nc, m, f.xn, f.n, f.h_t[:, :, 1:S + 1], scale_w=w.n1w, scale_b=w.n1b)
            time_mix(nc, m, f, w)
            normalise(nc, m, f.xn, f.n, f.h_t[:, :, 1:S + 1], scale_w=w.n2w, scale_b=w.n2b)
            channel_mix(nc, m, f, w)
            gated_ffn(nc, m, g, wgu[:, :, 0:F1], wgu[:, :, F1:2 * F1], wp, True, b)
    
        ar = Arena(arena)
        m.xn_t = ar.take(KD, S)
        wqkv = ar.take(KD, 3 * D)
        bqkv = ar.take(3 * D)
        wo = ar.take(KD, D)
        bo = ar.take(D)
        w = Memory()
        w.up = ar.take(KD, M3 * P)
        w.gate = ar.take(KD, M3 * P)
        w.down = ar.take(M3, D)
        w.a = ar.take(KD, 2 * P)
        w.b = ar.take(2, M3 * P)
        w.da = ar.take(M3, P)
        w.db = ar.take(D)
        w.route = ar.take(KD, E3)
        load_weights(nc, [(wqkv, rows(io.w_qkv3)), (bqkv, io.b_qkv3.partition_broadcast(P)),
                          (wo, rows(io.w_out3)), (bo, io.b_out3.partition_broadcast(P)),
                          (w.up, rows(io.up3)), (w.gate, rows(io.gate3)), (w.down, rows(io.down3)),
                          (w.a[:, :, 0:P], rows(io.up_a)), (w.a[:, :, P:2 * P], rows(io.gate_a)),
                          (w.b[:, 0, :], io.up_b), (w.b[:, 1, :], io.gate_b), (w.da, rows(io.down_a)),
                          (w.db, io.down_b), (w.route, rows(io.route3))])
        base = ar.at
        a = attention_memory(m, ar, NM, HD, NM // 4, 8)
        x_in = Arena(arena, a.free + NT * D).take(NT, D)
        m.acc = None
        f = Memory()
        ar = Arena(arena, a.free)
        f.lg = ar.take(NT, E3)
        f.top = ar.take(NT, 8)
        f.idx = ar.take(NT, 8, dtype=U32)
        f.idxf = ar.take(NT, 8)
        f.tw = ar.take(NT, 2)
        f.red = ar.take(4)
        f.red_all = ar.take(4)
        f.oh = ar.take(2, S)
        f.wb = ar.take(2, S)
        at = ar.at
        f.ohx = ar.take(2, NT, P)
        f.wx = ar.take(2, NT, P)
        ar = Arena(arena, at)
        f.m0 = ar.take(2, CH)
        f.md = ar.take(2, CH)
        f.s = ar.take(2, CH)
        f.h = ar.take(2, 2, CH)
        f.mixed = ar.take(MIXED, CH)
        f.uu = ar.take(CH)
        f.u = ar.take(CH)
        with nc.Fori(0, B) as b:
            normalise(nc, m, x_in, a.xn, m.xn_t, xload=b, bias=bo)
            attention_operands(nc, m, a, wqkv, bqkv, 1, False, NM, HD)
            route_pairs(nc, m, f, w.route)
            lora_experts(nc, m, f, w, a, b)
            attention(nc, m, a, 4, 32)
            attention_finish(nc, m, a, 4, 32, wo, 1.0, b)
    
        with stage(nc, "x_out") as (block, x_out):
            @block.sync
            def _(sp):
                for b in range(B):
                    sp.dma_start(rows(out[b]), m.x[:, b * NT:(b + 1) * NT, :]).then_inc(x_out, 16)
                sp.wait_ge(x_out, 16 * B)



def rotation_tables(sign, n):
    inv = 1.0 / 10000.0 ** (np.arange(0, HD, 2, dtype=np.float32) / HD)
    ang = np.arange(n, dtype=np.float32)[:, None] * inv[None, :].astype(np.float32)
    cos, sin = np.cos(ang).astype(np.float32), np.sin(ang).astype(np.float32)
    return (np.ascontiguousarray(np.concatenate([cos, cos], 1)),
            np.ascontiguousarray(np.concatenate([-sign * sin, sign * sin], 1)))


def spline_grid(n_ctrl):
    t = np.linspace(0.0, n_ctrl - 1.0, F1 * D, dtype=np.float64)
    i = np.clip(np.floor(t).astype(np.int64), 0, n_ctrl - 2)
    f = (t - i).astype(np.float32).astype(np.float64)
    i = i.reshape(F1, D)
    f = f.reshape(F1, D)
    parts = [0.5 * (-f + 2 * f ** 2 - f ** 3), 0.5 * (2 - 5 * f ** 2 + 3 * f ** 3),
             0.5 * (f + 4 * f ** 2 - 3 * f ** 3), 0.5 * (-f ** 2 + f ** 3)]
    basis = np.zeros((NSEG, F1, D))
    o, h = np.indices((F1, D))
    for k in range(4):
        basis[i - i[:, :1] + k, o, h] = parts[k]
    window = np.clip(i[:, :1] - 1 + np.arange(NSEG)[None, :], 0, n_ctrl - 1)
    return window, basis.astype(np.float32)


def lay_out(v):
    v = {k: np.asarray(x) for k, x in v.items()}
    t = np.ascontiguousarray
    o = {"x": v["L0_attn_hidden_states"]}
    h = np.arange(NM)[:, None] * 3 * HD + np.arange(HD)[None, :]
    order = np.concatenate([(h + j * HD).ravel() for j in range(3)])
    o["w_qkv0"] = t(v["L0_attn_w_qkv"][order].T)
    o["b_qkv0"] = t(v["L0_attn_b_qkv"][order])
    o["w_up0"] = np.concatenate([v["L0_ffn_Wsh_up"], v["L0_ffn_Wrt_up"]])
    o["w_down0"] = np.concatenate([v["L0_ffn_Wsh_down"], v["L0_ffn_Wrt_down"]])
    o["w_router0"] = v["L0_ffn_W_router"]
    o["cos0"], o["sin0"] = rotation_tables(1.0, S)
    o["cos1"], o["sin1"] = (np.tile(np.repeat(x, 2, axis=0).ravel(), 2) for x in rotation_tables(-1.0, NM // 2))
    o["cos3"], o["sin3"] = rotation_tables(1.0, S)
    for n in "qkvo":
        o[f"w{n}1"] = t(v[f"L1_attn_w{n}"].T)
    for n in ("lq1", "lk1", "lq2", "lk2"):
        o[n] = v[f"L1_attn_{n}"]
    window, o["basis"] = spline_grid(v["L1_ffn_gate_cp"].shape[0])
    for n in ("gate", "up", "down"):
        o[f"win_{n}"] = t(v[f"L1_ffn_{n}_cp"][window])
    for n in ("r", "k", "v", "o", "cr", "ck", "cv"):
        o[f"w{n}2"] = v[f"L2_attn_W{n}"]
    for n, key in (("mix_r", "time_mix_r"), ("mix_k", "time_mix_k"), ("mix_v", "time_mix_v"), ("mix_c", "cm_mix"),
                   ("td", "time_decay"), ("tf", "time_faaaa"), ("n1w", "norm1_w"), ("n1b", "norm1_b"),
                   ("n2w", "norm2_w"), ("n2b", "norm2_b")):
        o[n] = v[f"L2_attn_{key}"].reshape(KD, P).T
    o["w_gate_up"] = v["L2_ffn_w_gate_up"]
    o["w_proj"] = v["L2_ffn_w_proj"]
    even_odd = np.concatenate([np.arange(0, HD, 2), np.arange(1, HD, 2)])
    qk = (np.arange(2 * NM)[:, None] * HD + even_odd[None, :]).ravel()
    order = np.concatenate([qk, np.arange(2 * D, 3 * D)])
    o["w_qkv3"] = t(v["L3_attn_w_qkv"][order].T)
    o["b_qkv3"] = t(v["L3_attn_b_qkv"][order])
    o["w_out3"] = t(v["L3_attn_w_out"].T)
    o["b_out3"] = v["L3_attn_b_out"]
    o["route3"] = t(v["L3_ffn_gate_w"].T)

    def padded(w, axis):
        widths = [(0, 0)] * w.ndim
        widths[axis] = (0, M3 * P - H3)
        return t(np.pad(w, widths))

    o["up3"] = padded(v["L3_ffn_w_up"].T, 1)
    o["gate3"] = padded(v["L3_ffn_w_gate"].T, 1)
    o["down3"] = padded(v["L3_ffn_w_down"].T, 0)
    for n in ("up", "gate"):
        o[f"{n}_a"] = t(v[f"L3_ffn_{n}_A"].reshape(P, D).T)
        o[f"{n}_b"] = padded(v[f"L3_ffn_{n}_B"].transpose(0, 2, 1).reshape(P, H3), 1)
    o["down_a"] = padded(v["L3_ffn_down_A"].reshape(P, H3).T, 0)
    o["down_b"] = t(v["L3_ffn_down_B"].transpose(0, 2, 1).reshape(P, D))
    return {k: t(x) for k, x in o.items()}


def kernel(**inputs):
    import concourse.bacc as bacc
    from concourse.bass_utils import run_bass_kernel_spmd

    nc = bacc.Bacc("TRN2", target_bir_lowering=False, num_devices=1)
    arrays = lay_out(inputs)
    io = Memory()
    io.__dict__.update({n: nc.dram_tensor(n, a.shape, mybir.dt.from_np(a.dtype), kind="ExternalInput").ap()
                        for n, a in arrays.items()})
    out = nc.dram_tensor("out", (B, S, D), F32, kind="ExternalOutput").ap()
    program(nc, io, out)
    result = run_bass_kernel_spmd(nc, [arrays], core_ids=[0])
    return result.results[0]["out"]
```

```python
import concourse.bass as bass
from concourse import mybir
from contextlib import ExitStack, contextmanager
import numpy as np

F32 = mybir.dt.float32
F16 = mybir.dt.float16
BF16 = mybir.dt.bfloat16
F32R = mybir.dt.float32r
U32 = mybir.dt.uint32
ALU = mybir.AluOpType
ACT = mybir.ActivationFunctionType
AX = mybir.AxisListType
RMAX = bass.bass_isa.ReduceOp.max
RADD = bass.bass_isa.ReduceOp.add

B, S, D = 4, 1024, 256
P = 128
NT = S // P
KD = D // P
CH = 512
NC = S // CH
TC = CH // P
HD = 16
NM = 16
LN_EPS = 1e-5
RMS_EPS = 1.1920929e-07
NEG = -1.0e30
E_SH, E_RT, F0 = 2, 16, 128
F1 = 1024
F2 = 768
H3, E3, R3 = 704, 8, 16
M3 = -(-H3 // P)
LAMBDA_INIT = 0.2
NSEG = 6
GROUP = 64
ARENA = 43600
MIXED = M3 + 3
M_ROW = 48


class Memory:
    pass


@contextmanager
def stage(nc, *names, pool=False):
    with ExitStack() as ctx:
        sems = [ctx.enter_context(nc.semaphore(n)) for n in names]
        with nc.Block(no_gpsimd_drain=not pool) as block:
            yield (block, *sems)
        for s in sems:
            nc.sync.sem_clear(s)
        nc.all_engine_barrier(sem_only=True)


class Steps:

    def __init__(self, engine, sem):
        self.engine, self.sem, self.count = engine, sem, 0

    def __call__(self, instruction):
        self.count += 1
        instruction.then_inc(self.sem, 1)
        self.engine.wait_ge(self.sem, self.count)


def view(ap, *dims):
    if len(dims) == 1:
        return ap
    names = " ".join(f"d{i}" for i in range(len(dims)))
    return ap.rearrange(f"p ({names}) -> p {names}", **{f"d{i}": n for i, n in enumerate(dims)})


def sum_so_far(m, batch, t):
    return sum_place(m, batch if m.acc is None else None, t)


def sum_place(m, batch, t):
    if batch is None:
        return m.acc[:, t, :]
    return m.x[:, bass.ds(batch * NT + t, 1), :].rearrange("p a c -> p (a c)")


class Arena:

    def __init__(self, tensor, start=0):
        self.tensor, self.at = tensor, start

    def take(self, *dims, dtype=F32):
        n = int(np.prod(dims))
        words = n if dtype in (F32, F32R, U32) else -(-n // 2)
        ap = self.tensor[:, self.at:self.at + words]
        self.at += words
        assert self.at <= self.tensor.shape[1], self.at
        return view(ap if dtype == ap.dtype else ap.bitcast(dtype), *dims)


def rows(dram, p=P):
    return dram.rearrange("(k p) n -> p k n", p=p)



def setup_constants(nc, m, io):
    with stage(nc, "cleared", "selected", "psum_cleared", "tables_in", pool=True) as (block, cleared, selected, psum_cleared, tables_in):
        @block.gpsimd
        def _(pool):
            pool.memset(m.ident[:, :], 0.0).then_inc(cleared, 1)
            pool.memset(m.mask_qk[:, :], 0.0).then_inc(cleared, 1)
            pool.memset(m.mask_kq[:, :], 0.0).then_inc(cleared, 1)
            pool.memset(m.ones_col[:, :], 1.0)
            pool.iota(m.iota16[:, :], [[1, 16]], base=0, channel_multiplier=0, allow_small_or_imprecise_dtypes=True)
            pool.iota(m.iota_x[:, :], [[1, E3], [0, R3]], base=0, channel_multiplier=0,
                      allow_small_or_imprecise_dtypes=True)
            pool.wait_ge(cleared, 3)
            pool.affine_select(out=m.ident[:, :], in_=m.ident[:, :], compare_op=ALU.not_equal, fill=1.0,
                               base=0, pattern=[[-1, P]], channel_multiplier=1).then_inc(selected, 1)
            pool.affine_select(out=m.mask_qk[:, :], in_=m.mask_qk[:, :], compare_op=ALU.is_ge, fill=NEG,
                               base=0, pattern=[[-1, P]], channel_multiplier=1).then_inc(selected, 1)
            pool.affine_select(out=m.mask_kq[:, :], in_=m.mask_kq[:, :], compare_op=ALU.is_ge, fill=NEG,
                               base=0, pattern=[[1, P]], channel_multiplier=-1).then_inc(selected, 1)

        @block.vector
        def _(dve):
            dve.memset(m.ps[:, :, :], 0.0).then_inc(psum_cleared, 1)
            dve.wait_ge(selected, 1)
            dve.tensor_copy(m.ident_h[:, :], m.ident[:, :])
            dve.tensor_copy(m.ident_b[:, :], m.ident[:, :])

        @block.sync
        def _(sp):
            for b in range(B):
                sp.dma_start(m.x[:, b * NT:(b + 1) * NT, :], rows(io.x[b])).then_inc(tables_in, 16)
            n = B
            for i, (cos, sin) in enumerate(((io.cos0, io.sin0), (io.cos3, io.sin3))):
                sp.dma_start(m.cos[:, i, :, :], rows(cos)).then_inc(tables_in, 16)
                sp.dma_start(m.sin[:, i, :, :], rows(sin)).then_inc(tables_in, 16)
                n += 2
            sp.wait_ge(tables_in, 16 * n)


def load_weights(nc, pairs):
    with stage(nc, "weights_in") as (block, weights_in):
        @block.sync
        def _(sp):
            for dst, src in pairs[0::2]:
                sp.dma_start(dst, src).then_inc(weights_in, 16)
            sp.wait_ge(weights_in, 16 * len(pairs))

        @block.scalar
        def _(act):
            for dst, src in pairs[1::2]:
                act.dma_start(dst, src).then_inc(weights_in, 16)



def normalise(nc, m, src, dst, dst_t, xload=None, bias=None, scale_w=None, scale_b=None, add_dst=None):
    with stage(nc, "src_in", "stats", "std_in", "std_done", "rstd_in", "normed", "turned", "stored") as \
            (block, src_in, stats, std_in, std_done, rstd_in, normed, turned, stored):
        var = m.small[:, 0:2 * NT].rearrange("p (t c) -> p t c", c=2)
        st = m.small[:, 2 * NT:8 * NT].rearrange("p (t c) -> p t c", c=6)
        std = m.small[:, 8 * NT:9 * NT]
        rstd = m.small[:, 9 * NT:10 * NT]
        veps = m.small[:, 10 * NT:11 * NT]

        @block.vector
        def _(dve):
            for t in range(NT):
                if xload is not None and t % 2 == 0:
                    dve.wait_ge(src_in, t // 2 + 1)
                dve.bn_stats(st[:, t, :], src[:, t, :]).then_inc(stats, 1)
            for t in range(NT):
                dve.wait_ge(stats, t + 1)
                dve.bn_aggr(var[:, t, :], st[:, t, :]).then_inc(std_in, 1)
            dve.wait_ge(std_in, NT)
            dve.tensor_scalar(veps, var[:, :, 1], LN_EPS, None, ALU.add).then_inc(std_in, 1)
            dve.wait_ge(std_done, 1)
            dve.reciprocal(rstd, std).then_inc(rstd_in, 1)
            dve.wait_ge(rstd_in, 1)
            for t in range(NT):
                dve.tensor_scalar(dst[:, t, :], src[:, t, :], var[:, t, 0:1], rstd[:, t:t + 1],
                                  ALU.subtract, ALU.mult).then_inc(normed, 1)
            if bias is not None:
                dve.wait_ge(normed, NT)
                dve.tensor_tensor(m.x[:, bass.ds(xload * NT, NT), :], src[:, :, :],
                                  bias[:, :].unsqueeze(1).broadcast_to([P, NT, D]), ALU.add)
            if add_dst is not None:
                dve.wait_ge(normed, NT)
                dve.tensor_tensor(add_dst[:, :, :], add_dst[:, :, :], dst[:, :, :], ALU.add)

        @block.tensor
        def _(pe):
            for t in range(NT):
                pe.wait_ge(normed, t + 1)
                for k in range(KD):
                    last = pe.transpose(m.ps[:, 4 * k + t // TC, (t % TC) * P:(t % TC + 1) * P],
                                        dst[:, t, k * P:(k + 1) * P], m.ident[:, :])
                last.then_inc(turned, 1)

        @block.scalar
        def _(act):
            if xload is not None:
                for t in range(0, NT, 2):
                    act.activation(src[:, t:t + 2, :], m.x[:, bass.ds(xload * NT + t, 2), :], ACT.Copy).then_inc(src_in, 1)
            act.wait_ge(std_in, NT + 1)
            act.activation(std, veps, ACT.Sqrt).then_inc(std_done, 1)
            for c in range(NC):
                act.wait_ge(turned, TC * (c + 1))
                for k in range(KD):
                    out = dst_t[:, k, c * CH:(c + 1) * CH]
                    if scale_w is None:
                        act.activation(out, m.ps[:, 4 * k + c, :], ACT.Identity)
                    else:
                        act.activation(out, m.ps[:, 4 * k + c, :], ACT.Identity,
                                       bias=scale_b[:, k:k + 1], scale=scale_w[:, k:k + 1])



def attention_operands(nc, m, a, wqkv, bias, table, rms, heads, vd):
    gh = 2 * NM
    behind = 1 if rms else 0
    lag = 2 + behind

    def sums(t):
        return m.small[:, (t % 2) * gh:(t % 2 + 1) * gh]

    def roots(t):
        return m.small[:, (2 + t % 2) * gh:(3 + t % 2) * gh]

    half = HD // 2
    if isinstance(table, int):
        cos = [m.cos[:, table, t, :].unsqueeze(1).broadcast_to([P, gh, HD]) for t in range(NT)]
        sin = [m.sin[:, table, t, :].unsqueeze(1).broadcast_to([P, gh, HD]) for t in range(NT)]
    else:
        cos, sin = ([v.rearrange("p (h c) -> p h c", c=HD)] * NT for v in table)
    names = ["proj", "taken", "steps", "pool_done", "rotated", "hi", "lo", "stacked", "turned", "stored", "cleared",
             "rms_in", "rms_std", "squared"]
    with stage(nc, *names, pool=True) as (block, proj, taken, steps, pool_done, rotated, hi, lo, stacked, turned, stored,
                               cleared, rms_in, rms_std, squared):
        def kcols(buf, parity, slot, n=1, step=1):
            c0 = P * parity + 64 * parity + HD * slot
            v = a.ks[:, buf, :].rearrange("p (n c) -> p n c", c=2 * P)
            if n == 1:
                return v[:, :, c0:c0 + HD]
            return v[:, :, c0:c0 + HD * step * n].rearrange("p n (s c) -> p n s c", c=HD * step)[:, :, :, 0:HD]

        @block.tensor
        def _(pe):
            def turn(t):
                pe.wait_ge(stacked, 3 * (t + 1))
                if t >= 1:
                    pe.wait_ge(stored, 2 * t)
                psq = m.ps[:, 4, :].bitcast(F16)
                psk = m.ps[:, 5:7, :].rearrange("p a b -> p (a b)").bitcast(F16)
                for n in range(NM // 2):
                    pe.transpose(psq[:, n * P:(n + 1) * P], a.qs[:, t % 2, n * P:(n + 1) * P], m.ident_h[:, :])
                for n in range(NM):
                    last = pe.transpose(psk[:, n * P:(n + 1) * P], a.ks[:, t % 2, n * P:(n + 1) * P], m.ident_h[:, :])
                last.then_inc(turned, 1)

            for t in range(NT):
                if t >= 2:
                    pe.wait_ge(taken, 2 * (t - 1))
                for j, (c0, w) in enumerate(((0, 512), (512, 256))):
                    for k in range(KD):
                        last = pe.matmul(m.ps[:, 2 * (t % 2) + j, 0:w], m.xn_t[:, k, t * P:(t + 1) * P],
                                         wqkv[:, k, c0:c0 + w], start=(k == 0), stop=(k == KD - 1))
                last.then_inc(proj, 1)
                if t >= lag:
                    turn(t - lag)
            for t in range(NT - lag, NT):
                turn(t)

        @block.vector
        def _(dve):
            step = Steps(dve, steps)

            def store(t):
                dve.wait_ge(turned, t + 1)
                dve.tensor_copy(a.q[:, :, t * P:(t + 1) * P],
                                m.ps[:, 4, :].bitcast(F16).rearrange("p (n c) -> p n c", c=P)).then_inc(stored, 1)

            def take(t):
                qk = a.qk[:, t % 3, :]
                v_out = a.v[:, t, :, 0:vd]
                dve.wait_ge(proj, t + 1)
                if t >= 3:
                    dve.wait_ge(lo, 3 * (t - 2))
                psv = m.ps[:, 2 * (t % 2) + 1, 0:D].rearrange("p (h c) -> p h c", h=heads)
                if bias is not None:
                    dve.tensor_tensor(qk, m.ps[:, 2 * (t % 2), :], bias[:, 0:512], ALU.add).then_inc(taken, 1)
                    dve.tensor_tensor(v_out, psv, bias[:, 512:768].rearrange("p (h c) -> p h c", h=heads),
                                      ALU.add).then_inc(taken, 1)
                else:
                    dve.tensor_copy(qk, m.ps[:, 2 * (t % 2), :]).then_inc(taken, 1)
                    dve.tensor_copy(v_out, psv).then_inc(taken, 1)

            def mean_squares(t):
                ss = sums(t)
                dve.wait_ge(squared, t + 1)
                step(dve.tensor_reduce(ss, a.t1[:, t % 2, :].rearrange("p (h c) -> p h c", c=HD), AX.X, ALU.add))
                dve.tensor_scalar(ss, ss, 1.0 / HD, RMS_EPS, ALU.mult, ALU.add).then_inc(rms_in, 1)

            def rotate(t):
                qk = a.qk[:, t % 3, :]
                qk3 = qk.rearrange("p (h c) -> p h c", c=HD)
                t1 = a.t1[:, t % 2, :]
                t13 = t1.rearrange("p (h c) -> p h c", c=HD)
                t23 = a.t2[:, t % 2, :].rearrange("p (h c) -> p h c", c=HD)
                dve.wait_ge(taken, 2 * t + 1)
                if rms:
                    dve.wait_ge(rms_std, t + 1)
                    step(dve.reciprocal(roots(t), roots(t)))
                    step(dve.tensor_tensor(qk3, qk3, roots(t).unsqueeze(2).broadcast_to([P, gh, HD]), ALU.mult))
                step(dve.tensor_tensor(t13, qk3, cos[t], ALU.mult))
                dve.tensor_tensor(t23[:, :, 0:half], qk3[:, :, half:HD],
                                  sin[t][:, :, 0:half], ALU.mult)
                step(dve.tensor_tensor(t23[:, :, half:HD], qk3[:, :, 0:half],
                                       sin[t][:, :, half:HD], ALU.mult))
                dve.tensor_tensor(qk, t1, a.t2[:, t % 2, :], ALU.add).then_inc(rotated, 1)

            for t in range(NT + lag):
                if t < NT:
                    take(t)
                if 0 <= t - behind < NT:
                    rotate(t - behind)
                if rms and t < NT:
                    mean_squares(t)
                if t >= lag:
                    store(t - lag)

        @block.scalar
        def _(act):
            def store(t):
                act.wait_ge(turned, t + 1)
                act.activation(a.k[:, :, t * P:(t + 1) * P],
                               m.ps[:, 5:7, :].rearrange("p a b -> p (a b)").bitcast(F16).rearrange(
                                   "p (n c) -> p n c", c=P), ACT.Copy).then_inc(stored, 1)

            def square(t):
                act.wait_ge(taken, 2 * t + 1)
                if t >= 2:
                    act.wait_ge(rotated, t - 1)
                act.activation(a.t1[:, t % 2, :], a.qk[:, t % 3, :], ACT.Square).then_inc(squared, 1)

            def root(t):
                act.wait_ge(rms_in, t + 1)
                act.activation(roots(t), sums(t), ACT.Sqrt).then_inc(rms_std, 1)

            def high(t):
                qk3 = a.qk[:, t % 3, :].rearrange("p (h c) -> p h c", c=HD)
                act.wait_ge(rotated, t + 1)
                if t == 0:
                    act.wait_ge(cleared, 4)
                qs4 = a.qs[:, t % 2, :].rearrange("p (h s c) -> p h s c", h=NM, c=HD)
                act.activation(qs4[:, :, 0:2, :], qk3[:, 0:NM, :].unsqueeze(2).broadcast_to([P, NM, 2, HD]),
                               ACT.Copy).then_inc(hi, 1)
                for parity in range(2):
                    act.activation(kcols(t % 2, parity, 0, 2, 2),
                                   qk3[:, NM + parity:2 * NM:2, :].unsqueeze(2).broadcast_to([P, NM // 2, 2, HD]),
                                   ACT.Copy).then_inc(hi, 1)

            for t in range(NT + lag):
                if rms and t < NT:
                    square(t)
                if t >= lag:
                    store(t - lag)
                if 0 <= t - behind < NT:
                    high(t - behind)
                if rms and t < NT:
                    root(t)

        @block.gpsimd
        def _(pool):
            pool.memset(a.qs[:, :, :].bitcast(F32), 0.0).then_inc(cleared, 1)
            pool.memset(a.ks[:, :, :].bitcast(F32), 0.0).then_inc(cleared, 1)
            pool.wait_ge(cleared, 2)
            for parity in range(2):
                c0 = 192 * parity + M_ROW
                pool.memset(a.ks[:, :, :].rearrange("p b (n c) -> p b n c", c=2 * P)[:, :, :, c0:c0 + 2],
                            1.0).then_inc(cleared, 1)
            pool.memset(a.v[:, :, :, vd:vd + 1], 1.0)
            for t in range(NT):
                qk3 = a.qk[:, t % 3, :].rearrange("p (h c) -> p h c", c=HD)
                qs4 = a.qs[:, t % 2, :].rearrange("p (h s c) -> p h s c", h=NM, c=HD)
                pool.wait_ge(hi, 3 * (t + 1))
                pool.tensor_tensor(qs4[:, :, 2, :], qk3[:, 0:NM, :], qs4[:, :, 0, :], ALU.subtract).then_inc(stacked, 1)
                for parity in range(2):
                    pool.tensor_tensor(kcols(t % 2, parity, 1), qk3[:, NM + parity:2 * NM:2, :],
                                       kcols(t % 2, parity, 0), ALU.subtract).then_inc(stacked, 1)
                pool.wait_ge(stacked, 3 * (t + 1))
                for _ in range(3):
                    pool.sem_inc(lo, 1)


class MaximumPass:

    SEMAPHORES = ("score_block_in", "score_block_out", "max_steps", "max_split", "max_rows_set_0", "max_rows_set_1")

    def __init__(self, m, a, sems):
        self.m, self.a, self.maps = m, a, 4
        self.block_in, self.block_out, self.steps, self.split_done, *self.rows_set = sems
        self.step_count = 0
        self.items, self.done = [], {}
        for g in range(NM // self.maps):
            i = 0
            for h in range(self.maps):
                for qt in range(NT):
                    for c in range(qt // TC + 1):
                        self.items.append(("block", g, h, qt, c))
                        i += 1
                        if i == 4 and g:
                            self.items.append(("turn", g - 1))
            self.done[len(self.items) - 1] = g
        self.items.append(("turn", NM // self.maps - 1))
        self.banks, self.share = [], {}

    def share_out(self, slots):
        total = 0.0
        for key, number, banks in slots:
            total += number
            start = len(self.banks)
            while len(self.banks) < min(round(total), len(self.items)):
                self.banks.append(banks[len(self.banks) % len(banks)])
            self.share[key] = range(start, len(self.banks))
        assert len(self.banks) == len(self.items)

    def bank(self, n):
        return self.m.ps[:, self.banks[n], :]

    def tensor_item(self, pe, n):
        m, a = self.m, self.a
        out = self.bank(n)
        if self.items[n][0] == "turn":
            g = self.items[n][1]
            pe.wait_ge(self.split_done, g + 1)
        before = [i for i in range(n) if self.banks[i] == self.banks[n]]
        if before:
            pe.wait_ge(self.block_out, before[-1] + 1)
        if self.items[n][0] == "turn":
            rows_out = out[0:2 * self.maps, :].bitcast(F16)
            for qt in range(NT):
                last = pe.transpose(rows_out[:, qt * P:(qt + 1) * P], a.mt[:, g % 2, qt, :], m.ident_h[:, :])
            last.then_inc(self.block_in, 1)
            return
        _, g, h, qt, c = self.items[n]
        w = min(CH, (qt + 1) * P - c * CH)
        diag = qt // TC == c
        hh = g * self.maps + h
        last = pe.matmul(out[:, 0:w], a.q[:, hh // 2, qt * P:(qt + 1) * P], a.k[:, hh, c * CH:c * CH + w],
                         start=True, stop=not diag)
        if diag:
            last = pe.matmul(out[:, w - P:w], m.ident_b[:, :], m.mask_qk[:, :], start=False, stop=True)
        last.then_inc(self.block_in, 1)

    def step(self, dve, instruction):
        self.step_count += 1
        instruction.then_inc(self.steps, 1)
        dve.wait_ge(self.steps, self.step_count)

    def tensor_share(self, pe, key):
        for n in self.share.get(key, ()):
            self.tensor_item(pe, n)

    def vector_share(self, dve, key):
        for n in self.share.get(key, ()):
            self.vector_item(dve, n)

    def vector_start(self, dve):
        self.step(dve, dve.memset(self.a.mp[:, :, :, :], NEG))

    def vector_item(self, dve, n):
        a, out = self.a, self.bank(n)
        dve.wait_ge(self.block_in, n + 1)
        if self.items[n][0] == "turn":
            g = self.items[n][1]
            if g >= 2:
                dve.wait_ge(self.rows_set[g % 2], 16 * self.maps * (g // 2))
            dve.tensor_copy(a.mrow[0:2 * self.maps, g % 2, :], out[0:2 * self.maps, :].bitcast(F16)
                            ).then_inc(self.block_out, 1)
            return
        _, g, h, qt, c = self.items[n]
        w = min(CH, (qt + 1) * P - c * CH)
        dve.reduce_max(a.mp[:, h, qt, c:c + 1], out[:, 0:w], AX.X).then_inc(self.block_out, 1)
        if n in self.done:
            dve.wait_ge(self.block_out, n + 1)
            mt = a.mt[:, g % 2, :, :].rearrange("p t (h s) -> p h t s", s=2)
            self.step(dve, dve.tensor_reduce(a.mf[:, :, :], a.mp[:, :, :, :], AX.X, ALU.max, negate=True))
            self.step(dve, dve.tensor_copy(mt[:, :, :, 0], a.mf[:, :, :]))
            dve.tensor_tensor(mt[:, :, :, 1], a.mf[:, :, :], mt[:, :, :, 0], ALU.subtract).then_inc(self.split_done, 1)

    def sync_rows(self, sp):
        for n, item in enumerate(self.items):
            if item[0] == "turn":
                g = item[1]
                sp.wait_ge(self.block_out, n + 1)
                for h in range(self.maps):
                    r0 = M_ROW + 64 * (h % 2)
                    sp.dma_start(self.a.q[r0:r0 + 2, (g * self.maps + h) // 2, :],
                                 self.a.mrow[2 * h:2 * h + 2, g % 2, :]).then_inc(self.rows_set[g % 2], 16)
        for rows_set in self.rows_set:
            sp.wait_ge(rows_set, 16 * NM // 2)


def attention(nc, m, a, maps, width):
    groups = NM // maps
    n_exp = NM * NT
    ring = a.p.shape[1]
    lag = 1 if maps == 4 else 2
    with stage(nc, "scored", "exped", "summed", "evac") as (block, scored, exped, summed, evac):
        @block.tensor
        def _(pe):
            def score(u):
                n, hh = divmod(u, maps)
                g, kt = divmod(n, NT)
                h = g * maps + hh
                if u >= 3:
                    pe.wait_ge(exped, u - 2)
                bank = 2 + 2 * (u % 3)
                for c in range(kt // TC, NC):
                    q0 = max(kt * P, c * CH)
                    diag = c == kt // TC
                    last = pe.matmul(m.ps[:, bank + c, q0 - c * CH:CH], a.k[:, h, kt * P:(kt + 1) * P],
                                     a.q[:, h // 2, q0:(c + 1) * CH], start=True, stop=not diag)
                    if diag:
                        last = pe.matmul(m.ps[:, bank + c, q0 - c * CH:q0 - c * CH + P], m.ident_b[:, :],
                                         m.mask_kq[:, :], start=False, stop=True)
                last.then_inc(scored, 1)

            def values(n):
                g, kt = divmod(n, NT)
                pe.wait_ge(exped, maps * (n + 1))
                for c in range(kt // TC, NC):
                    if kt == 0 and g >= 1:
                        pe.wait_ge(evac, NC * (g - 1) + c + 1)
                    q0 = max(kt * P, c * CH)
                    for hh in range(maps):
                        h = g * maps + hh
                        p = a.p[:, (maps * n + hh) % ring, q0:(c + 1) * CH]
                        vh = h * a.v.shape[2] // NM
                        w = a.v.shape[3]
                        last = pe.matmul(m.ps[width * hh:width * hh + w, c, q0 - c * CH:CH], a.v[:, kt, vh, :], p,
                                         start=(kt == 0), stop=(kt == TC * (c + 1) - 1))
                last.then_inc(summed, 1)

            for n in range(groups * NT):
                for hh in range(maps):
                    score(maps * n + hh)
                    if hh == maps // 2 and n >= lag:
                        values(n - lag)
            for n in range(groups * NT - lag, groups * NT):
                values(n)

        @block.scalar
        def _(act):
            def store(g, c):
                act.wait_ge(summed, NT * g + TC * (c + 1))
                act.activation(a.o[:, g, c * CH:(c + 1) * CH], m.ps[:, c, :], ACT.Copy).then_inc(evac, 1)

            for u in range(n_exp):
                n, hh = divmod(u, maps)
                g, kt = divmod(n, NT)
                act.wait_ge(scored, u + 1)
                if u >= ring:
                    act.wait_ge(summed, (u - ring) // maps + 1)
                bank = 2 + 2 * (u % 3)
                act.activation(a.p[:, u % ring, kt * P:S],
                               m.ps[:, bank:bank + 2, :].rearrange("p a b -> p (a b)")[:, kt * P:S],
                               ACT.Exp, scale=HD ** -0.5).then_inc(exped, 1)
                if hh == maps - 1:
                    if kt == TC - 1 + lag:
                        store(g, 0)
                    if kt == lag - 1 and g >= 1:
                        store(g - 1, 1)
            store(groups - 1, 1)


def attention_finish(nc, m, a, maps, width, wout, out_scale, batch=None):
    groups = NM // maps
    banks = groups * P // CH
    with stage(nc, "turned", "steps", "given", "y_turned", "y_stored", "projected", "added") as \
            (block, turned, steps, given, y_turned, y_stored, projected, added):
        @block.tensor
        def _(pe):
            def project(t):
                pe.wait_ge(given, t + 1)
                if t >= 1:
                    pe.wait_ge(y_stored, t)
                for k in range(KD):
                    last = pe.transpose(m.ps[:, 6, k * P:(k + 1) * P], a.y[:, t % 2, k * P:(k + 1) * P], m.ident[:, :])
                last.then_inc(y_turned, 1)
                pe.wait_ge(y_stored, t + 1)
                if t >= 1:
                    pe.wait_ge(added, t)
                for k in range(KD):
                    last = pe.matmul(m.ps[:, 7, 0:D], a.yt[:, t % 2, k * P:(k + 1) * P], wout[:, k, :],
                                     start=(k == 0), stop=(k == KD - 1))
                last.then_inc(projected, 1)

            for t in range(NT):
                if t >= 2:
                    pe.wait_ge(given, t - 1)
                bank = banks * (t % 2)
                for g in range(groups):
                    last = pe.transpose(m.ps[:, bank + g // TC, (g % TC) * P:(g % TC + 1) * P],
                                        a.o[:, g, t * P:(t + 1) * P], m.ident[:, :])
                last.then_inc(turned, 1)
                if wout is not None and t >= 1:
                    project(t - 1)
            if wout is not None:
                project(NT - 1)

        if wout is not None:
            @block.scalar
            def _(act):
                for t in range(NT):
                    act.wait_ge(y_turned, t + 1)
                    act.activation(a.yt[:, t % 2, :], m.ps[:, 6, 0:D], ACT.Copy).then_inc(y_stored, 1)

        @block.vector
        def _(dve):
            step = Steps(dve, steps)

            def add(t):
                dve.wait_ge(projected, t + 1)
                dve.scalar_tensor_tensor(sum_place(m, batch, t), m.ps[:, 7, 0:D], out_scale, sum_so_far(m, batch, t),
                                         ALU.mult, ALU.add).then_inc(added, 1)

            for t in range(NT):
                bank = banks * (t % 2)
                sums = m.ps[:, bank:bank + banks, :].rearrange("p a b -> p (a b)").rearrange("p (h c) -> p h c", c=width)
                y = a.y[:, t % 2, :]
                dve.wait_ge(turned, t + 1)
                if t >= 1:
                    dve.wait_ge(given, t)
                if maps == 4:
                    r = m.small[:, 0:NM]
                    y3 = y.rearrange("p (h c) -> p h c", c=HD)
                    step(dve.reciprocal(r, sums[:, :, HD]))
                    if wout is not None and t >= 2:
                        dve.wait_ge(y_turned, t - 1)
                    ins = dve.tensor_tensor(y3, sums[:, :, 0:HD], r.unsqueeze(2).broadcast_to([P, NM, HD]), ALU.mult)
                    if wout is not None:
                        ins.then_inc(given, 1)
                    else:
                        ins.then_inc(given, 1)
                        dve.wait_ge(given, t + 1)
                        dve.tensor_tensor(sum_place(m, batch, t), m.acc[:, t, :], y, ALU.add)
                else:
                    vd = 2 * HD
                    r = m.small[:, 0:NM]
                    pair = sums.rearrange("p (h s) c -> p h s c", s=2)
                    r2 = r.rearrange("p (h s) -> p h s", s=2)
                    y3 = y.rearrange("p (h c) -> p h c", c=vd)
                    z3 = a.z[:, :].rearrange("p (h c) -> p h c", c=vd)
                    step(dve.reciprocal(r, sums[:, :, vd]))
                    step(dve.tensor_scalar(r2[:, :, 1], r2[:, :, 1], m.lam[:, 0:1], None, ALU.mult))
                    if t >= 2:
                        dve.wait_ge(y_turned, t - 1)
                    dve.tensor_tensor(y3, pair[:, :, 0, 0:vd], r2[:, :, 0].unsqueeze(2).broadcast_to([P, NM // 2, vd]),
                                      ALU.mult)
                    step(dve.tensor_tensor(z3, pair[:, :, 1, 0:vd],
                                           r2[:, :, 1].unsqueeze(2).broadcast_to([P, NM // 2, vd]), ALU.mult))
                    dve.tensor_tensor(y, y, a.z[:, :], ALU.subtract).then_inc(given, 1)
                    dve.wait_ge(given, t + 1)
                if wout is not None and t >= 1:
                    add(t - 1)
            if wout is not None:
                add(NT - 1)


def attention_memory(m, ar, heads, vd, groups, ring):
    a = Memory()
    a.q = ar.take(NM // 2, S, dtype=F16)
    a.o = Arena(ar.tensor, ar.at).take(groups, S)
    ar.take(S)
    a.k = ar.take(NM, S, dtype=F16)
    a.v = ar.take(NT, heads, vd + 1)
    a.mp = ar.take(4, NT, 2)
    a.mf = ar.take(4, NT)
    a.mt = ar.take(2, NT, 8, dtype=F16)
    a.mrow = ar.take(2, S, dtype=F16)
    base = ar.at
    a.free = base
    a.p = ar.take(ring, S)
    pre = Arena(ar.tensor, base)
    a.qk = pre.take(3, 512)
    a.t1 = pre.take(2, 512)
    a.t2 = pre.take(2, 512)
    a.qs = pre.take(2, NM * 64, dtype=F16)
    a.ks = pre.take(2, NM * P, dtype=F16)
    post = Arena(ar.tensor, base)
    a.y = post.take(2, D)
    a.yt = post.take(2, D)
    a.z = post.take(D)
    a.xn = Arena(ar.tensor, base).take(NT, D)
    return a



GATED_WORDS = 5 * CH
FFN_PARTS = 2 * KD * S + 4 * F1 // P * CH


def gated_memory(data, parts):
    f = Memory()
    ar = Arena(data)
    f.inter = ar.take(3, CH)
    f.gate = ar.take(2, CH)
    ar = Arena(parts)
    f.x = ar.take(2, KD, S, dtype=F32R)
    f.h = ar.take(2, 2, F1 // P, CH, dtype=F32R)
    return f


def gated_ffn(nc, m, f, wg, wu, wd, rms, batch):
    ni = F1 // P
    units = NC * ni
    with stage(nc, "x_high", "x_low", "upped", "silued", "gated", "high", "low", "squared", "square_steps", "downed",
               "added", "steps", "sumsq", "ms_in", "rms_done", pool=rms) as \
            (block, x_high, x_low, upped, silued, gated, high, low, squared, square_steps, downed,
             added, steps, sumsq, ms_in, rms_done):
        ms, root, inv = (m.small[:, i * NT:(i + 1) * NT] for i in range(3))
        products = [(0, 0), (0, 1), (1, 0)][:1 + len(wg)]

        @block.tensor
        def _(pe):
            def up(n):
                c, i = divmod(n, ni)
                if n >= 3:
                    pe.wait_ge(gated, n - 2)
                if i == 0:
                    pe.wait_ge(x_low, KD * (c + 1))
                for j, w in enumerate((wg, wu)):
                    terms = [(k, q) for k in range(KD) for q in products]
                    for k, (wp, xp) in terms:
                        last = pe.matmul(m.ps[:, 2 * (n % 3) + j, :], w[wp][:, k, i * P:(i + 1) * P],
                                         f.x[:, xp, k, c * CH:(c + 1) * CH], start=(k, (wp, xp)) == terms[0],
                                         stop=(k, (wp, xp)) == terms[-1])
                    last.then_inc(upped, 1)

            def down(c):
                pe.wait_ge(low, ni * (c + 1))
                if rms:
                    pe.wait_ge(squared, (ni - 1) * (c + 1))
                    if c >= 1:
                        pe.wait_ge(added, TC * c)
                    for j in range(TC):
                        last = pe.matmul(m.ps[:, 7, j:j + 1], f.acc[:, c, j * P:(j + 1) * P], m.ones_col[:, 0:1],
                                         start=True, stop=True)
                    last.then_inc(sumsq, 1)
                for j in range(TC):
                    t = c * TC + j
                    if j % 2 == 0:
                        if c >= 1:
                            pe.wait_ge(added, t - TC + 2)
                        if rms and j == 2:
                            pe.wait_ge(ms_in, c + 1)
                    terms = [(i, q) for i in range(ni) for q in products]
                    for i, (wp, hp) in terms:
                        last = pe.matmul(m.ps[:, 6 + j // 2, (j % 2) * D:(j % 2 + 1) * D],
                                         f.h[:, hp, c % 2, i, j * P:(j + 1) * P], wd[wp][:, i, :],
                                         start=(i, (wp, hp)) == terms[0], stop=(i, (wp, hp)) == terms[-1])
                    if j % 2 == 1:
                        last.then_inc(downed, 1)

            for n in range(units):
                up(n)
                if n % ni == 2 and n >= ni:
                    down(n // ni - 1)
            down(NC - 1)

        @block.scalar
        def _(act):
            def split_x(c):
                for k in range(KD):
                    act.activation(f.x[:, 0, k, c * CH:(c + 1) * CH], m.xn_t[:, k, c * CH:(c + 1) * CH],
                                   ACT.Copy).then_inc(x_high, 1)

            def split(n):
                c, i = divmod(n, ni)
                act.wait_ge(gated, n + 1)
                act.activation(f.h[:, 0, c % 2, i, :], f.inter[:, n % 3, :], ACT.Copy).then_inc(high, 1)

            def roots(c):
                act.wait_ge(ms_in, c + 1)
                act.activation(root[:, c * TC:(c + 1) * TC], ms[:, c * TC:(c + 1) * TC], ACT.Sqrt).then_inc(rms_done, 1)

            split_x(0)
            for n in range(units):
                act.wait_ge(upped, 2 * n + 1)
                if n >= 2:
                    act.wait_ge(gated, n - 1)
                act.activation(f.gate[:, n % 2, :], m.ps[:, 2 * (n % 3), :], ACT.Silu).then_inc(silued, 1)
                if n >= 1:
                    split(n - 1)
                if n == 1:
                    split_x(1)
                if rms and n == ni + 2:
                    roots(0)
            split(units - 1)
            if rms:
                roots(NC - 1)

        @block.vector
        def _(dve):
            step = Steps(dve, steps)

            def split_x(c):
                for k in range(KD):
                    dve.wait_ge(x_high, KD * c + k + 1)
                    cols = slice(c * CH, (c + 1) * CH)
                    dve.tensor_tensor(f.x[:, 1, k, cols], m.xn_t[:, k, cols], f.x[:, 0, k, cols].bitcast(F32),
                                      ALU.subtract).then_inc(x_low, 1)

            def split(n):
                c, i = divmod(n, ni)
                dve.wait_ge(high, n + 1)
                dve.tensor_tensor(f.h[:, 1, c % 2, i, :], f.inter[:, n % 3, :], f.h[:, 0, c % 2, i, :].bitcast(F32),
                                  ALU.subtract).then_inc(low, 1)

            def mean_squares(c):
                cols = slice(c * TC, (c + 1) * TC)
                dve.wait_ge(sumsq, c + 1)
                dve.tensor_scalar(ms[:, cols], m.ps[:, 7, 0:TC], 1.0 / F1, RMS_EPS, ALU.mult, ALU.add).then_inc(ms_in, 1)
                dve.wait_ge(rms_done, c + 1)
                step(dve.reciprocal(inv[:, cols], root[:, cols]))

            def add(c):
                for j in range(TC):
                    t = c * TC + j
                    dve.wait_ge(downed, t // 2 + 1)
                    out = m.ps[:, 6 + j // 2, (j % 2) * D:(j % 2 + 1) * D]
                    if rms:
                        dve.scalar_tensor_tensor(sum_place(m, batch, t), out, inv[:, t:t + 1], m.acc[:, t, :],
                                                 ALU.mult, ALU.add).then_inc(added, 1)
                    else:
                        dve.tensor_tensor(sum_place(m, batch, t), out, m.acc[:, t, :], ALU.add).then_inc(added, 1)

            split_x(0)
            for n in range(units):
                dve.wait_ge(silued, n + 1)
                dve.wait_ge(upped, 2 * n + 2)
                if n >= 3:
                    dve.wait_ge(low, n - 2)
                    if rms:
                        dve.wait_ge(square_steps, n - 2)
                dve.tensor_tensor(f.inter[:, n % 3, :], f.gate[:, n % 2, :], m.ps[:, 2 * (n % 3) + 1, :],
                                  ALU.mult).then_inc(gated, 1)
                if n >= 1:
                    split(n - 1)
                if n == 1:
                    split_x(1)
                if rms and n == ni + 2:
                    mean_squares(0)
                if n == ni + 3:
                    add(0)
            split(units - 1)
            if rms:
                mean_squares(NC - 1)
            add(NC - 1)

        if rms:
            @block.gpsimd
            def _(pool):
                for n in range(units):
                    c, i = divmod(n, ni)
                    pool.wait_ge(gated, n + 1)
                    inter = f.inter[:, n % 3, :]
                    if i >= 2 or (i == 1 and c >= 1):
                        pool.wait_ge(squared, (ni - 1) * c + i - 1)
                    pool.tensor_tensor(f.acc[:, c, :] if i == 0 else f.sq[:, :], inter, inter,
                                       ALU.mult).then_inc(square_steps, 1)
                    if i >= 1:
                        pool.wait_ge(square_steps, n + 1)
                        pool.tensor_tensor(f.acc[:, c, :], f.acc[:, c, :], f.sq[:, :], ALU.add).then_inc(squared, 1)



def route(nc, m, f, w_router):
    with stage(nc, "logits", "steps", "shifted", "exped") as (block, logits, steps, shifted, exped):
        @block.tensor
        def _(pe):
            for t in range(NT):
                for k in range(KD):
                    last = pe.matmul(m.ps[:, 0, t * E_RT:(t + 1) * E_RT], m.xn_t[:, k, t * P:(t + 1) * P],
                                     w_router[:, k, :], start=(k == 0), stop=(k == KD - 1))
            last.then_inc(logits, 1)

        @block.scalar
        def _(act):
            act.wait_ge(shifted, 1)
            act.activation(f.prob[:, :, :], f.prob[:, :, :], ACT.Exp).then_inc(exped, 1)

        @block.vector
        def _(dve):
            step = Steps(dve, steps)
            lg = m.ps[:, 0, 0:NT * E_RT].rearrange("p (t e) -> p t e", e=E_RT)
            mx = m.small[:, 0:NT]
            dve.wait_ge(logits, 1)
            step(dve.reduce_max(mx, lg, AX.X))
            dve.tensor_tensor(f.prob[:, :, :], lg, mx.unsqueeze(2).broadcast_to([P, NT, E_RT]),
                              ALU.subtract).then_inc(shifted, 1)
            dve.wait_ge(exped, 1)
            step(dve.tensor_reduce(mx, f.prob[:, :, :], AX.X, ALU.add))
            step(dve.reciprocal(mx, mx))
            step(dve.tensor_tensor(f.prob[:, :, :], f.prob[:, :, :], mx.unsqueeze(2).broadcast_to([P, NT, E_RT]),
                                   ALU.mult))
            for t in range(NT):
                dve.max(f.top[:, t, :], f.prob[:, t, :]).then_inc(steps, 1)
            step.count += NT
            dve.wait_ge(steps, step.count)
            for t in range(NT):
                dve.max_index(f.idx[:, t, :], f.top[:, t, :], f.prob[:, t, :]).then_inc(steps, 1)
            step.count += NT
            dve.wait_ge(steps, step.count)
            step(dve.tensor_copy(f.idxf[:, :, :], f.idx[:, :, :]))
            for t in range(NT):
                for r, out in enumerate((f.gate_w, f.prob)):
                    dve.tensor_scalar(out[:, t, :], m.iota16[:, :], f.idxf[:, t, r:r + 1], f.top[:, t, r:r + 1],
                                      ALU.is_equal, ALU.mult).then_inc(steps, 1)
            step.count += 2 * NT
            dve.wait_ge(steps, step.count)
            dve.tensor_tensor(f.gate_w[:, :, :], f.gate_w[:, :, :], f.prob[:, :, :], ALU.add)


def experts(nc, m, f, a, wup, wdown):
    ne = E_SH + E_RT
    units = NC * ne
    with stage(nc, "upped", "gelued", "downed", "added", *MaximumPass.SEMAPHORES) as \
            (block, upped, gelued, downed, added, *max_sems):
        mp = MaximumPass(m, a, max_sems)
        slots = KD + TC
        mp.share_out([((n, i), len(mp.items) / (slots * units), (4, 5, 6, 7))
                      for n in range(units) for i in range(slots)])

        def product(n, j):
            return m.ps[:, 2 + j // 2, (j % 2) * D:(j % 2 + 1) * D]

        @block.tensor
        def _(pe):
            def down(n, j):
                c, e = divmod(n, ne)
                if j == 0:
                    pe.wait_ge(gelued, n + 1)
                u = n * TC + j
                if j % 2 == 0 and n >= 1:
                    pe.wait_ge(added, u - TC + 2)
                last = pe.matmul(product(n, j), f.mid[:, n % 3, j * P:(j + 1) * P], wdown[:, e, :],
                                 start=True, stop=True)
                if j % 2 == 1:
                    last.then_inc(downed, 1)

            for n in range(units + 1):
                if n < units:
                    c, e = divmod(n, ne)
                    if n >= 2:
                        pe.wait_ge(gelued, n - 1)
                    for k in range(KD):
                        last = pe.matmul(m.ps[:, n % 2, :], wup[:, e, k, :], m.xn_t[:, k, c * CH:(c + 1) * CH],
                                         start=(k == 0), stop=(k == KD - 1))
                        if k == KD - 1:
                            last.then_inc(upped, 1)
                        mp.tensor_share(pe, (n, k))
                for j in range(TC):
                    mp.tensor_share(pe, (n, KD + j))
                    if n >= 1:
                        down(n - 1, j)

        @block.scalar
        def _(act):
            for n in range(units):
                act.wait_ge(upped, n + 1)
                if n >= 3:
                    act.wait_ge(downed, TC // 2 * (n - 2))
                act.activation(f.mid[:, n % 3, :], m.ps[:, n % 2, :], ACT.Gelu).then_inc(gelued, 1)

        @block.vector
        def _(dve):
            def add(n, j):
                c, e = divmod(n, ne)
                u = n * TC + j
                t = c * TC + j
                dve.wait_ge(downed, u // 2 + 1)
                if e >= 1:
                    dve.wait_ge(added, u - TC + 1)
                out = product(n, j)
                if e < E_SH:
                    dve.tensor_tensor(m.acc[:, t, :], out, m.acc[:, t, :], ALU.add).then_inc(added, 1)
                else:
                    dve.scalar_tensor_tensor(m.acc[:, t, :], out, f.gate_w[:, t, e - E_SH:e - E_SH + 1],
                                             m.acc[:, t, :], ALU.mult, ALU.add).then_inc(added, 1)

            mp.vector_start(dve)
            for n in range(units + 1):
                for k in range(KD):
                    mp.vector_share(dve, (n, k))
                for j in range(TC):
                    mp.vector_share(dve, (n, KD + j))
                    if n >= 1:
                        add(n - 1, j)

        @block.sync
        def _(sp):
            mp.sync_rows(sp)



def spline_weights(nc, m, f, io, wg, wu, wd):
    nt = F1 // P
    with stage(nc, "windows_in", "basis_in_0", "basis_in_1", "formed", "steps", "turned", "stored", "split",
               pool=True) as \
            (block, windows_in, basis_in_0, basis_in_1, formed, steps, turned, stored, split):
        basis_in = (basis_in_0, basis_in_1)
        basis_gu = io.basis.rearrange("s (t p) n -> t p s n", p=P)
        basis_d = io.basis.rearrange("s (h p c) n -> h c p s n", p=P, c=4)
        tiles = [("gu", t) for t in range(nt)] + [("d", t) for t in range(nt)]
        units = []
        for n, (kind, t) in enumerate(tiles):
            if kind == "gu":
                for w, win in ((wg, f.win[:, 0, t, :]), (wu, f.win[:, 1, t, :])):
                    units.append((n, win, [part[:, :, t * P:(t + 1) * P] for part in w]))
            else:
                h, c = divmod(t, 4)
                units.append((n, f.win[:, 2, t, :], [part[:, 2 * c:2 * c + 2, h * P:(h + 1) * P] for part in wd]))

        @block.sync
        def _(sp):
            for i, win in enumerate((io.win_gate, io.win_up)):
                sp.dma_start(f.win[:, i, :, :], rows(win)).then_inc(windows_in, 16)
            for h in range(KD):
                sp.dma_start(f.win[:, 2, 4 * h:4 * h + 4, :],
                             io.win_down.rearrange("(h p c) s -> h p c s", p=P, c=4)[h]).then_inc(windows_in, 16)
            for n, (kind, t) in enumerate(tiles):
                if n >= 2:
                    last_use = max(i for i, u in enumerate(units) if u[0] == n - 2)
                    sp.wait_ge(formed, last_use + 1)
                src = basis_gu[t] if kind == "gu" else basis_d[t // 4][t % 4]
                sp.dma_start(f.basis[:, n % 2, :, :], src).then_inc(basis_in[n % 2], 16)

        @block.vector
        def _(dve):
            step = Steps(dve, steps)
            dve.wait_ge(windows_in, 64)
            for i, (n, win, out) in enumerate(units):
                dve.wait_ge(basis_in[n % 2], 16 * (n // 2 + 1))
                if i >= 2:
                    dve.wait_ge(turned, i - 1)
                w = f.w[:, i % 2, :]
                step(dve.tensor_scalar(w, f.basis[:, n % 2, 0, :], win[:, 0:1], None, ALU.mult))
                for s in range(1, NSEG):
                    ins = dve.scalar_tensor_tensor(w, f.basis[:, n % 2, s, :], win[:, s:s + 1], w, ALU.mult, ALU.add)
                    if s < NSEG - 1:
                        step(ins)
                ins.then_inc(formed, 1)

        @block.tensor
        def _(pe):
            for i in range(len(units)):
                pe.wait_ge(formed, i + 1)
                if i >= 2:
                    pe.wait_ge(stored, 2 * (i - 1))
                for k in range(KD):
                    last = pe.transpose(m.ps[:, i % 2, k * P:(k + 1) * P], f.w[:, i % 2, k * P:(k + 1) * P],
                                        m.ident[:, :])
                last.then_inc(turned, 1)

        @block.scalar
        def _(act):
            for i, (n, win, out) in enumerate(units):
                act.wait_ge(turned, i + 1)
                turned_w = m.ps[:, i % 2, 0:D].rearrange("p (k n) -> p k n", k=KD)
                if i >= 2:
                    act.wait_ge(split, i - 1)
                act.activation(out[0], turned_w, ACT.Copy).then_inc(stored, 1)
                act.activation(f.whole[:, i % 2, :, :], turned_w, ACT.Copy).then_inc(stored, 1)

        @block.gpsimd
        def _(pool):
            for i, (n, win, out) in enumerate(units):
                pool.wait_ge(stored, 2 * (i + 1))
                pool.tensor_tensor(out[1], f.whole[:, i % 2, :, :], out[0].bitcast(F32), ALU.subtract).then_inc(split, 1)


def lambda_scalar(nc, m, f, io):
    n = 2 * HD
    with stage(nc, "lam_in", "steps", "dots", "exped") as (block, lam_in, steps, dots, exped):
        @block.sync
        def _(sp):
            for i, src in enumerate((io.lq1, io.lk1, io.lq2, io.lk2)):
                sp.dma_start(f.lqk[:, i, :], src.partition_broadcast(P)).then_inc(lam_in, 16)

        @block.vector
        def _(dve):
            step = Steps(dve, steps)
            dve.wait_ge(lam_in, 64)
            pair = f.lqk[:, :, :].rearrange("p (a b) n -> p a b n", b=2)
            step(dve.tensor_tensor(f.dot[:, :, :], pair[:, :, 0, :], pair[:, :, 1, :], ALU.mult))
            dve.tensor_reduce(m.small[:, 0:2], f.dot[:, :, :], AX.X, ALU.add).then_inc(dots, 1)
            dve.wait_ge(exped, 1)
            step(dve.tensor_tensor(m.lam[:, :], m.small[:, 2:3], m.small[:, 3:4], ALU.subtract))
            dve.tensor_scalar(m.lam[:, :], m.lam[:, :], LAMBDA_INIT, None, ALU.add)

        @block.scalar
        def _(act):
            act.wait_ge(dots, 1)
            act.activation(m.small[:, 2:4], m.small[:, 0:2], ACT.Exp).then_inc(exped, 1)



def ternary_weights(nc, m, f, io, wgu, wp):
    ngu, npj = 2 * F1 // P, D // P
    n_gu, n_p = ngu * D // GROUP, npj * F1 // GROUP
    ng = n_gu + n_p
    with stage(nc, "raw_in", "steps", "ready", "turned", "stored") as (block, raw_in, steps, ready, turned, stored):
        @block.sync
        def _(sp):
            sp.dma_start(f.raw[:, 0:n_gu * GROUP].rearrange("p (t n) -> p t n", n=D), rows(io.w_gate_up)).then_inc(raw_in, 16)
            sp.dma_start(f.raw[:, n_gu * GROUP:ng * GROUP].rearrange("p (t n) -> p t n", n=F1),
                         rows(io.w_proj)).then_inc(raw_in, 16)

        @block.vector
        def _(dve):
            step = Steps(dve, steps)
            g3 = lambda ap: ap.rearrange("p (g n) -> p g n", n=GROUP)
            bc = lambda s: s.unsqueeze(2).broadcast_to([P, ng, GROUP])
            dve.wait_ge(raw_in, 32)
            step(dve.tensor_copy(f.wb[:, :], f.raw[:, :]))
            step(dve.tensor_reduce(f.thr[:, :], g3(f.wb[:, :]), AX.X, ALU.add, apply_absolute_value=True))
            step(dve.tensor_scalar(f.sc[:, :], f.thr[:, :], 1.0 / GROUP, None, ALU.mult))
            step(dve.tensor_scalar(f.sc[:, :], f.sc[:, :], 1e-8, None, ALU.max))
            step(dve.tensor_scalar(f.thr[:, :], f.sc[:, :], 257.0 / 512.0, None, ALU.mult))
            step(dve.tensor_tensor(g3(f.q1[:, :]), g3(f.wb[:, :]), bc(f.thr[:, :]), ALU.is_gt))
            step(dve.tensor_scalar(f.thr[:, :], f.thr[:, :], -1.0, None, ALU.mult))
            step(dve.tensor_tensor(g3(f.q2[:, :]), g3(f.wb[:, :]), bc(f.thr[:, :]), ALU.is_lt))
            step(dve.tensor_tensor(f.q1[:, :], f.q1[:, :], f.q2[:, :], ALU.subtract))
            step(dve.tensor_tensor(g3(f.q1[:, :]), g3(f.q1[:, :]), bc(f.sc[:, :]), ALU.mult))
            step(dve.tensor_tensor(f.q1[:, :], f.q1[:, :], f.wb[:, :], ALU.subtract))
            dve.tensor_tensor(f.q1[:, :], f.q1[:, :], f.wb[:, :], ALU.add).then_inc(ready, 1)

        turns = [(f.q1[:, (2 * t + k) * P:(2 * t + k + 1) * P], wgu[:, k, t * P:(t + 1) * P])
                 for k in range(KD) for t in range(ngu)]
        turns += [(f.q1[:, n_gu * GROUP + h * F1 + j * P:n_gu * GROUP + h * F1 + (j + 1) * P],
                   wp[:, j, h * P:(h + 1) * P]) for h in range(npj) for j in range(F1 // P)]

        @block.tensor
        def _(pe):
            pe.wait_ge(ready, 1)
            for u in range(len(turns) // 4):
                if u >= 4:
                    pe.wait_ge(stored, 4 * (u - 3))
                for i in range(4):
                    last = pe.transpose(m.ps[:, u % 4, :].bitcast(BF16)[:, i * P:(i + 1) * P], turns[4 * u + i][0],
                                        m.ident_b[:, :])
                last.then_inc(turned, 1)

        @block.scalar
        def _(act):
            for u in range(len(turns) // 4):
                act.wait_ge(turned, u + 1)
                for i in range(4):
                    act.activation(turns[4 * u + i][1], m.ps[:, u % 4, :].bitcast(BF16)[:, i * P:(i + 1) * P],
                                   ACT.Copy).then_inc(stored, 1)


def time_mix_scalars(nc, m, w):
    with stage(nc, "steps") as (block, steps):
        @block.vector
        def _(dve):
            dve.tensor_scalar(w.omix[:, :, :], w.mix[:, :, :], -1.0, 1.0, ALU.mult, ALU.add)

        @block.scalar
        def _(act):
            act.activation(w.decay[:, :], w.td[:, :], ACT.Exp).then_inc(steps, 1)
            act.wait_ge(steps, 1)
            act.activation(w.decay[:, :], w.decay[:, :], ACT.Exp, scale=-1.0)
            act.activation(w.bonus[:, :], w.tf[:, :], ACT.Exp)


def mixed_with_last(dve, step, out, h_t, mix, omix, j):
    for k in range(KD):
        step(dve.tensor_scalar(out[:, k, :], h_t[:, k, 0:S], omix[:, j, k:k + 1], None, ALU.mult))
        ins = dve.scalar_tensor_tensor(out[:, k, :], h_t[:, k, 1:S + 1], mix[:, j, k:k + 1], out[:, k, :],
                                       ALU.mult, ALU.add)
        if k == 0:
            step(ins)
    return ins


def time_mix(nc, m, f, w):
    order = (("k", w.wk, 1), ("v", w.wv, 2), ("r", w.wr, 0))
    with stage(nc, "mixed", "steps", "proj", "k_kept", "kv_made", "r_kept", "wkv", "outed", "added", "summed") as \
            (block, mixed, steps, proj, k_kept, kv_made, r_kept, wkv, outed, added, summed):
        @block.tensor
        def _(pe):
            for n, (name, wt, j) in enumerate(order):
                pe.wait_ge(mixed, n + 1)
                for o in range(KD):
                    for c in range(NC):
                        u = 4 * n + 2 * o + c
                        if u >= 8:
                            pe.wait_ge(k_kept, u - 8 + 1)
                        for k in range(KD):
                            last = pe.matmul(m.ps[:, u % 8, :], wt[:, k, o * P:(o + 1) * P],
                                             f.mix[:, j, k, c * CH:(c + 1) * CH], start=(k == 0), stop=(k == KD - 1))
                        last.then_inc(proj, 1)
            for t in range(NT):
                pe.wait_ge(wkv, KD)
                if t < 4:
                    pe.wait_ge(kv_made, 4)
                else:
                    pe.wait_ge(summed, t - 3)
                for k in range(KD):
                    last = pe.matmul(m.ps[:, 4 + t % 4, 0:D], f.st[:, k, t * P:(t + 1) * P], w.wo[:, k, :],
                                     start=(k == 0), stop=(k == KD - 1))
                last.then_inc(outed, 1)

        @block.scalar
        def _(act):
            for u in range(4):
                act.wait_ge(proj, u + 1)
                act.activation(f.kk[:, u // 2, (u % 2) * CH:(u % 2 + 1) * CH], m.ps[:, u, :], ACT.Copy).then_inc(k_kept, 1)
            for u in range(4):
                act.wait_ge(proj, 8 + u + 1)
                act.activation(f.rs[:, u // 2, (u % 2) * CH:(u % 2 + 1) * CH], m.ps[:, u, :],
                               ACT.Sigmoid).then_inc(r_kept, 1)

        @block.vector
        def _(dve):
            step = Steps(dve, steps)
            for name, wt, j in order:
                mixed_with_last(dve, step, f.mix[:, j, :, :], f.h_t, w.mix, w.omix, j).then_inc(mixed, 1)
            for u in range(4):
                dve.wait_ge(proj, 4 + u + 1)
                dve.wait_ge(k_kept, u + 1)
                part = f.kk[:, u // 2, (u % 2) * CH:(u % 2 + 1) * CH]
                dve.tensor_tensor(part, part, m.ps[:, 4 + u, :], ALU.mult).then_inc(kv_made, 1)
            dve.wait_ge(kv_made, 4)
            for k in range(KD):
                step(dve.tensor_tensor_scan(f.st[:, k, :], w.decay[:, k:k + 1].broadcast_to([P, S]), f.kk[:, k, :],
                                            0.0, ALU.mult, ALU.add))
                step(dve.scalar_tensor_tensor(f.st[:, k, 0:1], f.kk[:, k, 0:1], w.bonus[:, k:k + 1], f.st[:, k, 0:1],
                                              ALU.mult, ALU.add))
                dve.wait_ge(r_kept, 2 * (k + 1))
                dve.tensor_tensor(f.st[:, k, :], f.st[:, k, :], f.rs[:, k, :], ALU.mult).then_inc(wkv, 1)
            for t in range(NT):
                dve.wait_ge(outed, t + 1)
                dve.tensor_tensor(f.xn[:, t, :], f.xn[:, t, :], m.ps[:, 4 + t % 4, 0:D], ALU.add).then_inc(summed, 1)
                dve.wait_ge(summed, t + 1)
                dve.tensor_tensor(m.acc[:, t, :], m.acc[:, t, :], f.xn[:, t, :], ALU.add)


def channel_mix(nc, m, f, w):
    nf = F2 // P
    with stage(nc, "mixed", "steps", "upped", "squared", "gate_in", "gated", "downed", "scaled", "added") as \
            (block, mixed, steps, upped, squared, gate_in, gated, downed, scaled, added):
        @block.tensor
        def _(pe):
            def down(c):
                for j in range(TC):
                    t = c * TC + j
                    if t >= 2:
                        pe.wait_ge(gated, t - 1)
                    for k in range(KD):
                        last = pe.matmul(m.ps[:, 4 + t % 2, 0:D], f.mix[:, 0, k, t * P:(t + 1) * P], w.wcr[:, k, :],
                                         start=(k == 0), stop=(k == KD - 1))
                    last.then_inc(gate_in, 1)
                    pe.wait_ge(squared, nf * (c + 1))
                    if t >= 2:
                        pe.wait_ge(scaled, t - 1)
                    for i in range(nf):
                        last = pe.matmul(m.ps[:, 6 + t % 2, 0:D], f.kc[:, c, i, j * P:(j + 1) * P], w.wcv[:, i, :],
                                         start=(i == 0), stop=(i == nf - 1))
                    last.then_inc(downed, 1)

            pe.wait_ge(mixed, 1)
            for c in range(NC):
                for i in range(nf):
                    n = c * nf + i
                    if n >= 4:
                        pe.wait_ge(squared, n - 3)
                    for k in range(KD):
                        last = pe.matmul(m.ps[:, n % 4, :], w.wck[:, k, i * P:(i + 1) * P],
                                         f.mix[:, 0, k, c * CH:(c + 1) * CH], start=(k == 0), stop=(k == KD - 1))
                    last.then_inc(upped, 1)
            for c in range(NC):
                down(c)

        @block.scalar
        def _(act):
            for n in range(NC * nf):
                act.wait_ge(upped, n + 1)
                act.activation(f.kc[:, n // nf, n % nf, :], m.ps[:, n % 4, :], ACT.Square).then_inc(squared, 1)
            for t in range(NT):
                act.wait_ge(gate_in, t + 1)
                if t >= 2:
                    act.wait_ge(scaled, t - 1)
                act.activation(f.sg[:, t % 2, :], m.ps[:, 4 + t % 2, 0:D], ACT.Sigmoid).then_inc(gated, 1)

        @block.vector
        def _(dve):
            step = Steps(dve, steps)
            mixed_with_last(dve, step, f.mix[:, 0, :, :], f.h_t, w.mix, w.omix, 3).then_inc(mixed, 1)
            for t in range(NT):
                dve.wait_ge(gated, t + 1)
                dve.wait_ge(downed, t + 1)
                if t >= 1:
                    dve.wait_ge(added, t)
                dve.tensor_tensor(f.tmp[:, :], f.sg[:, t % 2, :], m.ps[:, 6 + t % 2, 0:D], ALU.mult).then_inc(scaled, 1)
                dve.wait_ge(scaled, t + 1)
                dve.tensor_tensor(m.acc[:, t, :], m.acc[:, t, :], f.tmp[:, :], ALU.add).then_inc(added, 1)


def clear_first_column(nc, f):
    with stage(nc, "unused", pool=True) as (block, unused):
        @block.gpsimd
        def _(pool):
            pool.memset(f.h_t[:, :, 0:1], 0.0)



def route_pairs(nc, m, f, w_gate):
    with stage(nc, "logits", "kept", "steps", "maxes", "maxes_all", "shifted", "exped", "sums", "sums_all",
               "spread", "turned", pool=True) as \
            (block, logits, kept, steps, maxes, maxes_all, shifted, exped, sums, sums_all, spread, turned):
        tw = f.tw[:, :, :]
        by_slot = tw.rearrange("p t r -> p r t")

        @block.tensor
        def _(pe):
            for t in range(NT):
                for k in range(KD):
                    last = pe.matmul(m.ps[:, 7, t * E3:(t + 1) * E3], m.xn_t[:, k, t * P:(t + 1) * P],
                                     w_gate[:, k, :], start=(k == 0), stop=(k == KD - 1))
            last.then_inc(logits, 1)
            n = 0
            for r in range(2):
                for kind, src in enumerate((f.ohx, f.wx)):
                    for t in range(NT):
                        n += 1
                        pe.wait_ge(spread, n)
                        last = pe.transpose(m.ps[:, 4 * r + 2 * kind + t // TC, (t % TC) * P:(t % TC + 1) * P],
                                            src[:, r, t, :], m.ident[:, :])
                        if t % TC == TC - 1:
                            last.then_inc(turned, 1)

        @block.scalar
        def _(act):
            act.wait_ge(shifted, 1)
            act.activation(tw, tw, ACT.Exp).then_inc(exped, 1)
            for n in range(8):
                r, kind, c = n // 4, n // 2 % 2, n % 2
                act.wait_ge(turned, n + 1)
                dst = (f.oh, f.wb)[kind]
                act.activation(dst[:, r, c * CH:(c + 1) * CH], m.ps[:, n, :], ACT.Copy)

        @block.gpsimd
        def _(pool):
            pool.wait_ge(maxes, 1)
            pool.partition_all_reduce(f.red_all[:, 0:2], f.red[:, 0:2], P, RMAX).then_inc(maxes_all, 1)
            pool.wait_ge(sums, 1)
            pool.partition_all_reduce(f.red_all[:, 2:4], f.red[:, 2:4], P, RADD).then_inc(sums_all, 1)

        @block.vector
        def _(dve):
            step = Steps(dve, steps)
            dve.wait_ge(logits, 1)
            step(dve.tensor_copy(f.lg[:, :, :], m.ps[:, 7, 0:NT * E3].rearrange("p (t e) -> p t e", e=E3)))
            for t in range(NT):
                dve.max(f.top[:, t, :], f.lg[:, t, :]).then_inc(steps, 1)
            step.count += NT
            dve.wait_ge(steps, step.count)
            for t in range(NT):
                dve.max_index(f.idx[:, t, :], f.top[:, t, :], f.lg[:, t, :]).then_inc(steps, 1)
            dve.tensor_reduce(f.red[:, 0:2], f.top[:, :, 0:2].rearrange("p t r -> p r t"), AX.X,
                              ALU.max).then_inc(maxes, 1)
            step.count += NT
            dve.wait_ge(steps, step.count)
            step(dve.tensor_copy(f.idxf[:, :, :], f.idx[:, :, :]))
            dve.wait_ge(maxes_all, 1)
            dve.tensor_tensor(tw, f.top[:, :, 0:2], f.red_all[:, 0:2].unsqueeze(1).broadcast_to([P, NT, 2]),
                              ALU.subtract).then_inc(shifted, 1)
            dve.wait_ge(exped, 1)
            dve.tensor_reduce(f.red[:, 2:4], by_slot, AX.X, ALU.add).then_inc(sums, 1)
            dve.wait_ge(sums_all, 1)
            step(dve.reciprocal(f.red[:, 0:2], f.red_all[:, 2:4]))
            step(dve.tensor_tensor(tw, tw, f.red[:, 0:2].unsqueeze(1).broadcast_to([P, NT, 2]), ALU.mult))
            for r in range(2):
                for t in range(NT):
                    dve.tensor_scalar(f.ohx[:, r, t, :], m.iota_x[:, :], f.idxf[:, t, r:r + 1], 2.0,
                                      ALU.is_equal, ALU.mult).then_inc(spread, 1)
                for t in range(NT):
                    dve.tensor_copy(f.wx[:, r, t, :], f.tw[:, t, r:r + 1].broadcast_to([P, P])).then_inc(spread, 1)


def lora_experts(nc, m, f, w, a, batch):
    with stage(nc, "low_in", "low_read", "low_made", "firsts", "seconds", "silued", "gated", "weighted", "mixed",
               "lowered", "masked", "u_made", "downed", "added", *MaximumPass.SEMAPHORES, pool=True) as \
            (block, low_in, low_read, low_made, firsts, seconds, silued, gated, weighted, mixed,
             lowered, masked, u_made, downed, added, *max_sems):
        units = NC * M3
        slots = []
        for n in range(units):
            up = [("first", n, i) for i in range(2 * (KD + 1))]
            rest = [("second", n, j) for j in range(2) if n >= 1] + [("lower", n)] * (n >= 2)
            slots += rest + up if n == M3 else up + rest
            if n == M3 + 2:
                slots += [("down", 0, j, i) for j in range(TC) for i in range(3)]
        slots += [("down", 1, j, i) for j in range(TC - 1) for i in range(3)]
        mp = MaximumPass(m, a, max_sems)
        downs = sum(key[0] == "down" for key in slots)
        rate = (len(mp.items) - downs) / (len(slots) - downs)
        mp.share_out([(key, 1 if key[0] == "down" else rate, (7,) if key[0] == "down" else (6, 7)) for key in slots])

        def item_count(key):
            return mp.share[key].stop

        @block.tensor
        def _(pe):
            def low(c):
                if c >= 1:
                    pe.wait_ge(mp.block_out, item_count(("lower", M3)))
                for j in range(2):
                    if j == 1:
                        pe.wait_ge(low_read, 2 * c + 1)
                    for k in range(KD):
                        last = pe.matmul(m.ps[:, 6, :], w.a[:, k, j * P:(j + 1) * P],
                                         m.xn_t[:, k, c * CH:(c + 1) * CH], start=(k == 0), stop=(k == KD - 1))
                    last.then_inc(low_in, 1)

            def first(n):
                c, i = divmod(n, M3)
                if n >= 2:
                    pe.wait_ge(gated, 2 * (n - 1))
                if i == 0:
                    pe.wait_ge(low_made, 2 * (c + 1))
                for j, wt in enumerate((w.up, w.gate)):
                    for k in range(KD):
                        pe.matmul(m.ps[:, 2 * (n % 2) + j, :], wt[:, k, i * P:(i + 1) * P],
                                  m.xn_t[:, k, c * CH:(c + 1) * CH], start=(k == 0), stop=False)
                        mp.tensor_share(pe, ("first", n, 3 * j + k))
                    pe.matmul(m.ps[:, 2 * (n % 2) + j, :], w.b[:, j, i * P:(i + 1) * P],
                              f.m0[:, j, :], start=False, stop=True).then_inc(firsts, 1)
                    mp.tensor_share(pe, ("first", n, 3 * j + KD))

            def second(n):
                pe.wait_ge(gated, 2 * n + 1)
                for j in range(2):
                    i = n % M3
                    pe.matmul(m.ps[:, 2 * (n % 2) + j, :], w.b[:, j, i * P:(i + 1) * P], f.md[:, j, :],
                              start=False, stop=True, skip_group_check=True).then_inc(seconds, 1)
                    mp.tensor_share(pe, ("second", n + 1, j))

            def lower(n):
                c, i = divmod(n, M3)
                pe.wait_ge(weighted, 2 * (n + 1))
                if i == 0 and c >= 1:
                    pe.wait_ge(masked, 2 * c)
                for r in range(2):
                    last = pe.matmul(m.ps[:, 4 + r, :], w.da[:, i, :], f.h[:, r, n % 2, :],
                                     start=(i == 0), stop=(i == M3 - 1))
                    if r == 0:
                        mp.tensor_share(pe, ("lower", n + 2))
                last.then_inc(lowered, 1)

            def down(c):
                pe.wait_ge(mixed, M3 * (c + 1))
                pe.wait_ge(u_made, c + 1)
                pe.wait_ge(mp.block_out, item_count(("lower", M3 + 2 if c == 0 else units - 1)))
                for j in range(TC):
                    t = c * TC + j
                    if j % 2 == 0 and j >= 2:
                        pe.wait_ge(added, t)
                    out = m.ps[:, 6, (j % 2) * D:(j % 2 + 1) * D]
                    for i in range(M3):
                        pe.matmul(out, f.mixed[:, (c * M3 + i) % MIXED, j * P:(j + 1) * P], w.down[:, i, :],
                                  start=(i == 0), stop=False)
                        if i % 2 == 1:
                            mp.tensor_share(pe, ("down", c, j, i // 2))
                    last = pe.matmul(out, f.u[:, j * P:(j + 1) * P], w.db[:, :], start=False, stop=True)
                    if j % 2 == 1:
                        last.then_inc(downed, 1)
                if c + 1 < NC:
                    pe.wait_ge(added, TC * (c + 1))

            low(0)
            for n in range(units):
                if n == M3:
                    second(n - 1)
                    lower(n - 2)
                    low(1)
                    first(n)
                else:
                    first(n)
                    if n >= 1:
                        second(n - 1)
                    if n >= 2:
                        lower(n - 2)
                if n == M3 + 2:
                    down(0)
            second(units - 1)
            lower(units - 2)
            lower(units - 1)
            down(1)

        @block.scalar
        def _(act):
            def silu(n, r):
                act.wait_ge((firsts, seconds)[r], 2 * n + 1)
                if n >= 1:
                    act.wait_ge(gated, 2 * (n - 1) + r + 1)
                act.activation(f.s[:, r, :], m.ps[:, 2 * (n % 2), :], ACT.Silu).then_inc(silued, 1)

            for n in range(units):
                silu(n, 0)
                silu(n, 1)

        @block.vector
        def _(dve):
            def low(c):
                cols = slice(c * CH, (c + 1) * CH)
                if c >= 1:
                    dve.wait_ge(seconds, 2 * M3 * c)
                for j in range(2):
                    dve.wait_ge(low_in, 2 * c + j + 1)
                    mp.step(dve, dve.tensor_tensor(f.m0[:, j, :], f.oh[:, 0, cols], m.ps[:, 6, :], ALU.mult))
                    dve.tensor_tensor(f.md[:, j, :], f.oh[:, 1, cols], m.ps[:, 6, :], ALU.mult).then_inc(low_read, 1)
                    dve.wait_ge(low_read, 2 * c + j + 1)
                    dve.tensor_tensor(f.md[:, j, :], f.md[:, j, :], f.m0[:, j, :], ALU.subtract).then_inc(low_made, 1)

            def gate(n, r):
                dve.wait_ge(silued, 2 * n + r + 1)
                dve.wait_ge((firsts, seconds)[r], 2 * n + 2)
                if n >= 2:
                    dve.wait_ge(lowered, n - 1)
                    dve.wait_ge(mixed, n - 1)
                dve.tensor_tensor(f.h[:, r, n % 2, :], f.s[:, r, :], m.ps[:, 2 * (n % 2) + 1, :],
                                  ALU.mult).then_inc(gated, 1)

            def lowrank(c):
                cols = slice(c * CH, (c + 1) * CH)
                dve.wait_ge(lowered, M3 * (c + 1))
                if c >= 1:
                    dve.wait_ge(downed, TC // 2 * c)
                dve.tensor_tensor(f.u[:, :], f.oh[:, 0, cols], m.ps[:, 4, :], ALU.mult).then_inc(masked, 1)
                dve.tensor_tensor(f.uu[:, :], f.oh[:, 1, cols], m.ps[:, 5, :], ALU.mult).then_inc(masked, 1)
                dve.wait_ge(masked, 2 * (c + 1))
                dve.tensor_tensor(f.u[:, :], f.u[:, :], f.uu[:, :], ALU.add).then_inc(u_made, 1)

            def add(c):
                for j in range(TC):
                    t = c * TC + j
                    for i in range(3):
                        mp.vector_share(dve, ("down", c, j, i))
                    if j % 2 == 1:
                        dve.wait_ge(downed, t // 2 + 1)
                        for u in (t - 1, t):
                            dve.tensor_tensor(sum_place(m, batch, u), sum_place(m, batch, u),
                                              m.ps[:, 6, (u % 2) * D:(u % 2 + 1) * D], ALU.add).then_inc(added, 1)

            def up_share(n):
                for i in range(2 * (KD + 1)):
                    mp.vector_share(dve, ("first", n, i))

            def second_share(n):
                for j in range(2):
                    mp.vector_share(dve, ("second", n, j))

            mp.vector_start(dve)
            low(0)
            for n in range(units):
                if n == M3:
                    second_share(n)
                    gate(n - 1, 1)
                    mp.vector_share(dve, ("lower", n))
                    low(1)
                    up_share(n)
                    gate(n, 0)
                else:
                    up_share(n)
                    second_share(n)
                    if n >= 1:
                        gate(n - 1, 1)
                    gate(n, 0)
                    mp.vector_share(dve, ("lower", n))
                if n == M3 + 1:
                    lowrank(0)
                if n == M3 + 2:
                    add(0)
            gate(units - 1, 1)
            lowrank(1)
            add(1)

        @block.gpsimd
        def _(pool):
            for n in range(units):
                c, i = divmod(n, M3)
                for r in range(2):
                    pool.wait_ge(gated, 2 * n + r + 1)
                    pool.tensor_tensor(f.h[:, r, n % 2, :], f.h[:, r, n % 2, :], f.wb[:, r, c * CH:(c + 1) * CH],
                                       ALU.mult).then_inc(weighted, 1)
                pool.wait_ge(weighted, 2 * (n + 1))
                if n >= MIXED:
                    pool.wait_ge(downed, TC // 2)
                pool.tensor_tensor(f.mixed[:, n % MIXED, :], f.h[:, 0, n % 2, :], f.h[:, 1, n % 2, :],
                                   ALU.add).then_inc(mixed, 1)

        @block.sync
        def _(sp):
            mp.sync_rows(sp)



def program(nc, io, out):
    with ExitStack() as ctx:
        def sb(name, shape, dt=F32):
            return ctx.enter_context(nc.sbuf_tensor(name, shape, dt))

        m = Memory()
        m.ps = ctx.enter_context(nc.psum_tensor("ps", [P, 8, CH], F32))
        m.x = sb("x_all", [P, B * NT, D])
        m.ident = sb("ident", [P, P])
        m.ident_h = sb("ident_h", [P, P], F16)
        m.ident_b = sb("ident_b", [P, P], BF16)
        m.mask_qk = sb("mask_qk", [P, P], BF16)
        m.mask_kq = sb("mask_kq", [P, P], BF16)
        m.ones_col = sb("ones_col", [P, 1])
        m.iota16 = sb("iota16", [P, E_RT])
        m.iota_x = sb("iota_x", [P, P])
        m.cos = sb("cos", [P, 2, NT, HD])
        m.sin = sb("sin", [P, 2, NT, HD])
        m.small = sb("small", [P, 8 * NM])
        m.lam = sb("lam", [P, 1])

        setup_constants(nc, m, io)

        @contextmanager
        def place(name, words, dt=F32):
            with nc.sbuf_tensor(name, [P, words], dt) as tensor:
                yield tensor

        def start(arena):
            ar = Arena(arena)
            m.acc = ar.take(NT, D)
            m.xn_t = ar.take(KD, S)
            return ar

        with place("arena0", ARENA) as arena:
            ar = start(arena)
            wqkv = ar.take(KD, 3 * D)
            bqkv = ar.take(3 * D)
            wup = ar.take(E_SH + E_RT, KD, F0)
            wdown = ar.take(E_SH + E_RT, D)
            wroute = ar.take(KD, E_RT)
            load_weights(nc, [
                (wqkv, rows(io.w_qkv0)), (bqkv, io.b_qkv0.partition_broadcast(P)),
                *[(wup[:, :, k, :], io.w_up0[:, k * P:(k + 1) * P, :].rearrange("e p n -> p e n")) for k in range(KD)],
                (wdown, io.w_down0.rearrange("e p n -> p e n")), (wroute, rows(io.w_router0))])
            base = ar.at
            a = attention_memory(m, ar, NM, HD, NM // 4, 8)
            f = Memory()
            ar = Arena(arena, a.free)
            f.prob = ar.take(NT, E_RT)
            f.gate_w = ar.take(NT, E_RT)
            f.top = ar.take(NT, 8)
            f.idx = ar.take(NT, 8, dtype=U32)
            f.idxf = ar.take(NT, 8)
            f.mid = ar.take(3, CH)
            with nc.Fori(0, B) as b:
                normalise(nc, m, m.acc, a.xn, m.xn_t, xload=b)
                attention_operands(nc, m, a, wqkv, bqkv, 0, False, NM, HD)
                route(nc, m, f, wroute)
                experts(nc, m, f, a, wup, wdown)
                attention(nc, m, a, 4, 32)
                attention_finish(nc, m, a, 4, 32, None, 1.0, b)

        fixed, split = 2 * NT * D + 3 * KD * D + KD * D + 4 * NM * HD, 6 * KD * F1
        rest = ARENA - fixed - split
        with place("arena1", fixed) as arena, place("weight_parts1", split, F32R) as parts:
            ar = start(arena)
            wqkv = ar.take(KD, 3 * D)
            wo = ar.take(KD, D)
            turn = (ar.take(2 * NM * HD), ar.take(2 * NM * HD))
            ar = Arena(parts)
            wg = [ar.take(KD, F1, dtype=F32R) for _ in range(2)]
            wu = [ar.take(KD, F1, dtype=F32R) for _ in range(2)]
            wd = [ar.take(F1 // P, D, dtype=F32R) for _ in range(2)]
            load_weights(nc, [(wqkv[:, :, j * D:(j + 1) * D], rows(w)) for j, w in
                              enumerate((io.wq1, io.wk1, io.wv1))] + [(wo, rows(io.wo1)),
                              (turn[0], io.cos1.partition_broadcast(P)), (turn[1], io.sin1.partition_broadcast(P))])
            with place("making1", rest) as making:
                f = Memory()
                ar = Arena(making)
                f.win = ar.take(3, F1 // P, NSEG)
                f.basis = ar.take(2, NSEG, D)
                f.w = ar.take(2, D)
                f.whole = ar.take(2, KD, P)
                f.lqk = ar.take(4, 2 * HD)
                f.dot = ar.take(2, 2 * HD)
                spline_weights(nc, m, f, io, wg, wu, wd)
                lambda_scalar(nc, m, f, io)
            with nc.Fori(0, B) as b:
                with place("attention1", rest) as data:
                    a = attention_memory(m, Arena(data), NM // 2, 2 * HD, NM // 2, 6)
                    normalise(nc, m, m.acc, a.xn, m.xn_t, xload=b)
                    attention_operands(nc, m, a, wqkv, None, turn, True, NM // 2, 2 * HD)
                    attention(nc, m, a, 2, 64)
                    attention_finish(nc, m, a, 2, 64, wo, 1.0 - LAMBDA_INIT)
                with place("ffn1", rest - FFN_PARTS) as data, place("ffn_parts1", FFN_PARTS, F32R) as parts:
                    gated_ffn(nc, m, gated_memory(data, parts), wg, wu, wd, False, b)

        fixed, split = 12000, 3 * KD * F1
        rest = ARENA - fixed - split
        with place("arena2", fixed) as arena, place("weights2", split, F32R) as parts:
            ar = start(arena)
            w = Memory()
            w.wr, w.wk, w.wv, w.wo, w.wcr = (ar.take(KD, D) for _ in range(5))
            w.wck = ar.take(KD, F2)
            w.wcv = ar.take(F2 // P, D)
            w.mix = ar.take(4, KD)
            w.omix = ar.take(4, KD)
            w.td, w.tf, w.decay, w.bonus, w.n1w, w.n1b, w.n2w, w.n2b = (ar.take(KD) for _ in range(8))
            ar = Arena(parts)
            wgu = ar.take(KD, 2 * F1, dtype=F32R)
            wp = ar.take(F1 // P, D, dtype=F32R)

            load_weights(nc, [(w.wr, rows(io.wr2)), (w.wk, rows(io.wk2)), (w.wv, rows(io.wv2)), (w.wo, rows(io.wo2)),
                              (w.wcr, rows(io.wcr2)), (w.wck, rows(io.wck2)), (w.wcv, rows(io.wcv2)),
                              *[(w.mix[:, j, :], v) for j, v in
                                enumerate((io.mix_r, io.mix_k, io.mix_v, io.mix_c))],
                              (w.td, io.td), (w.tf, io.tf), (w.n1w, io.n1w),
                              (w.n1b, io.n1b), (w.n2w, io.n2w), (w.n2b, io.n2b)])
            with place("making2", rest) as making:
                ng = (2 * F1 * D + D * F1) // P // GROUP
                f = Memory()
                ar = Arena(making)
                f.raw = ar.take(ng * GROUP)
                f.wb = ar.take(ng * GROUP, dtype=BF16)
                f.q1 = ar.take(ng * GROUP, dtype=BF16)
                f.q2 = ar.take(ng * GROUP, dtype=BF16)
                f.thr = ar.take(ng)
                f.sc = ar.take(ng, dtype=BF16)
                ternary_weights(nc, m, f, io, wgu, wp)
            time_mix_scalars(nc, m, w)
            with nc.Fori(0, B) as b:
                with place("mixes2", rest) as data:
                    f = Memory()
                    ar = Arena(data)
                    f.xn = ar.take(NT, D)
                    f.n = ar.take(NT, D)
                    f.h_t = ar.take(KD, S + 1)
                    f.mix = ar.take(3, KD, S)
                    f.rs = ar.take(KD, S)
                    f.kk = ar.take(KD, S)
                    f.st = ar.take(KD, S)
                    f.kc = Arena(data, 2 * NT * D + KD * (S + 1) + KD * S).take(NC, F2 // P, CH)
                    f.sg = Arena(data).take(2, D)
                    f.tmp = Arena(data, 2 * D).take(D)
                    normalise(nc, m, m.acc, f.xn, m.xn_t, xload=b)
                    clear_first_column(nc, f)
                    normalise(nc, m, f.xn, f.n, f.h_t[:, :, 1:S + 1], scale_w=w.n1w, scale_b=w.n1b)
                    time_mix(nc, m, f, w)
                    normalise(nc, m, f.xn, f.n, f.h_t[:, :, 1:S + 1], scale_w=w.n2w, scale_b=w.n2b)
                    channel_mix(nc, m, f, w)
                with place("ffn2", rest - FFN_PARTS) as data, place("ffn_parts2", FFN_PARTS, F32R) as parts:
                    f = gated_memory(data, parts)
                    ar = Arena(data, GATED_WORDS)
                    f.acc = ar.take(NC, CH)
                    f.sq = ar.take(CH)
                    gated_ffn(nc, m, f, [wgu[:, :, 0:F1]], [wgu[:, :, F1:2 * F1]], [wp], True, b)

        with place("arena3", ARENA) as arena:
            ar = Arena(arena)
            m.xn_t = ar.take(KD, S)
            wqkv = ar.take(KD, 3 * D)
            bqkv = ar.take(3 * D)
            wo = ar.take(KD, D)
            bo = ar.take(D)
            w = Memory()
            w.up = ar.take(KD, M3 * P)
            w.gate = ar.take(KD, M3 * P)
            w.down = ar.take(M3, D)
            w.a = ar.take(KD, 2 * P)
            w.b = ar.take(2, M3 * P)
            w.da = ar.take(M3, P)
            w.db = ar.take(D)
            w.route = ar.take(KD, E3)
            load_weights(nc, [(wqkv, rows(io.w_qkv3)), (bqkv, io.b_qkv3.partition_broadcast(P)),
                              (wo, rows(io.w_out3)), (bo, io.b_out3.partition_broadcast(P)),
                              (w.up, rows(io.up3)), (w.gate, rows(io.gate3)), (w.down, rows(io.down3)),
                              (w.a[:, :, 0:P], rows(io.up_a)), (w.a[:, :, P:2 * P], rows(io.gate_a)),
                              (w.b[:, 0, :], io.up_b), (w.b[:, 1, :], io.gate_b), (w.da, rows(io.down_a)),
                              (w.db, io.down_b), (w.route, rows(io.route3))])
            base = ar.at
            a = attention_memory(m, ar, NM, HD, NM // 4, 8)
            x_in = Arena(arena, a.free + NT * D).take(NT, D)
            m.acc = None
            f = Memory()
            ar = Arena(arena, a.free)
            f.lg = ar.take(NT, E3)
            f.top = ar.take(NT, 8)
            f.idx = ar.take(NT, 8, dtype=U32)
            f.idxf = ar.take(NT, 8)
            f.tw = ar.take(NT, 2)
            f.red = ar.take(4)
            f.red_all = ar.take(4)
            f.oh = ar.take(2, S)
            f.wb = ar.take(2, S)
            at = ar.at
            f.ohx = ar.take(2, NT, P)
            f.wx = ar.take(2, NT, P)
            ar = Arena(arena, at)
            f.m0 = ar.take(2, CH)
            f.md = ar.take(2, CH)
            f.s = ar.take(2, CH)
            f.h = ar.take(2, 2, CH)
            f.mixed = ar.take(MIXED, CH)
            f.uu, f.u = a.o[:, 0, 0:CH], a.o[:, 0, CH:S]
            with nc.Fori(0, B) as b:
                normalise(nc, m, x_in, a.xn, m.xn_t, xload=b, bias=bo)
                attention_operands(nc, m, a, wqkv, bqkv, 1, False, NM, HD)
                route_pairs(nc, m, f, w.route)
                lora_experts(nc, m, f, w, a, b)
                attention(nc, m, a, 4, 32)
                attention_finish(nc, m, a, 4, 32, wo, 1.0, b)
    
        with stage(nc, "x_out") as (block, x_out):
            @block.sync
            def _(sp):
                for b in range(B):
                    sp.dma_start(rows(out[b]), m.x[:, b * NT:(b + 1) * NT, :]).then_inc(x_out, 16)
                sp.wait_ge(x_out, 16 * B)



def rotation_tables(sign, n):
    inv = 1.0 / 10000.0 ** (np.arange(0, HD, 2, dtype=np.float32) / HD)
    ang = np.arange(n, dtype=np.float32)[:, None] * inv[None, :].astype(np.float32)
    cos, sin = np.cos(ang).astype(np.float32), np.sin(ang).astype(np.float32)
    return (np.ascontiguousarray(np.concatenate([cos, cos], 1)),
            np.ascontiguousarray(np.concatenate([-sign * sin, sign * sin], 1)))


def spline_grid(n_ctrl):
    t = np.linspace(0.0, n_ctrl - 1.0, F1 * D, dtype=np.float64)
    i = np.clip(np.floor(t).astype(np.int64), 0, n_ctrl - 2)
    f = (t - i).astype(np.float32).astype(np.float64)
    i = i.reshape(F1, D)
    f = f.reshape(F1, D)
    parts = [0.5 * (-f + 2 * f ** 2 - f ** 3), 0.5 * (2 - 5 * f ** 2 + 3 * f ** 3),
             0.5 * (f + 4 * f ** 2 - 3 * f ** 3), 0.5 * (-f ** 2 + f ** 3)]
    basis = np.zeros((NSEG, F1, D))
    o, h = np.indices((F1, D))
    for k in range(4):
        basis[i - i[:, :1] + k, o, h] = parts[k]
    window = np.clip(i[:, :1] - 1 + np.arange(NSEG)[None, :], 0, n_ctrl - 1)
    return window, basis.astype(np.float32)


def lay_out(v):
    v = {k: np.asarray(x) for k, x in v.items()}
    t = np.ascontiguousarray
    o = {"x": v["L0_attn_hidden_states"]}
    h = np.arange(NM)[:, None] * 3 * HD + np.arange(HD)[None, :]
    order = np.concatenate([(h + j * HD).ravel() for j in range(3)])
    o["w_qkv0"] = t(v["L0_attn_w_qkv"][order].T)
    o["b_qkv0"] = t(v["L0_attn_b_qkv"][order])
    o["w_up0"] = np.concatenate([v["L0_ffn_Wsh_up"], v["L0_ffn_Wrt_up"]])
    o["w_down0"] = np.concatenate([v["L0_ffn_Wsh_down"], v["L0_ffn_Wrt_down"]])
    o["w_router0"] = v["L0_ffn_W_router"]
    o["cos0"], o["sin0"] = rotation_tables(1.0, S)
    o["cos1"], o["sin1"] = (np.tile(np.repeat(x, 2, axis=0).ravel(), 2) for x in rotation_tables(-1.0, NM // 2))
    o["cos3"], o["sin3"] = rotation_tables(1.0, S)
    for n in "qkvo":
        o[f"w{n}1"] = t(v[f"L1_attn_w{n}"].T)
    for n in ("lq1", "lk1", "lq2", "lk2"):
        o[n] = v[f"L1_attn_{n}"]
    window, o["basis"] = spline_grid(v["L1_ffn_gate_cp"].shape[0])
    for n in ("gate", "up", "down"):
        o[f"win_{n}"] = t(v[f"L1_ffn_{n}_cp"][window])
    for n in ("r", "k", "v", "o", "cr", "ck", "cv"):
        o[f"w{n}2"] = v[f"L2_attn_W{n}"]
    for n, key in (("mix_r", "time_mix_r"), ("mix_k", "time_mix_k"), ("mix_v", "time_mix_v"), ("mix_c", "cm_mix"),
                   ("td", "time_decay"), ("tf", "time_faaaa"), ("n1w", "norm1_w"), ("n1b", "norm1_b"),
                   ("n2w", "norm2_w"), ("n2b", "norm2_b")):
        o[n] = v[f"L2_attn_{key}"].reshape(KD, P).T
    o["w_gate_up"] = v["L2_ffn_w_gate_up"]
    o["w_proj"] = v["L2_ffn_w_proj"]
    even_odd = np.concatenate([np.arange(0, HD, 2), np.arange(1, HD, 2)])
    qk = (np.arange(2 * NM)[:, None] * HD + even_odd[None, :]).ravel()
    order = np.concatenate([qk, np.arange(2 * D, 3 * D)])
    o["w_qkv3"] = t(v["L3_attn_w_qkv"][order].T)
    o["b_qkv3"] = t(v["L3_attn_b_qkv"][order])
    o["w_out3"] = t(v["L3_attn_w_out"].T)
    o["b_out3"] = v["L3_attn_b_out"]
    o["route3"] = t(v["L3_ffn_gate_w"].T)

    def padded(w, axis):
        widths = [(0, 0)] * w.ndim
        widths[axis] = (0, M3 * P - H3)
        return t(np.pad(w, widths))

    o["up3"] = padded(v["L3_ffn_w_up"].T, 1)
    o["gate3"] = padded(v["L3_ffn_w_gate"].T, 1)
    o["down3"] = padded(v["L3_ffn_w_down"].T, 0)
    for n in ("up", "gate"):
        o[f"{n}_a"] = t(v[f"L3_ffn_{n}_A"].reshape(P, D).T)
        o[f"{n}_b"] = padded(v[f"L3_ffn_{n}_B"].transpose(0, 2, 1).reshape(P, H3), 1)
    o["down_a"] = padded(v["L3_ffn_down_A"].reshape(P, H3).T, 0)
    o["down_b"] = t(v["L3_ffn_down_B"].transpose(0, 2, 1).reshape(P, D))
    return {k: t(x) for k, x in o.items()}


def kernel(**inputs):
    import concourse.bacc as bacc
    from concourse.bass_utils import run_bass_kernel_spmd

    nc = bacc.Bacc("TRN2", target_bir_lowering=False, num_devices=1)
    arrays = lay_out(inputs)
    io = Memory()
    io.__dict__.update({n: nc.dram_tensor(n, a.shape, mybir.dt.from_np(a.dtype), kind="ExternalInput").ap()
                        for n, a in arrays.items()})
    out = nc.dram_tensor("out", (B, S, D), F32, kind="ExternalOutput").ap()
    program(nc, io, out)
    result = run_bass_kernel_spmd(nc, [arrays], core_ids=[0])
    return result.results[0]["out"]
```

```python
import concourse.bass as bass
from concourse import mybir
from contextlib import ExitStack, contextmanager
import numpy as np

F32 = mybir.dt.float32
F16 = mybir.dt.float16
BF16 = mybir.dt.bfloat16
F32R = mybir.dt.float32r
U32 = mybir.dt.uint32
ALU = mybir.AluOpType
ACT = mybir.ActivationFunctionType
AX = mybir.AxisListType
RMAX = bass.bass_isa.ReduceOp.max
RADD = bass.bass_isa.ReduceOp.add

B, S, D = 4, 1024, 256
P = 128
NT = S // P
KD = D // P
CH = 512
NC = S // CH
TC = CH // P
HD = 16
NM = 16
LN_EPS = 1e-5
RMS_EPS = 1.1920929e-07
NEG = -1.0e30
E_SH, E_RT, F0 = 2, 16, 128
F1 = 1024
F2 = 768
H3, E3, R3 = 704, 8, 16
M3 = -(-H3 // P)
LAMBDA_INIT = 0.2
NSEG = 6
GROUP = 64
ARENA = 43600
MIXED = M3 + 3
M_ROW = 48


class Memory:
    pass


@contextmanager
def stage(nc, *names, pool=False):
    with ExitStack() as ctx:
        sems = [ctx.enter_context(nc.semaphore(n)) for n in names]
        with nc.Block(no_gpsimd_drain=not pool) as block:
            yield (block, *sems)
        for s in sems:
            nc.sync.sem_clear(s)
        nc.all_engine_barrier(sem_only=True)


class Steps:

    def __init__(self, engine, sem):
        self.engine, self.sem, self.count = engine, sem, 0

    def __call__(self, instruction):
        self.count += 1
        instruction.then_inc(self.sem, 1)
        self.engine.wait_ge(self.sem, self.count)


def view(ap, *dims):
    if len(dims) == 1:
        return ap
    names = " ".join(f"d{i}" for i in range(len(dims)))
    return ap.rearrange(f"p ({names}) -> p {names}", **{f"d{i}": n for i, n in enumerate(dims)})


def sum_so_far(m, batch, t):
    return sum_place(m, batch if m.acc is None else None, t)


def sum_place(m, batch, t):
    if batch is None:
        return m.acc[:, t, :]
    return m.x[:, bass.ds(batch * NT + t, 1), :].rearrange("p a c -> p (a c)")


class Arena:

    def __init__(self, tensor, start=0):
        self.tensor, self.at = tensor, start

    def take(self, *dims, dtype=F32):
        n = int(np.prod(dims))
        words = n if dtype in (F32, F32R, U32) else -(-n // 2)
        ap = self.tensor[:, self.at:self.at + words]
        self.at += words
        assert self.at <= self.tensor.shape[1], self.at
        return view(ap if dtype == ap.dtype else ap.bitcast(dtype), *dims)


def rows(dram, p=P):
    return dram.rearrange("(k p) n -> p k n", p=p)



def setup_constants(nc, m, io):
    with stage(nc, "cleared", "selected", "psum_cleared", "tables_in", pool=True) as (block, cleared, selected, psum_cleared, tables_in):
        @block.gpsimd
        def _(pool):
            pool.memset(m.ident[:, :], 0.0).then_inc(cleared, 1)
            pool.memset(m.mask_qk[:, :], 0.0).then_inc(cleared, 1)
            pool.memset(m.mask_kq[:, :], 0.0).then_inc(cleared, 1)
            pool.memset(m.ones_col[:, :], 1.0)
            pool.iota(m.iota16[:, :], [[1, 16]], base=0, channel_multiplier=0, allow_small_or_imprecise_dtypes=True)
            pool.iota(m.iota_x[:, :], [[1, E3], [0, R3]], base=0, channel_multiplier=0,
                      allow_small_or_imprecise_dtypes=True)
            pool.wait_ge(cleared, 3)
            pool.affine_select(out=m.ident[:, :], in_=m.ident[:, :], compare_op=ALU.not_equal, fill=1.0,
                               base=0, pattern=[[-1, P]], channel_multiplier=1).then_inc(selected, 1)
            pool.affine_select(out=m.mask_qk[:, :], in_=m.mask_qk[:, :], compare_op=ALU.is_ge, fill=NEG,
                               base=0, pattern=[[-1, P]], channel_multiplier=1).then_inc(selected, 1)
            pool.affine_select(out=m.mask_kq[:, :], in_=m.mask_kq[:, :], compare_op=ALU.is_ge, fill=NEG,
                               base=0, pattern=[[1, P]], channel_multiplier=-1).then_inc(selected, 1)

        @block.vector
        def _(dve):
            dve.memset(m.ps[:, :, :], 0.0).then_inc(psum_cleared, 1)
            dve.wait_ge(selected, 1)
            dve.tensor_copy(m.ident_h[:, :], m.ident[:, :])
            dve.tensor_copy(m.ident_b[:, :], m.ident[:, :])

        @block.sync
        def _(sp):
            sp.dma_start(m.x[:, 0:NT, :], rows(io.x[0])).then_inc(tables_in, 16)
            n = 1
            for i, (cos, sin) in enumerate(((io.cos0, io.sin0), (io.cos3, io.sin3))):
                sp.dma_start(m.cos[:, i, :, :], rows(cos)).then_inc(tables_in, 16)
                sp.dma_start(m.sin[:, i, :, :], rows(sin)).then_inc(tables_in, 16)
                n += 2
            sp.wait_ge(tables_in, 16 * n)


def load_weights(nc, pairs, later=(), later_in=None):
    with stage(nc, "weights_in") as (block, weights_in):
        @block.sync
        def _(sp):
            for dst, src in pairs[0::2]:
                sp.dma_start(dst, src).then_inc(weights_in, 16)
            for dst, src in later[0::2]:
                sp.dma_start(dst, src).then_inc(later_in, 16)
            sp.wait_ge(weights_in, 16 * len(pairs))

        @block.scalar
        def _(act):
            for dst, src in pairs[1::2]:
                act.dma_start(dst, src).then_inc(weights_in, 16)
            for dst, src in later[1::2]:
                act.dma_start(dst, src).then_inc(later_in, 16)



class Normalisation:

    SEMAPHORES = ("src_in", "stats", "std_in", "std_done", "rstd_in", "normed", "tile_turned", "pair_stored")

    def __init__(self, m, src, dst, dst_t, sems, xload=None, bias=None, scale_w=None, scale_b=None, after=None):
        self.m, self.src, self.dst, self.dst_t, self.xload, self.bias = m, src, dst, dst_t, xload, bias
        self.scale_w, self.scale_b = scale_w, scale_b
        self.after = after
        self.bank = 4 if after is None else 0
        (self.src_in, self.stats, self.std_in, self.std_done, self.rstd_in, self.normed, self.turned,
         self.stored) = sems
        small = m.norm[:, 0 if after is None else 1, :]
        self.var = small[:, 0:2 * NT].rearrange("p (t c) -> p t c", c=2)
        self.st = small[:, 2 * NT:8 * NT].rearrange("p (t c) -> p t c", c=6)
        self.std, self.rstd, self.veps = (small[:, i * NT:(i + 1) * NT] for i in range(8, 11))

    def vector(self, dve):
        src = self.src
        for t in range(NT):
            if self.after is not None:
                dve.wait_ge(self.after.normed, t + 1)
            if self.xload is not None and t % 2 == 0:
                dve.wait_ge(self.src_in, t // 2 + 1)
            dve.bn_stats(self.st[:, t, :], src[:, t, :]).then_inc(self.stats, 1)
        for t in range(NT):
            dve.wait_ge(self.stats, t + 1)
            dve.bn_aggr(self.var[:, t, :], self.st[:, t, :]).then_inc(self.std_in, 1)
        dve.wait_ge(self.std_in, NT)
        dve.tensor_scalar(self.veps, self.var[:, :, 1], LN_EPS, None, ALU.add).then_inc(self.std_in, 1)
        dve.wait_ge(self.std_done, 1)
        dve.reciprocal(self.rstd, self.std).then_inc(self.rstd_in, 1)
        dve.wait_ge(self.rstd_in, 1)
        for t in range(NT):
            dve.tensor_scalar(self.dst[:, t, :], src[:, t, :], self.var[:, t, 0:1], self.rstd[:, t:t + 1],
                              ALU.subtract, ALU.mult).then_inc(self.normed, 1)
        if self.bias is not None:
            dve.tensor_tensor(self.m.x[:, bass.ds(self.xload * NT, NT), :], src[:, :, :],
                              self.bias[:, :].unsqueeze(1).broadcast_to([P, NT, D]), ALU.add)

    def tensor(self, pe):
        for t in range(NT):
            pe.wait_ge(self.normed, t + 1)
            for k in range(KD):
                at = (2 * k + t % 2) * P
                last = pe.transpose(self.m.ps[:, self.bank + t // 2, at:at + P], self.dst[:, t, k * P:(k + 1) * P],
                                    self.m.ident[:, :])
            last.then_inc(self.turned, 1)

    def scalar(self, act):
        m = self.m
        if self.xload is not None:
            for t in range(0, NT, 2):
                act.activation(self.src[:, t:t + 2, :], m.x[:, bass.ds(self.xload * NT + t, 2), :],
                               ACT.Copy).then_inc(self.src_in, 1)
        act.wait_ge(self.std_in, NT + 1)
        act.activation(self.std, self.veps, ACT.Sqrt).then_inc(self.std_done, 1)
        for i in range(NT // 2):
            act.wait_ge(self.turned, 2 * (i + 1))
            cols = slice(2 * i * P, 2 * (i + 1) * P)
            pair = m.ps[:, self.bank + i, :].rearrange("p (k n) -> p k n", k=KD)
            if self.scale_w is None:
                act.activation(self.dst_t[:, :, cols], pair, ACT.Identity).then_inc(self.stored, 1)
            else:
                for k in range(KD):
                    last = act.activation(self.dst_t[:, k, cols], pair[:, k, :], ACT.Identity,
                                          bias=self.scale_b[:, k:k + 1], scale=self.scale_w[:, k:k + 1])
                last.then_inc(self.stored, 1)


def normalise(nc, m, src, dst, dst_t, **options):
    with stage(nc, *Normalisation.SEMAPHORES) as (block, *sems):
        norm = Normalisation(m, src, dst, dst_t, sems, **options)

        @block.vector
        def _(dve):
            norm.vector(dve)

        @block.tensor
        def _(pe):
            norm.tensor(pe)

        @block.scalar
        def _(act):
            norm.scalar(act)


def normalise_twice(nc, m, f, batch, scale_w, scale_b):
    n = len(Normalisation.SEMAPHORES)
    seconds = [f"second_{name}" for name in Normalisation.SEMAPHORES]
    with stage(nc, *Normalisation.SEMAPHORES, *seconds, pool=True) as (block, *sems):
        first = Normalisation(m, m.acc, f.xn, m.xn_t, sems[:n], xload=batch)
        second = Normalisation(m, f.xn, f.n, f.h_t[:, :, 1:S + 1], sems[n:], scale_w=scale_w, scale_b=scale_b,
                               after=first)

        @block.vector
        def _(dve):
            first.vector(dve)
            second.vector(dve)

        @block.tensor
        def _(pe):
            first.tensor(pe)
            second.tensor(pe)

        @block.scalar
        def _(act):
            first.scalar(act)
            second.scalar(act)

        @block.gpsimd
        def _(pool):
            pool.memset(f.h_t[:, :, 0:1], 0.0)



def attention_operands(nc, m, a, src, batch, out_bias, wqkv, bias, table, rms, heads, vd):
    gh = 2 * NM
    behind = 1 if rms else 0
    lag = 2 + behind

    def sums(t):
        return m.small[:, (t % 2) * gh:(t % 2 + 1) * gh]

    def roots(t):
        return m.small[:, (2 + t % 2) * gh:(3 + t % 2) * gh]

    half = HD // 2
    if isinstance(table, int):
        cos = [m.cos[:, table, t, :].unsqueeze(1).broadcast_to([P, gh, HD]) for t in range(NT)]
        sin = [m.sin[:, table, t, :].unsqueeze(1).broadcast_to([P, gh, HD]) for t in range(NT)]
    else:
        cos, sin = ([v.rearrange("p (h c) -> p h c", c=HD)] * NT for v in table)
    names = ["proj", "taken", "steps", "pool_done", "rotated", "hi", "lo", "stacked", "turned", "stored", "cleared",
             "rms_in", "rms_std", "squared"]
    with stage(nc, *names, *Normalisation.SEMAPHORES, pool=True) as (block, proj, taken, steps, pool_done, rotated, hi, lo, stacked, turned, stored,
                               cleared, rms_in, rms_std, squared, *norm_sems):
        norm = Normalisation(m, src, a.xn, m.xn_t, norm_sems, xload=batch, bias=out_bias)

        def kcols(buf, parity, slot, n=1, step=1):
            c0 = P * parity + 64 * parity + HD * slot
            v = a.ks[:, buf, :].rearrange("p (n c) -> p n c", c=2 * P)
            if n == 1:
                return v[:, :, c0:c0 + HD]
            return v[:, :, c0:c0 + HD * step * n].rearrange("p n (s c) -> p n s c", c=HD * step)[:, :, :, 0:HD]

        @block.tensor
        def _(pe):
            def turn(t):
                pe.wait_ge(stacked, 3 * (t + 1))
                if t >= 1:
                    pe.wait_ge(stored, 2 * t)
                psq = m.ps[:, 4, :].bitcast(F16)
                psk = m.ps[:, 5:7, :].rearrange("p a b -> p (a b)").bitcast(F16)
                for n in range(NM // 2):
                    pe.transpose(psq[:, n * P:(n + 1) * P], a.qs[:, t % 2, n * P:(n + 1) * P], m.ident_h[:, :])
                for n in range(NM):
                    last = pe.transpose(psk[:, n * P:(n + 1) * P], a.ks[:, t % 2, n * P:(n + 1) * P], m.ident_h[:, :])
                last.then_inc(turned, 1)

            norm.tensor(pe)
            for t in range(NT):
                if t >= 2:
                    pe.wait_ge(taken, 2 * (t - 1))
                pe.wait_ge(norm.stored, t // 2 + 1)
                if t == 2:
                    pe.wait_ge(norm.stored, NT // 2)
                for j, (c0, w) in enumerate(((0, 512), (512, 256))):
                    for k in range(KD):
                        last = pe.matmul(m.ps[:, 2 * (t % 2) + j, 0:w], m.xn_t[:, k, t * P:(t + 1) * P],
                                         wqkv[:, k, c0:c0 + w], start=(k == 0), stop=(k == KD - 1))
                last.then_inc(proj, 1)
                if t >= lag:
                    turn(t - lag)
            for t in range(NT - lag, NT):
                turn(t)

        @block.vector
        def _(dve):
            step = Steps(dve, steps)

            def store(t):
                dve.wait_ge(turned, t + 1)
                dve.tensor_copy(a.q[:, :, t * P:(t + 1) * P],
                                m.ps[:, 4, :].bitcast(F16).rearrange("p (n c) -> p n c", c=P)).then_inc(stored, 1)

            def take(t):
                qk = a.qk[:, t % 3, :]
                v_out = a.v[:, t, :, 0:vd]
                dve.wait_ge(proj, t + 1)
                if t >= 3:
                    dve.wait_ge(lo, 3 * (t - 2))
                psv = m.ps[:, 2 * (t % 2) + 1, 0:D].rearrange("p (h c) -> p h c", h=heads)
                if bias is not None:
                    dve.tensor_tensor(qk, m.ps[:, 2 * (t % 2), :], bias[:, 0:512], ALU.add).then_inc(taken, 1)
                    dve.tensor_tensor(v_out, psv, bias[:, 512:768].rearrange("p (h c) -> p h c", h=heads),
                                      ALU.add).then_inc(taken, 1)
                else:
                    dve.tensor_copy(qk, m.ps[:, 2 * (t % 2), :]).then_inc(taken, 1)
                    dve.tensor_copy(v_out, psv).then_inc(taken, 1)

            def mean_squares(t):
                ss = sums(t)
                dve.wait_ge(squared, t + 1)
                step(dve.tensor_reduce(ss, a.t1[:, t % 2, :].rearrange("p (h c) -> p h c", c=HD), AX.X, ALU.add))
                dve.tensor_scalar(ss, ss, 1.0 / HD, RMS_EPS, ALU.mult, ALU.add).then_inc(rms_in, 1)

            def rotate(t):
                qk = a.qk[:, t % 3, :]
                qk3 = qk.rearrange("p (h c) -> p h c", c=HD)
                t1 = a.t1[:, t % 2, :]
                t13 = t1.rearrange("p (h c) -> p h c", c=HD)
                t23 = a.t2[:, t % 2, :].rearrange("p (h c) -> p h c", c=HD)
                dve.wait_ge(taken, 2 * t + 1)
                if rms:
                    dve.wait_ge(rms_std, t + 1)
                    step(dve.reciprocal(roots(t), roots(t)))
                    step(dve.tensor_tensor(qk3, qk3, roots(t).unsqueeze(2).broadcast_to([P, gh, HD]), ALU.mult))
                step(dve.tensor_tensor(t13, qk3, cos[t], ALU.mult))
                dve.tensor_tensor(t23[:, :, 0:half], qk3[:, :, half:HD],
                                  sin[t][:, :, 0:half], ALU.mult)
                step(dve.tensor_tensor(t23[:, :, half:HD], qk3[:, :, 0:half],
                                       sin[t][:, :, half:HD], ALU.mult))
                dve.tensor_tensor(qk, t1, a.t2[:, t % 2, :], ALU.add).then_inc(rotated, 1)

            norm.vector(dve)
            for t in range(NT + lag):
                if t < NT:
                    take(t)
                if 0 <= t - behind < NT:
                    rotate(t - behind)
                if rms and t < NT:
                    mean_squares(t)
                if t >= lag:
                    store(t - lag)

        @block.scalar
        def _(act):
            def store(t):
                act.wait_ge(turned, t + 1)
                act.activation(a.k[:, :, t * P:(t + 1) * P],
                               m.ps[:, 5:7, :].rearrange("p a b -> p (a b)").bitcast(F16).rearrange(
                                   "p (n c) -> p n c", c=P), ACT.Copy).then_inc(stored, 1)

            def square(t):
                act.wait_ge(taken, 2 * t + 1)
                if t >= 2:
                    act.wait_ge(rotated, t - 1)
                act.activation(a.t1[:, t % 2, :], a.qk[:, t % 3, :], ACT.Square).then_inc(squared, 1)

            def root(t):
                act.wait_ge(rms_in, t + 1)
                act.activation(roots(t), sums(t), ACT.Sqrt).then_inc(rms_std, 1)

            def high(t):
                qk3 = a.qk[:, t % 3, :].rearrange("p (h c) -> p h c", c=HD)
                act.wait_ge(rotated, t + 1)
                if t == 0:
                    act.wait_ge(cleared, 4)
                qs4 = a.qs[:, t % 2, :].rearrange("p (h s c) -> p h s c", h=NM, c=HD)
                act.activation(qs4[:, :, 0:2, :], qk3[:, 0:NM, :].unsqueeze(2).broadcast_to([P, NM, 2, HD]),
                               ACT.Copy).then_inc(hi, 1)
                for parity in range(2):
                    act.activation(kcols(t % 2, parity, 0, 2, 2),
                                   qk3[:, NM + parity:2 * NM:2, :].unsqueeze(2).broadcast_to([P, NM // 2, 2, HD]),
                                   ACT.Copy).then_inc(hi, 1)

            norm.scalar(act)
            for t in range(NT + lag):
                if rms and t < NT:
                    square(t)
                if t >= lag:
                    store(t - lag)
                if 0 <= t - behind < NT:
                    high(t - behind)
                if rms and t < NT:
                    root(t)

        @block.gpsimd
        def _(pool):
            pool.memset(a.qs[:, :, :].bitcast(F32), 0.0).then_inc(cleared, 1)
            pool.memset(a.ks[:, :, :].bitcast(F32), 0.0).then_inc(cleared, 1)
            pool.wait_ge(cleared, 2)
            for parity in range(2):
                c0 = 192 * parity + M_ROW
                pool.memset(a.ks[:, :, :].rearrange("p b (n c) -> p b n c", c=2 * P)[:, :, :, c0:c0 + 2],
                            1.0).then_inc(cleared, 1)
            pool.memset(a.v[:, :, :, vd:vd + 1], 1.0)
            for t in range(NT):
                qk3 = a.qk[:, t % 3, :].rearrange("p (h c) -> p h c", c=HD)
                qs4 = a.qs[:, t % 2, :].rearrange("p (h s c) -> p h s c", h=NM, c=HD)
                pool.wait_ge(hi, 3 * (t + 1))
                pool.tensor_tensor(qs4[:, :, 2, :], qk3[:, 0:NM, :], qs4[:, :, 0, :], ALU.subtract).then_inc(stacked, 1)
                for parity in range(2):
                    pool.tensor_tensor(kcols(t % 2, parity, 1), qk3[:, NM + parity:2 * NM:2, :],
                                       kcols(t % 2, parity, 0), ALU.subtract).then_inc(stacked, 1)
                pool.wait_ge(stacked, 3 * (t + 1))
                for _ in range(3):
                    pool.sem_inc(lo, 1)


class MaximumPass:

    SEMAPHORES = ("score_block_in", "score_block_out", "max_steps", "max_split", "max_rows_set_0", "max_rows_set_1")

    def __init__(self, m, a, sems):
        self.m, self.a, self.maps = m, a, 4
        self.block_in, self.block_out, self.steps, self.split_done, *self.rows_set = sems
        self.step_count = 0
        self.items, self.done = [], {}
        for g in range(NM // self.maps):
            i = 0
            for h in range(self.maps):
                for qt in range(NT):
                    for c in range(qt // TC + 1):
                        self.items.append(("block", g, h, qt, c))
                        i += 1
                        if i == 4 and g:
                            self.items.append(("turn", g - 1))
            self.done[len(self.items) - 1] = g
        self.items.append(("turn", NM // self.maps - 1))
        self.banks, self.share = [], {}

    def share_out(self, slots):
        total = 0.0
        for key, number, banks in slots:
            total += number
            start = len(self.banks)
            while len(self.banks) < min(round(total), len(self.items)):
                self.banks.append(banks[len(self.banks) % len(banks)])
            self.share[key] = range(start, len(self.banks))
        assert len(self.banks) == len(self.items)

    def bank(self, n):
        return self.m.ps[:, self.banks[n], :]

    def tensor_item(self, pe, n):
        m, a = self.m, self.a
        out = self.bank(n)
        if self.items[n][0] == "turn":
            g = self.items[n][1]
            pe.wait_ge(self.split_done, g + 1)
        before = [i for i in range(n) if self.banks[i] == self.banks[n]]
        if before:
            pe.wait_ge(self.block_out, before[-1] + 1)
        if self.items[n][0] == "turn":
            rows_out = out[0:2 * self.maps, :].bitcast(F16)
            for qt in range(NT):
                last = pe.transpose(rows_out[:, qt * P:(qt + 1) * P], a.mt[:, g % 2, qt, :], m.ident_h[:, :])
            last.then_inc(self.block_in, 1)
            return
        _, g, h, qt, c = self.items[n]
        w = min(CH, (qt + 1) * P - c * CH)
        diag = qt // TC == c
        hh = g * self.maps + h
        last = pe.matmul(out[:, 0:w], a.q[:, hh // 2, qt * P:(qt + 1) * P], a.k[:, hh, c * CH:c * CH + w],
                         start=True, stop=not diag)
        if diag:
            last = pe.matmul(out[:, w - P:w], m.ident_b[:, :], m.mask_qk[:, :], start=False, stop=True)
        last.then_inc(self.block_in, 1)

    def step(self, dve, instruction):
        self.step_count += 1
        instruction.then_inc(self.steps, 1)
        dve.wait_ge(self.steps, self.step_count)

    def tensor_share(self, pe, key):
        for n in self.share.get(key, ()):
            self.tensor_item(pe, n)

    def vector_share(self, dve, key):
        for n in self.share.get(key, ()):
            self.vector_item(dve, n)

    def vector_start(self, dve):
        self.step(dve, dve.memset(self.a.mp[:, :, :, :], NEG))

    def vector_item(self, dve, n):
        a, out = self.a, self.bank(n)
        dve.wait_ge(self.block_in, n + 1)
        if self.items[n][0] == "turn":
            g = self.items[n][1]
            if g >= 2:
                dve.wait_ge(self.rows_set[g % 2], 16 * self.maps * (g // 2))
            dve.tensor_copy(a.mrow[0:2 * self.maps, g % 2, :], out[0:2 * self.maps, :].bitcast(F16)
                            ).then_inc(self.block_out, 1)
            return
        _, g, h, qt, c = self.items[n]
        w = min(CH, (qt + 1) * P - c * CH)
        dve.reduce_max(a.mp[:, h, qt, c:c + 1], out[:, 0:w], AX.X).then_inc(self.block_out, 1)
        if n in self.done:
            dve.wait_ge(self.block_out, n + 1)
            mt = a.mt[:, g % 2, :, :].rearrange("p t (h s) -> p h t s", s=2)
            self.step(dve, dve.tensor_reduce(a.mf[:, :, :], a.mp[:, :, :, :], AX.X, ALU.max, negate=True))
            self.step(dve, dve.tensor_copy(mt[:, :, :, 0], a.mf[:, :, :]))
            dve.tensor_tensor(mt[:, :, :, 1], a.mf[:, :, :], mt[:, :, :, 0], ALU.subtract).then_inc(self.split_done, 1)

    def sync_rows(self, sp):
        for n, item in enumerate(self.items):
            if item[0] == "turn":
                g = item[1]
                sp.wait_ge(self.block_out, n + 1)
                for h in range(self.maps):
                    r0 = M_ROW + 64 * (h % 2)
                    sp.dma_start(self.a.q[r0:r0 + 2, (g * self.maps + h) // 2, :],
                                 self.a.mrow[2 * h:2 * h + 2, g % 2, :]).then_inc(self.rows_set[g % 2], 16)
        for rows_set in self.rows_set:
            sp.wait_ge(rows_set, 16 * NM // 2)


def attention(nc, m, a, maps, width):
    groups = NM // maps
    n_exp = NM * NT
    ring = a.p.shape[1]
    lag = 1 if maps == 4 else 2
    with stage(nc, "scored", "exped", "summed", "evac") as (block, scored, exped, summed, evac):
        @block.tensor
        def _(pe):
            def score(u):
                n, hh = divmod(u, maps)
                g, kt = divmod(n, NT)
                h = g * maps + hh
                if u >= 3:
                    pe.wait_ge(exped, u - 2)
                bank = 2 + 2 * (u % 3)
                for c in range(kt // TC, NC):
                    q0 = max(kt * P, c * CH)
                    diag = c == kt // TC
                    last = pe.matmul(m.ps[:, bank + c, q0 - c * CH:CH], a.k[:, h, kt * P:(kt + 1) * P],
                                     a.q[:, h // 2, q0:(c + 1) * CH], start=True, stop=not diag)
                    if diag:
                        last = pe.matmul(m.ps[:, bank + c, q0 - c * CH:q0 - c * CH + P], m.ident_b[:, :],
                                         m.mask_kq[:, :], start=False, stop=True)
                last.then_inc(scored, 1)

            def values(n):
                g, kt = divmod(n, NT)
                pe.wait_ge(exped, maps * (n + 1))
                for c in range(kt // TC, NC):
                    if kt == 0 and g >= 1:
                        pe.wait_ge(evac, NC * (g - 1) + c + 1)
                    q0 = max(kt * P, c * CH)
                    for hh in range(maps):
                        h = g * maps + hh
                        p = a.p[:, (maps * n + hh) % ring, q0:(c + 1) * CH]
                        vh = h * a.v.shape[2] // NM
                        w = a.v.shape[3]
                        last = pe.matmul(m.ps[width * hh:width * hh + w, c, q0 - c * CH:CH], a.v[:, kt, vh, :], p,
                                         start=(kt == 0), stop=(kt == TC * (c + 1) - 1))
                last.then_inc(summed, 1)

            for n in range(groups * NT):
                for hh in range(maps):
                    score(maps * n + hh)
                    if hh == maps // 2 and n >= lag:
                        values(n - lag)
            for n in range(groups * NT - lag, groups * NT):
                values(n)

        @block.scalar
        def _(act):
            def store(g, c):
                act.wait_ge(summed, NT * g + TC * (c + 1))
                act.activation(a.o[:, g, c * CH:(c + 1) * CH], m.ps[:, c, :], ACT.Copy).then_inc(evac, 1)

            for u in range(n_exp):
                n, hh = divmod(u, maps)
                g, kt = divmod(n, NT)
                act.wait_ge(scored, u + 1)
                if u >= ring:
                    act.wait_ge(summed, (u - ring) // maps + 1)
                bank = 2 + 2 * (u % 3)
                act.activation(a.p[:, u % ring, kt * P:S],
                               m.ps[:, bank:bank + 2, :].rearrange("p a b -> p (a b)")[:, kt * P:S],
                               ACT.Exp, scale=HD ** -0.5).then_inc(exped, 1)
                if hh == maps - 1:
                    if kt == TC - 1 + lag:
                        store(g, 0)
                    if kt == lag - 1 and g >= 1:
                        store(g - 1, 1)
            store(groups - 1, 1)


def attention_finish(nc, m, a, maps, width, wout, out_scale, batch=None, stored=None):
    groups = NM // maps
    banks = groups * P // CH
    with stage(nc, "turned", "steps", "given", "y_turned", "y_stored", "projected", "added") as \
            (block, turned, steps, given, y_turned, y_stored, projected, added):
        if stored is not None:
            out, out_stored = stored
            by_batch = out.rearrange("b (t p) n -> p (b t) n", p=P)

            @block.sync
            def _(sp):
                for t in range(0, NT, TC):
                    sp.wait_ge(added, t + TC)
                    tiles = bass.ds(batch * NT + t, TC)
                    sp.dma_start(by_batch[:, tiles, :], m.x[:, tiles, :]).then_inc(out_stored, 16)

        @block.tensor
        def _(pe):
            def turn_back(t):
                pe.wait_ge(given, t + 1)
                if t >= 1:
                    pe.wait_ge(y_stored, t)
                for k in range(KD):
                    last = pe.transpose(m.ps[:, 6, k * P:(k + 1) * P], a.y[:, t % 2, k * P:(k + 1) * P], m.ident[:, :])
                last.then_inc(y_turned, 1)

            def project(t):
                pe.wait_ge(y_stored, t + 1)
                if t >= 1:
                    pe.wait_ge(added, t)
                for k in range(KD):
                    last = pe.matmul(m.ps[:, 7, 0:D], a.yt[:, t % 2, k * P:(k + 1) * P], wout[:, k, :],
                                     start=(k == 0), stop=(k == KD - 1))
                last.then_inc(projected, 1)

            for t in range(NT):
                if t >= 2:
                    pe.wait_ge(given, t - 1)
                bank = banks * (t % 2)
                for g in range(groups):
                    last = pe.transpose(m.ps[:, bank + g // TC, (g % TC) * P:(g % TC + 1) * P],
                                        a.o[:, g, t * P:(t + 1) * P], m.ident[:, :])
                last.then_inc(turned, 1)
                if wout is not None and t >= 1:
                    turn_back(t - 1)
                if wout is not None and t >= 2:
                    project(t - 2)
            if wout is not None:
                turn_back(NT - 1)
                project(NT - 2)
                project(NT - 1)

        if wout is not None:
            @block.scalar
            def _(act):
                for t in range(NT):
                    act.wait_ge(y_turned, t + 1)
                    act.activation(a.yt[:, t % 2, :], m.ps[:, 6, 0:D], ACT.Copy).then_inc(y_stored, 1)

        @block.vector
        def _(dve):
            step = Steps(dve, steps)

            def add(t):
                dve.wait_ge(projected, t + 1)
                dve.scalar_tensor_tensor(sum_place(m, batch, t), m.ps[:, 7, 0:D], out_scale, sum_so_far(m, batch, t),
                                         ALU.mult, ALU.add).then_inc(added, 1)

            for t in range(NT):
                bank = banks * (t % 2)
                sums = m.ps[:, bank:bank + banks, :].rearrange("p a b -> p (a b)").rearrange("p (h c) -> p h c", c=width)
                y = a.y[:, t % 2, :]
                dve.wait_ge(turned, t + 1)
                if t >= 1:
                    dve.wait_ge(given, t)
                if maps == 4:
                    r = m.small[:, 0:NM]
                    y3 = y.rearrange("p (h c) -> p h c", c=HD)
                    step(dve.reciprocal(r, sums[:, :, HD]))
                    if wout is not None and t >= 2:
                        dve.wait_ge(y_turned, t - 1)
                    ins = dve.tensor_tensor(y3, sums[:, :, 0:HD], r.unsqueeze(2).broadcast_to([P, NM, HD]), ALU.mult)
                    if wout is not None:
                        ins.then_inc(given, 1)
                    else:
                        ins.then_inc(given, 1)
                        dve.wait_ge(given, t + 1)
                        dve.tensor_tensor(sum_place(m, batch, t), m.acc[:, t, :], y, ALU.add)
                else:
                    vd = 2 * HD
                    r = m.small[:, 0:NM]
                    pair = sums.rearrange("p (h s) c -> p h s c", s=2)
                    r2 = r.rearrange("p (h s) -> p h s", s=2)
                    y3 = y.rearrange("p (h c) -> p h c", c=vd)
                    z3 = a.z[:, :].rearrange("p (h c) -> p h c", c=vd)
                    step(dve.reciprocal(r, sums[:, :, vd]))
                    step(dve.tensor_scalar(r2[:, :, 1], r2[:, :, 1], m.lam[:, 0:1], None, ALU.mult))
                    if t >= 2:
                        dve.wait_ge(y_turned, t - 1)
                    dve.tensor_tensor(y3, pair[:, :, 0, 0:vd], r2[:, :, 0].unsqueeze(2).broadcast_to([P, NM // 2, vd]),
                                      ALU.mult)
                    step(dve.tensor_tensor(z3, pair[:, :, 1, 0:vd],
                                           r2[:, :, 1].unsqueeze(2).broadcast_to([P, NM // 2, vd]), ALU.mult))
                    dve.tensor_tensor(y, y, a.z[:, :], ALU.subtract).then_inc(given, 1)
                    dve.wait_ge(given, t + 1)
                if wout is not None and t >= 2:
                    add(t - 2)
            if wout is not None:
                add(NT - 2)
                add(NT - 1)


def attention_memory(m, ar, heads, vd, groups, ring):
    a = Memory()
    a.q = ar.take(NM // 2, S, dtype=F16)
    a.o = Arena(ar.tensor, ar.at).take(groups, S)
    ar.take(S)
    key_place = ar.at
    a.k = ar.take(NM, S, dtype=F16)
    a.v = ar.take(NT, heads, vd + 1)
    a.mp = ar.take(4, NT, 2)
    a.mf = ar.take(4, NT)
    a.mt = ar.take(2, NT, 8, dtype=F16)
    a.mrow = ar.take(2, S, dtype=F16)
    base = ar.at
    a.free = base
    a.p = ar.take(ring, S)
    pre = Arena(ar.tensor, base)
    a.qk = pre.take(3, 512)
    a.t1 = pre.take(2, 512)
    a.t2 = pre.take(2, 512)
    a.qs = pre.take(2, NM * 64, dtype=F16)
    a.ks = pre.take(2, NM * P, dtype=F16)
    post = Arena(ar.tensor, base)
    a.y = post.take(2, D)
    a.yt = post.take(2, D)
    a.z = post.take(D)
    pre = Arena(ar.tensor, key_place)
    a.xn = pre.take(NT, D)
    a.x_in = pre.take(NT, D)
    return a



GATED_WORDS = 5 * CH
FFN_PARTS = 2 * KD * S + 4 * F1 // P * CH


def gated_memory(data, parts):
    f = Memory()
    ar = Arena(data)
    f.inter = ar.take(3, CH)
    f.gate = ar.take(2, CH)
    ar = Arena(parts)
    f.x = ar.take(2, KD, S, dtype=F32R)
    f.h = ar.take(2, 2, F1 // P, CH, dtype=F32R)
    return f


def gated_ffn(nc, m, f, wg, wu, wd, rms, batch):
    ni = F1 // P
    units = NC * ni
    with stage(nc, "x_high", "x_low", "upped", "silued", "gated", "high", "low", "square_even", "square_odd", "summed",
               "downed", "added", "steps", "sumsq", "ms_in", "rms_done", pool=rms) as \
            (block, x_high, x_low, upped, silued, gated, high, low, square_even, square_odd, summed,
             downed, added, steps, sumsq, ms_in, rms_done):
        ms, root, inv = (m.small[:, i * NT:(i + 1) * NT] for i in range(3))

        def sums(c):
            return m.ps[:, 0 if c == NC - 1 else 7, 0:TC]

        def adds(n):
            return (ni - 1) * (n // ni) + n % ni

        products = [(0, 0), (0, 1), (1, 0)][:1 + len(wg)]

        @block.tensor
        def _(pe):
            def up(n):
                c, i = divmod(n, ni)
                if n >= 3:
                    pe.wait_ge(gated, n - 2)
                if i == 0:
                    pe.wait_ge(x_low, KD * (c + 1))
                for j, w in enumerate((wg, wu)):
                    terms = [(k, q) for k in range(KD) for q in products]
                    for k, (wp, xp) in terms:
                        last = pe.matmul(m.ps[:, 2 * (n % 3) + j, :], w[wp][:, k, i * P:(i + 1) * P],
                                         f.x[:, xp, k, c * CH:(c + 1) * CH], start=(k, (wp, xp)) == terms[0],
                                         stop=(k, (wp, xp)) == terms[-1])
                    last.then_inc(upped, 1)

            def sum_squares(c):
                pe.wait_ge(summed, (ni - 1) * (c + 1))
                for j in range(TC):
                    last = pe.matmul(sums(c)[:, j:j + 1], f.acc[:, c, j * P:(j + 1) * P], m.ones_col[:, 0:1],
                                     start=True, stop=True)
                last.then_inc(sumsq, 1)

            def down(c):
                pe.wait_ge(low, ni * (c + 1))
                if rms and c < NC - 1:
                    sum_squares(c)
                for j in range(TC):
                    if rms and c == NC - 1 and j == 2:
                        pe.wait_ge(gated, units)
                        sum_squares(c)
                    t = c * TC + j
                    if j % 2 == 0:
                        if c >= 1:
                            pe.wait_ge(added, t - TC + 2)
                        if rms and j == 2 and c < NC - 1:
                            pe.wait_ge(ms_in, c + 1)
                    terms = [(i, q) for i in range(ni) for q in products]
                    for i, (wp, hp) in terms:
                        last = pe.matmul(m.ps[:, 6 + j // 2, (j % 2) * D:(j % 2 + 1) * D],
                                         f.h[:, hp, c % 2, i, j * P:(j + 1) * P], wd[wp][:, i, :],
                                         start=(i, (wp, hp)) == terms[0], stop=(i, (wp, hp)) == terms[-1])
                    if j % 2 == 1:
                        last.then_inc(downed, 1)

            for n in range(units):
                up(n)
                if n % ni == 2 and n >= ni:
                    down(n // ni - 1)
            down(NC - 1)

        @block.scalar
        def _(act):
            def split_x(c):
                for k in range(KD):
                    act.activation(f.x[:, 0, k, c * CH:(c + 1) * CH], m.xn_t[:, k, c * CH:(c + 1) * CH],
                                   ACT.Copy).then_inc(x_high, 1)

            def split(n):
                c, i = divmod(n, ni)
                act.wait_ge(gated, n + 1)
                act.activation(f.h[:, 0, c % 2, i, :], f.inter[:, n % 3, :], ACT.Copy).then_inc(high, 1)

            def roots(c):
                act.wait_ge(ms_in, c + 1)
                act.activation(root[:, c * TC:(c + 1) * TC], ms[:, c * TC:(c + 1) * TC], ACT.Sqrt).then_inc(rms_done, 1)

            split_x(0)
            for n in range(units):
                act.wait_ge(upped, 2 * n + 1)
                if n >= 2:
                    act.wait_ge(gated, n - 1)
                act.activation(f.gate[:, n % 2, :], m.ps[:, 2 * (n % 3), :], ACT.Silu).then_inc(silued, 1)
                if n >= 1:
                    split(n - 1)
                if n == 1:
                    split_x(1)
                if rms and n == ni + 2:
                    roots(0)
            split(units - 1)
            if rms:
                roots(NC - 1)

        @block.vector
        def _(dve):
            step = Steps(dve, steps)

            def split_x(c):
                for k in range(KD):
                    dve.wait_ge(x_high, KD * c + k + 1)
                    cols = slice(c * CH, (c + 1) * CH)
                    dve.tensor_tensor(f.x[:, 1, k, cols], m.xn_t[:, k, cols], f.x[:, 0, k, cols].bitcast(F32),
                                      ALU.subtract).then_inc(x_low, 1)

            def split(n):
                c, i = divmod(n, ni)
                dve.wait_ge(high, n + 1)
                dve.tensor_tensor(f.h[:, 1, c % 2, i, :], f.inter[:, n % 3, :], f.h[:, 0, c % 2, i, :].bitcast(F32),
                                  ALU.subtract).then_inc(low, 1)

            def mean_squares(c):
                cols = slice(c * TC, (c + 1) * TC)
                dve.wait_ge(sumsq, c + 1)
                dve.tensor_scalar(ms[:, cols], sums(c), 1.0 / F1, RMS_EPS, ALU.mult, ALU.add).then_inc(ms_in, 1)
                dve.wait_ge(rms_done, c + 1)
                step(dve.reciprocal(inv[:, cols], root[:, cols]))

            def add(c):
                for j in range(TC):
                    t = c * TC + j
                    dve.wait_ge(downed, t // 2 + 1)
                    out = m.ps[:, 6 + j // 2, (j % 2) * D:(j % 2 + 1) * D]
                    if rms:
                        dve.scalar_tensor_tensor(sum_place(m, batch, t), out, inv[:, t:t + 1], m.acc[:, t, :],
                                                 ALU.mult, ALU.add).then_inc(added, 1)
                    else:
                        dve.tensor_tensor(sum_place(m, batch, t), out, m.acc[:, t, :], ALU.add).then_inc(added, 1)

            split_x(0)
            for n in range(units):
                dve.wait_ge(silued, n + 1)
                dve.wait_ge(upped, 2 * n + 2)
                if n >= 3:
                    dve.wait_ge(low, n - 2)
                    if rms and (n - 3) % 2 == 0:
                        dve.wait_ge(square_even, (n - 3) // 2 + 1)
                dve.tensor_tensor(f.inter[:, n % 3, :], f.gate[:, n % 2, :], m.ps[:, 2 * (n % 3) + 1, :],
                                  ALU.mult).then_inc(gated, 1)
                if rms and n % 2 == 1:
                    dve.wait_ge(gated, n + 1)
                    if n >= 3:
                        dve.wait_ge(summed, adds(n - 2))
                    inter = f.inter[:, n % 3, :]
                    dve.tensor_tensor(f.sq[:, 1, :], inter, inter, ALU.mult).then_inc(square_odd, 1)
                if n >= 1:
                    split(n - 1)
                if n == 1:
                    split_x(1)
                if rms and n == ni + 2:
                    mean_squares(0)
                if n == ni + 3:
                    add(0)
            split(units - 1)
            if rms:
                mean_squares(NC - 1)
            add(NC - 1)

        if rms:
            @block.gpsimd
            def _(pool):
                for n in range(units):
                    c, i = divmod(n, ni)
                    if n % 2 == 0:
                        pool.wait_ge(gated, n + 1)
                        if n >= 4 and i >= 2:
                            pool.wait_ge(summed, adds(n - 2))
                        inter = f.inter[:, n % 3, :]
                        pool.tensor_tensor(f.acc[:, c, :] if i == 0 else f.sq[:, 0, :], inter, inter,
                                           ALU.mult).then_inc(square_even, 1)
                        pool.wait_ge(square_even, n // 2 + 1)
                    else:
                        pool.wait_ge(square_odd, n // 2 + 1)
                    if i >= 1:
                        if i >= 2:
                            pool.wait_ge(summed, adds(n - 1))
                        pool.tensor_tensor(f.acc[:, c, :], f.acc[:, c, :], f.sq[:, n % 2, :], ALU.add).then_inc(summed, 1)



class Routing:

    SEMAPHORES = ("logits", "route_steps", "shifted", "exped")
    PARTS = 4

    def __init__(self, m, f, w_router, sems):
        self.m, self.f, self.w_router = m, f, w_router
        self.logits, self.steps, self.shifted, self.exped = sems

    def tensor(self, pe):
        m = self.m
        for t in range(NT):
            for k in range(KD):
                last = pe.matmul(m.ps[:, 1, t * E_RT:(t + 1) * E_RT], m.xn_t[:, k, t * P:(t + 1) * P],
                                 self.w_router[:, k, :], start=(k == 0), stop=(k == KD - 1))
        last.then_inc(self.logits, 1)

    def scalar(self, act):
        act.wait_ge(self.shifted, 1)
        act.activation(self.f.prob[:, :, :], self.f.prob[:, :, :], ACT.Exp).then_inc(self.exped, 1)

    def vector(self, dve, part):
        m, f = self.m, self.f
        mx = m.small[:, 0:NT]
        spread = lambda: mx.unsqueeze(2).broadcast_to([P, NT, E_RT])
        if part == 0:
            self.step = Steps(dve, self.steps)
            lg = m.ps[:, 1, 0:NT * E_RT].rearrange("p (t e) -> p t e", e=E_RT)
            dve.wait_ge(self.logits, 1)
            self.step(dve.reduce_max(mx, lg, AX.X))
            dve.tensor_tensor(f.prob[:, :, :], lg, spread(), ALU.subtract).then_inc(self.shifted, 1)
        step = self.step
        if part == 1:
            dve.wait_ge(self.exped, 1)
            step(dve.tensor_reduce(mx, f.prob[:, :, :], AX.X, ALU.add))
            step(dve.reciprocal(mx, mx))
            step(dve.tensor_tensor(f.prob[:, :, :], f.prob[:, :, :], spread(), ALU.mult))
            for t in range(NT):
                dve.max(f.top[:, t, :], f.prob[:, t, :]).then_inc(self.steps, 1)
            step.count += NT
        if part == 2:
            dve.wait_ge(self.steps, step.count)
            for t in range(NT):
                dve.max_index(f.idx[:, t, :], f.top[:, t, :], f.prob[:, t, :]).then_inc(self.steps, 1)
            step.count += NT
            dve.wait_ge(self.steps, step.count)
            step(dve.tensor_copy(f.idxf[:, :, :], f.idx[:, :, :]))
        if part == 3:
            for t in range(NT):
                for r, out in enumerate((f.gate_w, f.prob)):
                    dve.tensor_scalar(out[:, t, :], m.iota16[:, :], f.idxf[:, t, r:r + 1], f.top[:, t, r:r + 1],
                                      ALU.is_equal, ALU.mult).then_inc(self.steps, 1)
            step.count += 2 * NT
            dve.wait_ge(self.steps, step.count)
            step(dve.tensor_tensor(f.gate_w[:, :, :], f.gate_w[:, :, :], f.prob[:, :, :], ALU.add))


def experts(nc, m, f, a, w_router, wup, wdown, weights):
    ne = E_SH + E_RT
    units = NC * ne
    n_max = len(MaximumPass.SEMAPHORES)
    with stage(nc, "upped", "gelued", "downed", "added", *MaximumPass.SEMAPHORES, *Routing.SEMAPHORES) as \
            (block, upped, gelued, downed, added, *sems):
        mp = MaximumPass(m, a, sems[:n_max])
        routing = Routing(m, f, w_router, sems[n_max:])
        slots = KD + TC
        lightly = Routing.PARTS
        per_step = len(mp.items) / (units - lightly)
        up = 0.9 * per_step / KD
        mp.share_out([((n, i), up if i < KD else (per_step - KD * up) / TC, (4, 5, 6, 7))
                      for n in range(lightly, units) for i in range(slots)])

        def product(n, j):
            return m.ps[:, 2 + j // 2, (j % 2) * D:(j % 2 + 1) * D]

        @block.tensor
        def _(pe):
            def down(n, j):
                c, e = divmod(n, ne)
                if j == 0:
                    pe.wait_ge(gelued, n + 1)
                u = n * TC + j
                if j % 2 == 0 and n >= 1:
                    pe.wait_ge(added, u - TC + 2)
                last = pe.matmul(product(n, j), f.mid[:, n % 3, j * P:(j + 1) * P], wdown[:, e, :],
                                 start=True, stop=True)
                if j % 2 == 1:
                    last.then_inc(downed, 1)

            routing.tensor(pe)
            pe.wait_ge(*weights)
            for n in range(units + 1):
                if n < units:
                    c, e = divmod(n, ne)
                    if n == 1:
                        pe.wait_ge(routing.shifted, 1)
                    if n >= 2:
                        pe.wait_ge(gelued, n - 1)
                    for k in range(KD):
                        last = pe.matmul(m.ps[:, n % 2, :], wup[:, e, k, :], m.xn_t[:, k, c * CH:(c + 1) * CH],
                                         start=(k == 0), stop=(k == KD - 1))
                        if k == KD - 1:
                            last.then_inc(upped, 1)
                        mp.tensor_share(pe, (n, k))
                for j in range(TC):
                    mp.tensor_share(pe, (n, KD + j))
                    if n >= 1:
                        down(n - 1, j)

        @block.scalar
        def _(act):
            for n in range(units):
                act.wait_ge(upped, n + 1)
                if n >= 3:
                    act.wait_ge(downed, TC // 2 * (n - 2))
                act.activation(f.mid[:, n % 3, :], m.ps[:, n % 2, :], ACT.Gelu).then_inc(gelued, 1)
                if n == 0:
                    routing.scalar(act)

        @block.vector
        def _(dve):
            def add(n, j):
                c, e = divmod(n, ne)
                u = n * TC + j
                t = c * TC + j
                dve.wait_ge(downed, u // 2 + 1)
                if e >= 1:
                    dve.wait_ge(added, u - TC + 1)
                out = product(n, j)
                if e < E_SH:
                    dve.tensor_tensor(m.acc[:, t, :], out, m.acc[:, t, :], ALU.add).then_inc(added, 1)
                else:
                    dve.scalar_tensor_tensor(m.acc[:, t, :], out, f.gate_w[:, t, e - E_SH:e - E_SH + 1],
                                             m.acc[:, t, :], ALU.mult, ALU.add).then_inc(added, 1)

            mp.vector_start(dve)
            routing.vector(dve, 0)
            for n in range(units + 1):
                if 1 <= n < Routing.PARTS:
                    routing.vector(dve, n)
                for k in range(KD):
                    mp.vector_share(dve, (n, k))
                for j in range(TC):
                    mp.vector_share(dve, (n, KD + j))
                    if n >= 1:
                        add(n - 1, j)

        @block.sync
        def _(sp):
            mp.sync_rows(sp)



def spline_weights(nc, m, f, io, wg, wu, wd):
    nt = F1 // P
    with stage(nc, "windows_in", "basis_in_0", "basis_in_1", "formed", "steps", "turned", "stored", "split",
               pool=True) as \
            (block, windows_in, basis_in_0, basis_in_1, formed, steps, turned, stored, split):
        basis_in = (basis_in_0, basis_in_1)
        basis_gu = io.basis.rearrange("s (t p) n -> t p s n", p=P)
        basis_d = io.basis.rearrange("s (h p c) n -> h c p s n", p=P, c=4)
        tiles = [("gu", t) for t in range(nt)] + [("d", t) for t in range(nt)]
        units = []
        for n, (kind, t) in enumerate(tiles):
            if kind == "gu":
                for w, win in ((wg, f.win[:, 0, t, :]), (wu, f.win[:, 1, t, :])):
                    units.append((n, win, [part[:, :, t * P:(t + 1) * P] for part in w]))
            else:
                h, c = divmod(t, 4)
                units.append((n, f.win[:, 2, t, :], [part[:, 2 * c:2 * c + 2, h * P:(h + 1) * P] for part in wd]))

        @block.sync
        def _(sp):
            for i, win in enumerate((io.win_gate, io.win_up)):
                sp.dma_start(f.win[:, i, :, :], rows(win)).then_inc(windows_in, 16)
            for h in range(KD):
                sp.dma_start(f.win[:, 2, 4 * h:4 * h + 4, :],
                             io.win_down.rearrange("(h p c) s -> h p c s", p=P, c=4)[h]).then_inc(windows_in, 16)
            for n, (kind, t) in enumerate(tiles):
                if n >= 2:
                    last_use = max(i for i, u in enumerate(units) if u[0] == n - 2)
                    sp.wait_ge(formed, last_use + 1)
                src = basis_gu[t] if kind == "gu" else basis_d[t // 4][t % 4]
                sp.dma_start(f.basis[:, n % 2, :, :], src).then_inc(basis_in[n % 2], 16)

        @block.vector
        def _(dve):
            step = Steps(dve, steps)
            dve.wait_ge(windows_in, 64)
            for i, (n, win, out) in enumerate(units):
                dve.wait_ge(basis_in[n % 2], 16 * (n // 2 + 1))
                if i >= 2:
                    dve.wait_ge(turned, i - 1)
                w = f.w[:, i % 2, :]
                step(dve.tensor_scalar(w, f.basis[:, n % 2, 0, :], win[:, 0:1], None, ALU.mult))
                for s in range(1, NSEG):
                    ins = dve.scalar_tensor_tensor(w, f.basis[:, n % 2, s, :], win[:, s:s + 1], w, ALU.mult, ALU.add)
                    if s < NSEG - 1:
                        step(ins)
                ins.then_inc(formed, 1)

        @block.tensor
        def _(pe):
            for i in range(len(units)):
                pe.wait_ge(formed, i + 1)
                if i >= 2:
                    pe.wait_ge(stored, 2 * (i - 1))
                for k in range(KD):
                    last = pe.transpose(m.ps[:, i % 2, k * P:(k + 1) * P], f.w[:, i % 2, k * P:(k + 1) * P],
                                        m.ident[:, :])
                last.then_inc(turned, 1)

        @block.scalar
        def _(act):
            for i, (n, win, out) in enumerate(units):
                act.wait_ge(turned, i + 1)
                turned_w = m.ps[:, i % 2, 0:D].rearrange("p (k n) -> p k n", k=KD)
                if i >= 2:
                    act.wait_ge(split, i - 1)
                act.activation(out[0], turned_w, ACT.Copy).then_inc(stored, 1)
                act.activation(f.whole[:, i % 2, :, :], turned_w, ACT.Copy).then_inc(stored, 1)

        @block.gpsimd
        def _(pool):
            for i, (n, win, out) in enumerate(units):
                pool.wait_ge(stored, 2 * (i + 1))
                pool.tensor_tensor(out[1], f.whole[:, i % 2, :, :], out[0].bitcast(F32), ALU.subtract).then_inc(split, 1)


def lambda_scalar(nc, m, f, io):
    n = 2 * HD
    with stage(nc, "lam_in", "steps", "dots", "exped") as (block, lam_in, steps, dots, exped):
        @block.sync
        def _(sp):
            for i, src in enumerate((io.lq1, io.lk1, io.lq2, io.lk2)):
                sp.dma_start(f.lqk[:, i, :], src.partition_broadcast(P)).then_inc(lam_in, 16)

        @block.vector
        def _(dve):
            step = Steps(dve, steps)
            dve.wait_ge(lam_in, 64)
            pair = f.lqk[:, :, :].rearrange("p (a b) n -> p a b n", b=2)
            step(dve.tensor_tensor(f.dot[:, :, :], pair[:, :, 0, :], pair[:, :, 1, :], ALU.mult))
            dve.tensor_reduce(m.small[:, 0:2], f.dot[:, :, :], AX.X, ALU.add).then_inc(dots, 1)
            dve.wait_ge(exped, 1)
            step(dve.tensor_tensor(m.lam[:, :], m.small[:, 2:3], m.small[:, 3:4], ALU.subtract))
            dve.tensor_scalar(m.lam[:, :], m.lam[:, :], LAMBDA_INIT, None, ALU.add)

        @block.scalar
        def _(act):
            act.wait_ge(dots, 1)
            act.activation(m.small[:, 2:4], m.small[:, 0:2], ACT.Exp).then_inc(exped, 1)



def ternary_weights(nc, m, f, wgu, wp):
    ngu, npj = 2 * F1 // P, D // P
    n_gu, n_p = ngu * D // GROUP, npj * F1 // GROUP
    ng = n_gu + n_p
    with stage(nc, "steps", "ready", "turned", "stored") as (block, steps, ready, turned, stored):
        @block.vector
        def _(dve):
            step = Steps(dve, steps)
            g3 = lambda ap: ap.rearrange("p (g n) -> p g n", n=GROUP)
            bc = lambda s: s.unsqueeze(2).broadcast_to([P, ng, GROUP])
            step(dve.tensor_copy(f.wb[:, :], f.raw[:, :]))
            step(dve.tensor_reduce(f.thr[:, :], g3(f.wb[:, :]), AX.X, ALU.add, apply_absolute_value=True))
            step(dve.tensor_scalar(f.sc[:, :], f.thr[:, :], 1.0 / GROUP, None, ALU.mult))
            step(dve.tensor_scalar(f.sc[:, :], f.sc[:, :], 1e-8, None, ALU.max))
            step(dve.tensor_scalar(f.thr[:, :], f.sc[:, :], 257.0 / 512.0, None, ALU.mult))
            step(dve.tensor_tensor(g3(f.q1[:, :]), g3(f.wb[:, :]), bc(f.thr[:, :]), ALU.is_gt))
            step(dve.tensor_scalar(f.thr[:, :], f.thr[:, :], -1.0, None, ALU.mult))
            step(dve.tensor_tensor(g3(f.q2[:, :]), g3(f.wb[:, :]), bc(f.thr[:, :]), ALU.is_lt))
            step(dve.tensor_tensor(f.q1[:, :], f.q1[:, :], f.q2[:, :], ALU.subtract))
            step(dve.tensor_tensor(g3(f.q1[:, :]), g3(f.q1[:, :]), bc(f.sc[:, :]), ALU.mult))
            step(dve.tensor_tensor(f.q1[:, :], f.q1[:, :], f.wb[:, :], ALU.subtract))
            dve.tensor_tensor(f.q1[:, :], f.q1[:, :], f.wb[:, :], ALU.add).then_inc(ready, 1)

        turns = [f.q1[:, (2 * t + k) * P:(2 * t + k + 1) * P] for k in range(KD) for t in range(ngu)]
        outs = [wgu[:, k, t * P:(t + 4) * P].rearrange("p (i n) -> p i n", n=P)
                for k in range(KD) for t in range(0, ngu, 4)]
        turns += [f.q1[:, n_gu * GROUP + h * F1 + j * P:n_gu * GROUP + h * F1 + (j + 1) * P]
                  for h in range(npj) for j in range(F1 // P)]
        outs += [wp[:, j:j + 4, h * P:(h + 1) * P] for h in range(npj) for j in range(0, F1 // P, 4)]

        @block.tensor
        def _(pe):
            pe.wait_ge(ready, 1)
            for u in range(len(turns) // 4):
                if u >= 4:
                    pe.wait_ge(stored, u - 3)
                for i in range(4):
                    last = pe.transpose(m.ps[:, u % 4, :].bitcast(BF16)[:, i * P:(i + 1) * P], turns[4 * u + i],
                                        m.ident_b[:, :])
                last.then_inc(turned, 1)

        @block.scalar
        def _(act):
            for u in range(len(turns) // 4):
                act.wait_ge(turned, u + 1)
                act.activation(outs[u], m.ps[:, u % 4, :].bitcast(BF16)[:, 0:4 * P].rearrange("p (i n) -> p i n", n=P),
                               ACT.Copy).then_inc(stored, 1)


def time_mix_scalars(nc, m, w, weights):
    with stage(nc, "steps") as (block, steps):
        @block.vector
        def _(dve):
            dve.wait_ge(*weights)
            dve.tensor_scalar(w.omix[:, :, :], w.mix[:, :, :], -1.0, 1.0, ALU.mult, ALU.add)

        @block.scalar
        def _(act):
            act.wait_ge(*weights)
            act.activation(w.decay[:, :], w.td[:, :], ACT.Exp).then_inc(steps, 1)
            act.wait_ge(steps, 1)
            act.activation(w.decay[:, :], w.decay[:, :], ACT.Exp, scale=-1.0)
            act.activation(w.bonus[:, :], w.tf[:, :], ACT.Exp)


def mixed_with_last(dve, step, out, h_t, mix, omix, j):
    for k in range(KD):
        step(dve.tensor_scalar(out[:, k, :], h_t[:, k, 0:S], omix[:, j, k:k + 1], None, ALU.mult))
        ins = dve.scalar_tensor_tensor(out[:, k, :], h_t[:, k, 1:S + 1], mix[:, j, k:k + 1], out[:, k, :],
                                       ALU.mult, ALU.add)
        if k == 0:
            step(ins)
    return ins


def time_mix(nc, m, f, w):
    order = (("k", w.wk, 1), ("v", w.wv, 2), ("r", w.wr, 0))
    with stage(nc, "mixed", "steps", "proj", "k_kept", "kv_made", "r_kept", "wkv", "outed", "added", "summed") as \
            (block, mixed, steps, proj, k_kept, kv_made, r_kept, wkv, outed, added, summed):
        @block.tensor
        def _(pe):
            for n, (name, wt, j) in enumerate(order):
                pe.wait_ge(mixed, n + 1)
                for o in range(KD):
                    for c in range(NC):
                        u = 4 * n + 2 * o + c
                        if u >= 8:
                            pe.wait_ge(k_kept, u - 8 + 1)
                        for k in range(KD):
                            last = pe.matmul(m.ps[:, u % 8, :], wt[:, k, o * P:(o + 1) * P],
                                             f.mix[:, j, k, c * CH:(c + 1) * CH], start=(k == 0), stop=(k == KD - 1))
                        last.then_inc(proj, 1)
            for t in range(NT):
                pe.wait_ge(wkv, KD)
                if t < 4:
                    pe.wait_ge(kv_made, 4)
                else:
                    pe.wait_ge(summed, t - 3)
                for k in range(KD):
                    last = pe.matmul(m.ps[:, 4 + t % 4, 0:D], f.st[:, k, t * P:(t + 1) * P], w.wo[:, k, :],
                                     start=(k == 0), stop=(k == KD - 1))
                last.then_inc(outed, 1)

        @block.scalar
        def _(act):
            for u in range(4):
                act.wait_ge(proj, u + 1)
                act.activation(f.kk[:, u // 2, (u % 2) * CH:(u % 2 + 1) * CH], m.ps[:, u, :], ACT.Copy).then_inc(k_kept, 1)
            for u in range(4):
                act.wait_ge(proj, 8 + u + 1)
                act.activation(f.rs[:, u // 2, (u % 2) * CH:(u % 2 + 1) * CH], m.ps[:, u, :],
                               ACT.Sigmoid).then_inc(r_kept, 1)

        @block.vector
        def _(dve):
            step = Steps(dve, steps)
            for name, wt, j in order:
                mixed_with_last(dve, step, f.mix[:, j, :, :], f.h_t, w.mix, w.omix, j).then_inc(mixed, 1)
            for u in range(4):
                dve.wait_ge(proj, 4 + u + 1)
                dve.wait_ge(k_kept, u + 1)
                part = f.kk[:, u // 2, (u % 2) * CH:(u % 2 + 1) * CH]
                dve.tensor_tensor(part, part, m.ps[:, 4 + u, :], ALU.mult).then_inc(kv_made, 1)
            dve.wait_ge(kv_made, 4)
            for k in range(KD):
                step(dve.tensor_tensor_scan(f.st[:, k, :], w.decay[:, k:k + 1].broadcast_to([P, S]), f.kk[:, k, :],
                                            0.0, ALU.mult, ALU.add))
                step(dve.scalar_tensor_tensor(f.st[:, k, 0:1], f.kk[:, k, 0:1], w.bonus[:, k:k + 1], f.st[:, k, 0:1],
                                              ALU.mult, ALU.add))
                dve.wait_ge(r_kept, 2 * (k + 1))
                dve.tensor_tensor(f.st[:, k, :], f.st[:, k, :], f.rs[:, k, :], ALU.mult).then_inc(wkv, 1)
            for t in range(NT):
                dve.wait_ge(outed, t + 1)
                dve.tensor_tensor(f.xn[:, t, :], f.xn[:, t, :], m.ps[:, 4 + t % 4, 0:D], ALU.add).then_inc(summed, 1)
                dve.wait_ge(summed, t + 1)
                dve.tensor_tensor(m.acc[:, t, :], m.acc[:, t, :], f.xn[:, t, :], ALU.add)


def channel_mix(nc, m, f, w):
    nf = F2 // P
    with stage(nc, "mixed", "steps", "upped", "squared", "gate_in", "gated", "downed", "scaled", "added") as \
            (block, mixed, steps, upped, squared, gate_in, gated, downed, scaled, added):
        @block.tensor
        def _(pe):
            def down(c):
                for j in range(TC):
                    t = c * TC + j
                    if t >= 2:
                        pe.wait_ge(gated, t - 1)
                    for k in range(KD):
                        last = pe.matmul(m.ps[:, 4 + t % 2, 0:D], f.mix[:, 0, k, t * P:(t + 1) * P], w.wcr[:, k, :],
                                         start=(k == 0), stop=(k == KD - 1))
                    last.then_inc(gate_in, 1)
                    pe.wait_ge(squared, nf * (c + 1))
                    if t >= 2:
                        pe.wait_ge(scaled, t - 1)
                    for i in range(nf):
                        last = pe.matmul(m.ps[:, 6 + t % 2, 0:D], f.kc[:, c, i, j * P:(j + 1) * P], w.wcv[:, i, :],
                                         start=(i == 0), stop=(i == nf - 1))
                    last.then_inc(downed, 1)

            pe.wait_ge(mixed, 1)
            for c in range(NC):
                for i in range(nf):
                    n = c * nf + i
                    if n >= 4:
                        pe.wait_ge(squared, n - 3)
                    for k in range(KD):
                        last = pe.matmul(m.ps[:, n % 4, :], w.wck[:, k, i * P:(i + 1) * P],
                                         f.mix[:, 0, k, c * CH:(c + 1) * CH], start=(k == 0), stop=(k == KD - 1))
                    last.then_inc(upped, 1)
            for c in range(NC):
                down(c)

        @block.scalar
        def _(act):
            for n in range(NC * nf):
                act.wait_ge(upped, n + 1)
                act.activation(f.kc[:, n // nf, n % nf, :], m.ps[:, n % 4, :], ACT.Square).then_inc(squared, 1)
            for t in range(NT):
                act.wait_ge(gate_in, t + 1)
                if t >= 2:
                    act.wait_ge(scaled, t - 1)
                act.activation(f.sg[:, t % 2, :], m.ps[:, 4 + t % 2, 0:D], ACT.Sigmoid).then_inc(gated, 1)

        @block.vector
        def _(dve):
            step = Steps(dve, steps)
            mixed_with_last(dve, step, f.mix[:, 0, :, :], f.h_t, w.mix, w.omix, 3).then_inc(mixed, 1)
            for t in range(NT):
                dve.wait_ge(gated, t + 1)
                dve.wait_ge(downed, t + 1)
                if t >= 1:
                    dve.wait_ge(added, t)
                dve.tensor_tensor(f.tmp[:, :], f.sg[:, t % 2, :], m.ps[:, 6 + t % 2, 0:D], ALU.mult).then_inc(scaled, 1)
                dve.wait_ge(scaled, t + 1)
                dve.tensor_tensor(m.acc[:, t, :], m.acc[:, t, :], f.tmp[:, :], ALU.add).then_inc(added, 1)



def route_pairs(nc, m, f, w_gate):
    with stage(nc, "logits", "kept", "steps", "maxes", "maxes_all", "shifted", "exped", "sums", "sums_all",
               "spread", "turned", pool=True) as \
            (block, logits, kept, steps, maxes, maxes_all, shifted, exped, sums, sums_all, spread, turned):
        tw = f.tw[:, :, :]
        by_slot = tw.rearrange("p t r -> p r t")

        @block.tensor
        def _(pe):
            for t in range(NT):
                for k in range(KD):
                    last = pe.matmul(m.ps[:, 7, t * E3:(t + 1) * E3], m.xn_t[:, k, t * P:(t + 1) * P],
                                     w_gate[:, k, :], start=(k == 0), stop=(k == KD - 1))
            last.then_inc(logits, 1)
            n = 0
            for r in range(2):
                for kind, src in enumerate((f.ohx, f.wx)):
                    for t in range(NT):
                        n += 1
                        pe.wait_ge(spread, n)
                        last = pe.transpose(m.ps[:, 4 * r + 2 * kind + t // TC, (t % TC) * P:(t % TC + 1) * P],
                                            src[:, r, t, :], m.ident[:, :])
                        if t % TC == TC - 1:
                            last.then_inc(turned, 1)

        @block.scalar
        def _(act):
            act.wait_ge(shifted, 1)
            act.activation(tw, tw, ACT.Exp).then_inc(exped, 1)
            for n in range(8):
                r, kind, c = n // 4, n // 2 % 2, n % 2
                act.wait_ge(turned, n + 1)
                dst = (f.oh, f.wb)[kind]
                act.activation(dst[:, r, c * CH:(c + 1) * CH], m.ps[:, n, :], ACT.Copy)

        @block.gpsimd
        def _(pool):
            pool.wait_ge(maxes, 1)
            pool.partition_all_reduce(f.red_all[:, 0:2], f.red[:, 0:2], P, RMAX).then_inc(maxes_all, 1)
            pool.wait_ge(sums, 1)
            pool.partition_all_reduce(f.red_all[:, 2:4], f.red[:, 2:4], P, RADD).then_inc(sums_all, 1)

        @block.vector
        def _(dve):
            step = Steps(dve, steps)
            dve.wait_ge(logits, 1)
            step(dve.tensor_copy(f.lg[:, :, :], m.ps[:, 7, 0:NT * E3].rearrange("p (t e) -> p t e", e=E3)))
            for t in range(NT):
                dve.max(f.top[:, t, :], f.lg[:, t, :]).then_inc(steps, 1)
            step.count += NT
            dve.wait_ge(steps, step.count)
            for t in range(NT):
                dve.max_index(f.idx[:, t, :], f.top[:, t, :], f.lg[:, t, :]).then_inc(steps, 1)
            dve.tensor_reduce(f.red[:, 0:2], f.top[:, :, 0:2].rearrange("p t r -> p r t"), AX.X,
                              ALU.max).then_inc(maxes, 1)
            step.count += NT
            dve.wait_ge(steps, step.count)
            step(dve.tensor_copy(f.idxf[:, :, :], f.idx[:, :, :]))
            dve.wait_ge(maxes_all, 1)
            dve.tensor_tensor(tw, f.top[:, :, 0:2], f.red_all[:, 0:2].unsqueeze(1).broadcast_to([P, NT, 2]),
                              ALU.subtract).then_inc(shifted, 1)
            dve.wait_ge(exped, 1)
            dve.tensor_reduce(f.red[:, 2:4], by_slot, AX.X, ALU.add).then_inc(sums, 1)
            dve.wait_ge(sums_all, 1)
            step(dve.reciprocal(f.red[:, 0:2], f.red_all[:, 2:4]))
            step(dve.tensor_tensor(tw, tw, f.red[:, 0:2].unsqueeze(1).broadcast_to([P, NT, 2]), ALU.mult))
            for r in range(2):
                for t in range(NT):
                    dve.tensor_scalar(f.ohx[:, r, t, :], m.iota_x[:, :], f.idxf[:, t, r:r + 1], 2.0,
                                      ALU.is_equal, ALU.mult).then_inc(spread, 1)
                for t in range(NT):
                    dve.tensor_copy(f.wx[:, r, t, :], f.tw[:, t, r:r + 1].broadcast_to([P, P])).then_inc(spread, 1)


def lora_experts(nc, m, f, w, a, batch, weights):
    with stage(nc, "low_in", "low_read", "low_made", "firsts", "seconds", "silued", "gated", "weighted", "mixed",
               "lowered", "masked", "u_made", "downed", "added", *MaximumPass.SEMAPHORES, pool=True) as \
            (block, low_in, low_read, low_made, firsts, seconds, silued, gated, weighted, mixed,
             lowered, masked, u_made, downed, added, *max_sems):
        units = NC * M3
        slots = []
        for n in range(units):
            up = [("first", n, i) for i in range(2 * (KD + 1))]
            rest = [("second", n, j) for j in range(2) if n >= 1] + [("lower", n)] * (n >= 2)
            slots += rest + up if n == M3 else up + rest
            if n == M3 + 2:
                slots += [("down", 0, j, i) for j in range(TC) for i in range(3)]
        slots += [("down", 1, j, i) for j in range(TC - 1) for i in range(3)]
        mp = MaximumPass(m, a, max_sems)
        fixed = {"down": 1, "second": 1.5, "lower": 0}
        left = len(mp.items) - sum(fixed.get(key[0], 0) for key in slots)
        rate = left / sum(key[0] == "first" for key in slots)
        mp.share_out([(key, fixed.get(key[0], rate), (7,) if key[0] == "down" else (6, 7)) for key in slots])

        def item_count(key):
            return mp.share[key].stop

        @block.tensor
        def _(pe):
            def low(c):
                if c >= 1:
                    pe.wait_ge(mp.block_out, item_count(("lower", M3)))
                for j in range(2):
                    if j == 1:
                        pe.wait_ge(low_read, 2 * c + 1)
                    for k in range(KD):
                        last = pe.matmul(m.ps[:, 6, :], w.a[:, k, j * P:(j + 1) * P],
                                         m.xn_t[:, k, c * CH:(c + 1) * CH], start=(k == 0), stop=(k == KD - 1))
                    last.then_inc(low_in, 1)

            def first(n):
                c, i = divmod(n, M3)
                if n >= 2:
                    pe.wait_ge(gated, 2 * (n - 1))
                if i == 0:
                    pe.wait_ge(low_made, 2 * (c + 1))
                for j, wt in enumerate((w.up, w.gate)):
                    for k in range(KD):
                        pe.matmul(m.ps[:, 2 * (n % 2) + j, :], wt[:, k, i * P:(i + 1) * P],
                                  m.xn_t[:, k, c * CH:(c + 1) * CH], start=(k == 0), stop=False)
                        mp.tensor_share(pe, ("first", n, 3 * j + k))
                    pe.matmul(m.ps[:, 2 * (n % 2) + j, :], w.b[:, j, i * P:(i + 1) * P],
                              f.m0[:, j, :], start=False, stop=True).then_inc(firsts, 1)
                    mp.tensor_share(pe, ("first", n, 3 * j + KD))

            def second(n):
                pe.wait_ge(gated, 2 * n + 1)
                for j in range(2):
                    i = n % M3
                    pe.matmul(m.ps[:, 2 * (n % 2) + j, :], w.b[:, j, i * P:(i + 1) * P], f.md[:, j, :],
                              start=False, stop=True, skip_group_check=True).then_inc(seconds, 1)
                    mp.tensor_share(pe, ("second", n + 1, j))

            def lower(n):
                c, i = divmod(n, M3)
                pe.wait_ge(weighted, 2 * (n + 1))
                if i == 0 and c >= 1:
                    pe.wait_ge(masked, 2 * c)
                for r in range(2):
                    last = pe.matmul(m.ps[:, 4 + r, :], w.da[:, i, :], f.h[:, r, n % 2, :],
                                     start=(i == 0), stop=(i == M3 - 1))
                    if r == 0:
                        mp.tensor_share(pe, ("lower", n + 2))
                last.then_inc(lowered, 1)

            def down(c):
                pe.wait_ge(mixed, M3 * (c + 1))
                pe.wait_ge(u_made, c + 1)
                pe.wait_ge(mp.block_out, item_count(("lower", M3 + 2 if c == 0 else units - 1)))
                for j in range(TC):
                    t = c * TC + j
                    if j % 2 == 0 and j >= 2:
                        pe.wait_ge(added, t)
                    out = m.ps[:, 6, (j % 2) * D:(j % 2 + 1) * D]
                    for i in range(M3):
                        pe.matmul(out, f.mixed[:, (c * M3 + i) % MIXED, j * P:(j + 1) * P], w.down[:, i, :],
                                  start=(i == 0), stop=False)
                        if i % 2 == 1:
                            mp.tensor_share(pe, ("down", c, j, i // 2))
                    last = pe.matmul(out, f.u[:, j * P:(j + 1) * P], w.db[:, :], start=False, stop=True)
                    if j % 2 == 1:
                        last.then_inc(downed, 1)
                if c + 1 < NC:
                    pe.wait_ge(added, TC * (c + 1))

            pe.wait_ge(*weights)
            low(0)
            for n in range(units):
                if n == M3:
                    second(n - 1)
                    lower(n - 2)
                    low(1)
                    first(n)
                else:
                    first(n)
                    if n >= 1:
                        second(n - 1)
                    if n >= 2:
                        lower(n - 2)
                if n == M3 + 2:
                    down(0)
            second(units - 1)
            lower(units - 2)
            lower(units - 1)
            down(1)

        @block.scalar
        def _(act):
            def silu(n, r):
                act.wait_ge((firsts, seconds)[r], 2 * n + 1)
                if n >= 1:
                    act.wait_ge(gated, 2 * (n - 1) + r + 1)
                act.activation(f.s[:, r, :], m.ps[:, 2 * (n % 2), :], ACT.Silu).then_inc(silued, 1)

            for n in range(units):
                silu(n, 0)
                silu(n, 1)

        @block.vector
        def _(dve):
            def low(c):
                cols = slice(c * CH, (c + 1) * CH)
                if c >= 1:
                    dve.wait_ge(seconds, 2 * M3 * c)
                for j in range(2):
                    dve.wait_ge(low_in, 2 * c + j + 1)
                    mp.step(dve, dve.tensor_tensor(f.m0[:, j, :], f.oh[:, 0, cols], m.ps[:, 6, :], ALU.mult))
                    dve.tensor_tensor(f.md[:, j, :], f.oh[:, 1, cols], m.ps[:, 6, :], ALU.mult).then_inc(low_read, 1)
                    dve.wait_ge(low_read, 2 * c + j + 1)
                    dve.tensor_tensor(f.md[:, j, :], f.md[:, j, :], f.m0[:, j, :], ALU.subtract).then_inc(low_made, 1)

            def gate(n, r):
                dve.wait_ge(silued, 2 * n + r + 1)
                dve.wait_ge((firsts, seconds)[r], 2 * n + 2)
                if n >= 2:
                    dve.wait_ge(lowered, n - 1)
                    dve.wait_ge(mixed, n - 1)
                dve.tensor_tensor(f.h[:, r, n % 2, :], f.s[:, r, :], m.ps[:, 2 * (n % 2) + 1, :],
                                  ALU.mult).then_inc(gated, 1)

            def lowrank(c):
                cols = slice(c * CH, (c + 1) * CH)
                dve.wait_ge(lowered, M3 * (c + 1))
                if c >= 1:
                    dve.wait_ge(downed, TC // 2 * c)
                dve.tensor_tensor(f.u[:, :], f.oh[:, 0, cols], m.ps[:, 4, :], ALU.mult).then_inc(masked, 1)
                dve.tensor_tensor(f.uu[:, :], f.oh[:, 1, cols], m.ps[:, 5, :], ALU.mult).then_inc(masked, 1)
                dve.wait_ge(masked, 2 * (c + 1))
                dve.tensor_tensor(f.u[:, :], f.u[:, :], f.uu[:, :], ALU.add).then_inc(u_made, 1)

            def add(c):
                for j in range(TC):
                    t = c * TC + j
                    for i in range(3):
                        mp.vector_share(dve, ("down", c, j, i))
                    if j % 2 == 1:
                        dve.wait_ge(downed, t // 2 + 1)
                        for u in (t - 1, t):
                            dve.tensor_tensor(sum_place(m, batch, u), sum_place(m, batch, u),
                                              m.ps[:, 6, (u % 2) * D:(u % 2 + 1) * D], ALU.add).then_inc(added, 1)

            def up_share(n):
                for i in range(2 * (KD + 1)):
                    mp.vector_share(dve, ("first", n, i))

            def second_share(n):
                for j in range(2):
                    mp.vector_share(dve, ("second", n, j))

            mp.vector_start(dve)
            low(0)
            for n in range(units):
                if n == M3:
                    second_share(n)
                    gate(n - 1, 1)
                    mp.vector_share(dve, ("lower", n))
                    low(1)
                    up_share(n)
                    gate(n, 0)
                else:
                    up_share(n)
                    second_share(n)
                    if n >= 1:
                        gate(n - 1, 1)
                    gate(n, 0)
                    mp.vector_share(dve, ("lower", n))
                if n == M3 + 1:
                    lowrank(0)
                if n == M3 + 2:
                    add(0)
            gate(units - 1, 1)
            lowrank(1)
            add(1)

        @block.gpsimd
        def _(pool):
            for n in range(units):
                c, i = divmod(n, M3)
                for r in range(2):
                    pool.wait_ge(gated, 2 * n + r + 1)
                    pool.tensor_tensor(f.h[:, r, n % 2, :], f.h[:, r, n % 2, :], f.wb[:, r, c * CH:(c + 1) * CH],
                                       ALU.mult).then_inc(weighted, 1)
                pool.wait_ge(weighted, 2 * (n + 1))
                if n >= MIXED:
                    pool.wait_ge(downed, TC // 2)
                pool.tensor_tensor(f.mixed[:, n % MIXED, :], f.h[:, 0, n % 2, :], f.h[:, 1, n % 2, :],
                                   ALU.add).then_inc(mixed, 1)

        @block.sync
        def _(sp):
            mp.sync_rows(sp)



def program(nc, io, out):
    with ExitStack() as ctx:
        def sb(name, shape, dt=F32):
            return ctx.enter_context(nc.sbuf_tensor(name, shape, dt))

        m = Memory()
        m.ps = ctx.enter_context(nc.psum_tensor("ps", [P, 8, CH], F32))
        m.x = sb("x_all", [P, B * NT, D])
        m.ident = sb("ident", [P, P])
        m.ident_h = sb("ident_h", [P, P], F16)
        m.ident_b = sb("ident_b", [P, P], BF16)
        m.mask_qk = sb("mask_qk", [P, P], BF16)
        m.mask_kq = sb("mask_kq", [P, P], BF16)
        m.ones_col = sb("ones_col", [P, 1])
        m.iota16 = sb("iota16", [P, E_RT])
        m.iota_x = sb("iota_x", [P, P])
        m.cos = sb("cos", [P, 2, NT, HD])
        m.sin = sb("sin", [P, 2, NT, HD])
        m.small = sb("small", [P, 8 * NM])
        m.norm = sb("norm", [P, 2, 11 * NT])
        m.lam = sb("lam", [P, 1])

        setup_constants(nc, m, io)
        late_in = ctx.enter_context(nc.semaphore("late_in"))
        out_stored = ctx.enter_context(nc.semaphore("out_stored"))
        late_done = 0

        @contextmanager
        def place(name, words, dt=F32):
            with nc.sbuf_tensor(name, [P, words], dt) as tensor:
                yield tensor

        def start(arena):
            ar = Arena(arena)
            m.acc = ar.take(NT, D)
            m.xn_t = ar.take(KD, S)
            return ar

        with place("arena0", ARENA) as arena:
            ar = start(arena)
            wqkv = ar.take(KD, 3 * D)
            bqkv = ar.take(3 * D)
            wup = ar.take(E_SH + E_RT, KD, F0)
            wdown = ar.take(E_SH + E_RT, D)
            wroute = ar.take(KD, E_RT)
            early = [(wqkv, rows(io.w_qkv0)), (bqkv, io.b_qkv0.partition_broadcast(P)), (wroute, rows(io.w_router0))]
            late = [*[(wup[:, :, k, :], io.w_up0[:, k * P:(k + 1) * P, :].rearrange("e p n -> p e n"))
                      for k in range(KD)],
                    (wdown, io.w_down0.rearrange("e p n -> p e n")),
                    *[(m.x[:, i * NT:(i + 1) * NT, :], rows(io.x[i])) for i in range(1, B)]]
            load_weights(nc, early, late, late_in)
            late_done += 16 * len(late)
            base = ar.at
            a = attention_memory(m, ar, NM, HD, NM // 4, 8)
            f = Memory()
            ar = Arena(arena, a.free)
            f.prob = ar.take(NT, E_RT)
            f.gate_w = ar.take(NT, E_RT)
            f.top = ar.take(NT, 8)
            f.idx = ar.take(NT, 8, dtype=U32)
            f.idxf = ar.take(NT, 8)
            f.mid = ar.take(3, CH)
            with nc.Fori(0, B) as b:
                attention_operands(nc, m, a, m.acc, b, None, wqkv, bqkv, 0, False, NM, HD)
                experts(nc, m, f, a, wroute, wup, wdown, (late_in, late_done))
                attention(nc, m, a, 4, 32)
                attention_finish(nc, m, a, 4, 32, None, 1.0, b)

        fixed, split = 2 * NT * D + 3 * KD * D + KD * D + 4 * NM * HD, 6 * KD * F1
        rest = ARENA - fixed - split
        with place("arena1", fixed) as arena, place("weight_parts1", split, F32R) as parts:
            ar = start(arena)
            wqkv = ar.take(KD, 3 * D)
            wo = ar.take(KD, D)
            turn = (ar.take(2 * NM * HD), ar.take(2 * NM * HD))
            ar = Arena(parts)
            wg = [ar.take(KD, F1, dtype=F32R) for _ in range(2)]
            wu = [ar.take(KD, F1, dtype=F32R) for _ in range(2)]
            wd = [ar.take(F1 // P, D, dtype=F32R) for _ in range(2)]
            load_weights(nc, [(wqkv[:, :, j * D:(j + 1) * D], rows(w)) for j, w in
                              enumerate((io.wq1, io.wk1, io.wv1))] + [(wo, rows(io.wo1)),
                              (turn[0], io.cos1.partition_broadcast(P)), (turn[1], io.sin1.partition_broadcast(P))])
            with place("making1", rest) as making:
                f = Memory()
                ar = Arena(making)
                f.win = ar.take(3, F1 // P, NSEG)
                f.basis = ar.take(2, NSEG, D)
                f.w = ar.take(2, D)
                f.whole = ar.take(2, KD, P)
                f.lqk = ar.take(4, 2 * HD)
                f.dot = ar.take(2, 2 * HD)
                spline_weights(nc, m, f, io, wg, wu, wd)
                lambda_scalar(nc, m, f, io)
            with nc.Fori(0, B) as b:
                with place("attention1", rest) as data:
                    a = attention_memory(m, Arena(data), NM // 2, 2 * HD, NM // 2, 6)
                    attention_operands(nc, m, a, m.acc, b, None, wqkv, None, turn, True, NM // 2, 2 * HD)
                    attention(nc, m, a, 2, 64)
                    attention_finish(nc, m, a, 2, 64, wo, 1.0 - LAMBDA_INIT)
                with place("ffn1", rest - FFN_PARTS) as data, place("ffn_parts1", FFN_PARTS, F32R) as parts:
                    gated_ffn(nc, m, gated_memory(data, parts), wg, wu, wd, False, b)

        fixed, split = 12000, 3 * KD * F1
        rest = ARENA - fixed - split
        with place("arena2", fixed) as arena, place("weights2", split, F32R) as parts:
            ar = start(arena)
            w = Memory()
            w.wr, w.wk, w.wv, w.wo, w.wcr = (ar.take(KD, D) for _ in range(5))
            w.wck = ar.take(KD, F2)
            w.wcv = ar.take(F2 // P, D)
            w.mix = ar.take(4, KD)
            w.omix = ar.take(4, KD)
            w.td, w.tf, w.decay, w.bonus, w.n1w, w.n1b, w.n2w, w.n2b = (ar.take(KD) for _ in range(8))
            ar = Arena(parts)
            wgu = ar.take(KD, 2 * F1, dtype=F32R)
            wp = ar.take(F1 // P, D, dtype=F32R)

            late = [(w.wr, rows(io.wr2)), (w.wk, rows(io.wk2)), (w.wv, rows(io.wv2)), (w.wo, rows(io.wo2)),
                    (w.wcr, rows(io.wcr2)), (w.wck, rows(io.wck2)), (w.wcv, rows(io.wcv2)),
                    *[(w.mix[:, j, :], v) for j, v in
                      enumerate((io.mix_r, io.mix_k, io.mix_v, io.mix_c))],
                    (w.td, io.td), (w.tf, io.tf), (w.n1w, io.n1w),
                    (w.n1b, io.n1b), (w.n2w, io.n2w), (w.n2b, io.n2b)]
            with place("making2", rest) as making:
                n_gu, n_p = 2 * F1 * D // P, D * F1 // P
                ng = (n_gu + n_p) // GROUP
                f = Memory()
                ar = Arena(making)
                f.raw = ar.take(ng * GROUP)
                f.wb = ar.take(ng * GROUP, dtype=BF16)
                f.q1 = ar.take(ng * GROUP, dtype=BF16)
                f.q2 = ar.take(ng * GROUP, dtype=BF16)
                f.thr = ar.take(ng)
                f.sc = ar.take(ng, dtype=BF16)
                early = [(f.raw[:, 0:n_gu].rearrange("p (t n) -> p t n", n=D), rows(io.w_gate_up)),
                         (f.raw[:, n_gu:n_gu + n_p].rearrange("p (t n) -> p t n", n=F1), rows(io.w_proj))]
                load_weights(nc, early, late, late_in)
                late_done += 16 * len(late)
                ternary_weights(nc, m, f, wgu, wp)
            time_mix_scalars(nc, m, w, (late_in, late_done))
            with nc.Fori(0, B) as b:
                with place("mixes2", rest) as data:
                    f = Memory()
                    ar = Arena(data)
                    f.xn = ar.take(NT, D)
                    f.n = ar.take(NT, D)
                    f.h_t = ar.take(KD, S + 1)
                    f.mix = ar.take(3, KD, S)
                    f.rs = ar.take(KD, S)
                    f.kk = ar.take(KD, S)
                    f.st = ar.take(KD, S)
                    f.kc = Arena(data, 2 * NT * D + KD * (S + 1) + KD * S).take(NC, F2 // P, CH)
                    f.sg = Arena(data).take(2, D)
                    f.tmp = Arena(data, 2 * D).take(D)
                    normalise_twice(nc, m, f, b, w.n1w, w.n1b)
                    time_mix(nc, m, f, w)
                    normalise(nc, m, f.xn, f.n, f.h_t[:, :, 1:S + 1], scale_w=w.n2w, scale_b=w.n2b)
                    channel_mix(nc, m, f, w)
                with place("ffn2", rest - FFN_PARTS) as data, place("ffn_parts2", FFN_PARTS, F32R) as parts:
                    f = gated_memory(data, parts)
                    ar = Arena(data, GATED_WORDS)
                    f.acc = ar.take(NC, CH)
                    f.sq = ar.take(2, CH)
                    gated_ffn(nc, m, f, [wgu[:, :, 0:F1]], [wgu[:, :, F1:2 * F1]], [wp], True, b)

        with place("arena3", ARENA) as arena:
            ar = Arena(arena)
            m.xn_t = ar.take(KD, S)
            wqkv = ar.take(KD, 3 * D)
            bqkv = ar.take(3 * D)
            wo = ar.take(KD, D)
            bo = ar.take(D)
            w = Memory()
            w.up = ar.take(KD, M3 * P)
            w.gate = ar.take(KD, M3 * P)
            w.down = ar.take(M3, D)
            w.a = ar.take(KD, 2 * P)
            w.b = ar.take(2, M3 * P)
            w.da = ar.take(M3, P)
            w.db = ar.take(D)
            w.route = ar.take(KD, E3)
            early = [(wqkv, rows(io.w_qkv3)), (bqkv, io.b_qkv3.partition_broadcast(P)), (wo, rows(io.w_out3)),
                     (bo, io.b_out3.partition_broadcast(P)), (w.route, rows(io.route3))]
            late = [(w.up, rows(io.up3)), (w.gate, rows(io.gate3)), (w.down, rows(io.down3)),
                    (w.a[:, :, 0:P], rows(io.up_a)), (w.a[:, :, P:2 * P], rows(io.gate_a)),
                    (w.b[:, 0, :], io.up_b), (w.b[:, 1, :], io.gate_b), (w.da, rows(io.down_a)),
                    (w.db, io.down_b)]
            load_weights(nc, early, late, late_in)
            late_done += 16 * len(late)
            base = ar.at
            a = attention_memory(m, ar, NM, HD, NM // 4, 8)
            m.acc = None
            f = Memory()
            ar = Arena(arena, a.free)
            f.lg = ar.take(NT, E3)
            f.top = ar.take(NT, 8)
            f.idx = ar.take(NT, 8, dtype=U32)
            f.idxf = ar.take(NT, 8)
            f.tw = ar.take(NT, 2)
            f.red = ar.take(4)
            f.red_all = ar.take(4)
            f.oh = ar.take(2, S)
            f.wb = ar.take(2, S)
            at = ar.at
            f.ohx = ar.take(2, NT, P)
            f.wx = ar.take(2, NT, P)
            ar = Arena(arena, at)
            f.m0 = ar.take(2, CH)
            f.md = ar.take(2, CH)
            f.s = ar.take(2, CH)
            f.h = ar.take(2, 2, CH)
            f.mixed = ar.take(MIXED, CH)
            f.uu, f.u = a.o[:, 0, 0:CH], a.o[:, 0, CH:S]
            with nc.Fori(0, B) as b:
                attention_operands(nc, m, a, a.x_in, b, bo, wqkv, bqkv, 1, False, NM, HD)
                route_pairs(nc, m, f, w.route)
                lora_experts(nc, m, f, w, a, b, (late_in, late_done))
                attention(nc, m, a, 4, 32)
                attention_finish(nc, m, a, 4, 32, wo, 1.0, b, (out, out_stored))
    
        with nc.Block() as block:
            @block.sync
            def _(sp):
                sp.wait_ge(out_stored, 16 * B * NC)



def rotation_tables(sign, n):
    inv = 1.0 / 10000.0 ** (np.arange(0, HD, 2, dtype=np.float32) / HD)
    ang = np.arange(n, dtype=np.float32)[:, None] * inv[None, :].astype(np.float32)
    cos, sin = np.cos(ang).astype(np.float32), np.sin(ang).astype(np.float32)
    return (np.ascontiguousarray(np.concatenate([cos, cos], 1)),
            np.ascontiguousarray(np.concatenate([-sign * sin, sign * sin], 1)))


def spline_grid(n_ctrl):
    t = np.linspace(0.0, n_ctrl - 1.0, F1 * D, dtype=np.float64)
    i = np.clip(np.floor(t).astype(np.int64), 0, n_ctrl - 2)
    f = (t - i).astype(np.float32).astype(np.float64)
    i = i.reshape(F1, D)
    f = f.reshape(F1, D)
    parts = [0.5 * (-f + 2 * f ** 2 - f ** 3), 0.5 * (2 - 5 * f ** 2 + 3 * f ** 3),
             0.5 * (f + 4 * f ** 2 - 3 * f ** 3), 0.5 * (-f ** 2 + f ** 3)]
    basis = np.zeros((NSEG, F1, D))
    o, h = np.indices((F1, D))
    for k in range(4):
        basis[i - i[:, :1] + k, o, h] = parts[k]
    window = np.clip(i[:, :1] - 1 + np.arange(NSEG)[None, :], 0, n_ctrl - 1)
    return window, basis.astype(np.float32)


def lay_out(v):
    v = {k: np.asarray(x) for k, x in v.items()}
    t = np.ascontiguousarray
    o = {"x": v["L0_attn_hidden_states"]}
    h = np.arange(NM)[:, None] * 3 * HD + np.arange(HD)[None, :]
    order = np.concatenate([(h + j * HD).ravel() for j in range(3)])
    o["w_qkv0"] = t(v["L0_attn_w_qkv"][order].T)
    o["b_qkv0"] = t(v["L0_attn_b_qkv"][order])
    o["w_up0"] = np.concatenate([v["L0_ffn_Wsh_up"], v["L0_ffn_Wrt_up"]])
    o["w_down0"] = np.concatenate([v["L0_ffn_Wsh_down"], v["L0_ffn_Wrt_down"]])
    o["w_router0"] = v["L0_ffn_W_router"]
    o["cos0"], o["sin0"] = rotation_tables(1.0, S)
    o["cos1"], o["sin1"] = (np.tile(np.repeat(x, 2, axis=0).ravel(), 2) for x in rotation_tables(-1.0, NM // 2))
    o["cos3"], o["sin3"] = rotation_tables(1.0, S)
    for n in "qkvo":
        o[f"w{n}1"] = t(v[f"L1_attn_w{n}"].T)
    for n in ("lq1", "lk1", "lq2", "lk2"):
        o[n] = v[f"L1_attn_{n}"]
    window, o["basis"] = spline_grid(v["L1_ffn_gate_cp"].shape[0])
    for n in ("gate", "up", "down"):
        o[f"win_{n}"] = t(v[f"L1_ffn_{n}_cp"][window])
    for n in ("r", "k", "v", "o", "cr", "ck", "cv"):
        o[f"w{n}2"] = v[f"L2_attn_W{n}"]
    for n, key in (("mix_r", "time_mix_r"), ("mix_k", "time_mix_k"), ("mix_v", "time_mix_v"), ("mix_c", "cm_mix"),
                   ("td", "time_decay"), ("tf", "time_faaaa"), ("n1w", "norm1_w"), ("n1b", "norm1_b"),
                   ("n2w", "norm2_w"), ("n2b", "norm2_b")):
        o[n] = v[f"L2_attn_{key}"].reshape(KD, P).T
    o["w_gate_up"] = v["L2_ffn_w_gate_up"]
    o["w_proj"] = v["L2_ffn_w_proj"]
    even_odd = np.concatenate([np.arange(0, HD, 2), np.arange(1, HD, 2)])
    qk = (np.arange(2 * NM)[:, None] * HD + even_odd[None, :]).ravel()
    order = np.concatenate([qk, np.arange(2 * D, 3 * D)])
    o["w_qkv3"] = t(v["L3_attn_w_qkv"][order].T)
    o["b_qkv3"] = t(v["L3_attn_b_qkv"][order])
    o["w_out3"] = t(v["L3_attn_w_out"].T)
    o["b_out3"] = v["L3_attn_b_out"]
    o["route3"] = t(v["L3_ffn_gate_w"].T)

    def padded(w, axis):
        widths = [(0, 0)] * w.ndim
        widths[axis] = (0, M3 * P - H3)
        return t(np.pad(w, widths))

    o["up3"] = padded(v["L3_ffn_w_up"].T, 1)
    o["gate3"] = padded(v["L3_ffn_w_gate"].T, 1)
    o["down3"] = padded(v["L3_ffn_w_down"].T, 0)
    for n in ("up", "gate"):
        o[f"{n}_a"] = t(v[f"L3_ffn_{n}_A"].reshape(P, D).T)
        o[f"{n}_b"] = padded(v[f"L3_ffn_{n}_B"].transpose(0, 2, 1).reshape(P, H3), 1)
    o["down_a"] = padded(v["L3_ffn_down_A"].reshape(P, H3).T, 0)
    o["down_b"] = t(v["L3_ffn_down_B"].transpose(0, 2, 1).reshape(P, D))
    return {k: t(x) for k, x in o.items()}


def kernel(**inputs):
    import concourse.bacc as bacc
    from concourse.bass_utils import run_bass_kernel_spmd

    nc = bacc.Bacc("TRN2", target_bir_lowering=False, num_devices=1)
    arrays = lay_out(inputs)
    io = Memory()
    io.__dict__.update({n: nc.dram_tensor(n, a.shape, mybir.dt.from_np(a.dtype), kind="ExternalInput").ap()
                        for n, a in arrays.items()})
    out = nc.dram_tensor("out", (B, S, D), F32, kind="ExternalOutput").ap()
    program(nc, io, out)
    result = run_bass_kernel_spmd(nc, [arrays], core_ids=[0])
    return result.results[0]["out"]
```
